# Optimizing a Trainium2 kernel written in Bass

```python
import numpy as np
import jax
import jax.numpy as jnp

def _softmax(x, axis=-1):
    return jax.nn.softmax(x, axis=axis)

def _gelu(x):
    return jax.nn.gelu(x, approximate=True)

def _silu(x):
    return jax.nn.silu(x)

def _sigmoid(x):
    return jax.nn.sigmoid(x)

def _layernorm(x, axis=-1, eps=1e-05):
    m = jnp.mean(x, axis=axis, keepdims=True)
    v = jnp.var(x, axis=axis, keepdims=True)
    return (x - m) / jnp.sqrt(v + eps)

def _scatter_add(tgt, idx, src, axis=0):
    return tgt.at[idx].add(src)

def _segment_sum(src, seg, n):
    return jax.ops.segment_sum(src, seg, n)
kernel_name = 'mk_xattn_ffn_d4_seqx_r8_9ecff3'

def setup_inputs(seed: int=0):
    np.random.seed(seed)
    _w = jnp.asarray

    def _rec_inputs():
        import jax
        import jax.numpy as jnp
        _rk = jax.random.key(seed)
        x = 7.22e-05 + 1 * jax.random.normal(jax.random.fold_in(_rk, 1), (16, 64, 128), jnp.float32)
        _lenS = 64 - jax.random.randint(jax.random.fold_in(_rk, 7), (16,), 0, max(1, 64 // 4) + 1, jnp.int32)
        _lenS2 = 64 - jax.random.randint(jax.random.fold_in(_rk, 8), (16,), 0, max(1, 64 // 4) + 1, jnp.int32)
        _ctx_1024P = jax.random.normal(jax.random.fold_in(_rk, 11), (16, 16, 128), jnp.float32)
        _ctx_1024c = jax.random.dirichlet(jax.random.fold_in(_rk, 511), 0.3 * jnp.ones((16,), jnp.float32), (16, 64))
        _ctx_1024t = jnp.einsum('bsk,bkd->bsd', _ctx_1024c, _ctx_1024P)
        _ctx_1024t = _ctx_1024t * jax.lax.rsqrt(jnp.mean(jnp.square(_ctx_1024t)) + 1e-12) * 0.953939
        ctx_1024 = 4.13588e-05 + 0.999923 * (_ctx_1024t + 0.3 * jax.random.normal(jax.random.fold_in(_rk, 611), (16, 64, 128), jnp.float32))
        fside_1x16xSxS2_0 = 7.48737e-06 + 1.00011 * jax.random.normal(jax.random.fold_in(_rk, 14), (1, 16, 64, 64), jnp.float32)
        _validS = jnp.arange(64)[None, :] < _lenS[:, None]
        _validS2 = jnp.arange(64)[None, :] < _lenS2[:, None]
        _causal = jnp.tril(jnp.ones((64, 64), dtype=bool))
        mask_BxS2_if0 = jnp.where(jnp.ones((16, 64), dtype=bool), 0, 1).astype(jnp.int32)
        mask_Bx1xSxS2_ik1 = jnp.where(jnp.broadcast_to(_validS2[:, None, None, :], (16, 1, 64, 64)), 1, 0).astype(jnp.int32)
        return (x, ctx_1024, fside_1x16xSxS2_0, mask_BxS2_if0, mask_Bx1xSxS2_ik1)
    x, ctx_1024, fside_1x16xSxS2_0, mask_BxS2_if0, mask_Bx1xSxS2_ik1 = _rec_inputs()

    def _L0_xattn_setup():
        import jax, jax.numpy as jnp
        import numpy as np
        D_MODEL = 128
        NHEAD = 16
        HEAD_DIM = D_MODEL // NHEAD
        key = jax.random.key(seed)
        ks = jax.random.split(key, 11)
        B, S, D = (4, 256, D_MODEL)
        scale = 1.0 / np.sqrt(D)
        inp = {'q': jax.random.normal(ks[0], (B, S, D), jnp.float32), 'k': jax.random.normal(ks[1], (B, S, D), jnp.float32), 'v': jax.random.normal(ks[2], (B, S, D), jnp.float32), 'Wq': jax.random.normal(ks[3], (D, D), jnp.float32) * scale, 'bq': jnp.zeros((D,), jnp.float32), 'Wk': jax.random.normal(ks[4], (D, D), jnp.float32) * scale, 'bk': jnp.zeros((D,), jnp.float32), 'Wv': jax.random.normal(ks[5], (D, D), jnp.float32) * scale, 'bv': jnp.zeros((D,), jnp.float32), 'Wo': jax.random.normal(ks[6], (D, D), jnp.float32) * scale, 'bo': jnp.zeros((D,), jnp.float32)}
        return inp
    _L0_xattn_all = _L0_xattn_setup()
    _L0_xattn_in = {k: v for k, v in _L0_xattn_all.items() if k in ('Wq', 'bq', 'Wk', 'bk', 'Wv', 'bv', 'Wo', 'bo')}
    del _L0_xattn_all

    def _L0_ffn_setup():
        import jax, jax.numpy as jnp
        import numpy as np
        B, T, D, H = (4, 256, 128, 256)
        E, S, K = (8, 2, 2)

        def _swiglu_stacked(x, w1, b1, w2, b2, w3, b3):
            p1 = jnp.einsum('btd,ndh->nbth', x, w1) + b1[:, None, None, :]
            p2 = jnp.einsum('btd,ndh->nbth', x, w2) + b2[:, None, None, :]
            glu = jax.nn.silu(p1) * p2
            return jnp.einsum('nbth,nhd->nbtd', glu, w3) + b3[:, None, None, :]
        key = jax.random.key(seed)
        ks = jax.random.split(key, 10)
        s = 0.02
        return {'x': jax.random.normal(ks[0], (B, T, D), jnp.float32), 'gate_w': jax.random.normal(ks[1], (D, E), jnp.float32) * s, 'gate_b': jnp.zeros((E,), jnp.float32), 'rw1': jax.random.normal(ks[2], (E, D, H), jnp.float32) * s, 'rb1': jnp.zeros((E, H), jnp.float32), 'rw2': jax.random.normal(ks[3], (E, D, H), jnp.float32) * s, 'rb2': jnp.zeros((E, H), jnp.float32), 'rw3': jax.random.normal(ks[4], (E, H, D), jnp.float32) * s, 'rb3': jnp.zeros((E, D), jnp.float32), 'sw1': jax.random.normal(ks[5], (S, D, H), jnp.float32) * s, 'sb1': jnp.zeros((S, H), jnp.float32), 'sw2': jax.random.normal(ks[6], (S, D, H), jnp.float32) * s, 'sb2': jnp.zeros((S, H), jnp.float32), 'sw3': jax.random.normal(ks[7], (S, H, D), jnp.float32) * s, 'sb3': jnp.zeros((S, D), jnp.float32)}
    _L0_ffn_all = _L0_ffn_setup()
    _L0_ffn_in = {k: v for k, v in _L0_ffn_all.items() if k in ('gate_w', 'gate_b', 'rw1', 'rb1', 'rw2', 'rb2', 'rw3', 'rb3', 'sw1', 'sb1', 'sw2', 'sb2', 'sw3', 'sb3')}
    del _L0_ffn_all

    def _L1_xattn_setup():
        import jax, jax.numpy as jnp
        import numpy as np
        N_HEADS = 4
        IN_FEATURES = 128

        def _channel_attention(qm, km, vm, scale):
            b, n, c = qm.shape
            d = c // N_HEADS
            qh = qm.reshape(b, n, N_HEADS, d).transpose(0, 2, 3, 1)
            kh = km.reshape(b, n, N_HEADS, d).transpose(0, 2, 3, 1)
            vh = vm.reshape(b, n, N_HEADS, d).transpose(0, 2, 3, 1)
            scores = jnp.einsum('bhdn,bhen->bhde', qh, kh) * scale
            attn = jax.nn.softmax(scores, axis=-1)
            out = jnp.einsum('bhde,bhen->bhdn', attn, vh)
            return out.transpose(0, 3, 1, 2).reshape(b, n, c)
        key = jax.random.key(seed)
        ks = jax.random.split(key, 20)
        B, HW, C = (2, 2048, 128)
        inp = {'q': jax.random.normal(ks[0], (B, HW, C), dtype=jnp.float32), 'k': jax.random.normal(ks[1], (B, HW, C), dtype=jnp.float32), 'v': jax.random.normal(ks[2], (B, HW, C), dtype=jnp.float32)}
        names = ['wqg', 'bqg', 'wkg', 'bkg', 'wvg', 'bvg', 'wql', 'bql', 'wkl', 'bkl', 'wvl', 'bvl', 'wp', 'bp']
        for i, n in enumerate(names):
            inp[n] = jax.random.normal(ks[3 + i], (C,), dtype=jnp.float32)
        return inp
    _L1_xattn_all = _L1_xattn_setup()
    _L1_xattn_in = {k: v for k, v in _L1_xattn_all.items() if k in ('wqg', 'bqg', 'wkg', 'bkg', 'wvg', 'bvg', 'wql', 'bql', 'wkl', 'bkl', 'wvl', 'bvl', 'wp', 'bp')}
    del _L1_xattn_all

    def _L1_ffn_setup():
        import jax, jax.numpy as jnp
        import numpy as np
        B, S, IN, OUT = (4, 1024, 128, 128)
        EPS = 1e-06

        def _xla_quantized_matmul(x2d, weight_q, weight_scale):
            amax = jnp.max(jnp.abs(x2d), axis=-1, keepdims=True)
            x_scale = jnp.maximum(amax, EPS) / 127.0
            x_q = jnp.clip(jnp.round(x2d / x_scale), -128, 127).astype(jnp.int8)
            acc = jax.lax.dot_general(x_q, weight_q, (((1,), (1,)), ((), ())), preferred_element_type=jnp.int32)
            return acc.astype(jnp.float32) * x_scale * weight_scale[None, :]
        key = jax.random.key(seed)
        k1, k2, k3, k4 = jax.random.split(key, 4)
        x = jax.random.normal(k1, (B, S, IN), dtype=jnp.float32)
        weight_q = jax.random.randint(k2, (OUT, IN), -128, 128, dtype=jnp.int32).astype(jnp.int8)
        weight_scale = jax.random.uniform(k3, (OUT,), dtype=jnp.float32, minval=0.001, maxval=0.01)
        bias = jax.random.normal(k4, (OUT,), dtype=jnp.float32) * 0.01
        return {'x': x, 'weight_q': weight_q, 'weight_scale': weight_scale, 'bias': bias}
    _L1_ffn_all = _L1_ffn_setup()
    _L1_ffn_in = {k: v for k, v in _L1_ffn_all.items() if k in ('weight_q', 'weight_scale', 'bias')}
    del _L1_ffn_all

    def _L2_xattn_setup():
        import jax, jax.numpy as jnp
        import numpy as np
        import math
        B, M, D, H, NK = (4, 256, 128, 16, 5)
        HD = D // H

        def _gather_pad0(x, idx):
            Bx, Hx, W, hd = x.shape
            valid = (idx >= 0) & (idx < W)
            idxc = jnp.clip(idx, 0, W - 1).reshape(Bx, Hx, -1)
            g = jnp.take_along_axis(x, idxc[..., None], axis=2)
            g = g.reshape(idx.shape + (hd,))
            return g * valid[..., None].astype(x.dtype)
        key = jax.random.key(seed)
        ks = jax.random.split(key, 9)
        w = lambda k, shape: jax.random.normal(k, shape, jnp.float32) * 0.02
        return {'k': jax.random.normal(ks[0], (B, M, D), jnp.float32), 'v': jax.random.normal(ks[1], (B, M, D), jnp.float32), 'q': jax.random.normal(ks[2], (B, M, D), jnp.float32), 'mask': jnp.zeros((B, M), jnp.int32), 'Wk': w(ks[3], (D, D)), 'bk': jnp.zeros((D,), jnp.float32), 'Wv': w(ks[4], (D, D)), 'bv': jnp.zeros((D,), jnp.float32), 'Wq': w(ks[5], (D, D)), 'bq': jnp.zeros((D,), jnp.float32), 'Woff': w(ks[6], (H * NK, D)), 'boff': jnp.zeros((H * NK,), jnp.float32), 'Wo': w(ks[7], (D, D)), 'bo': jnp.zeros((D,), jnp.float32)}
    _L2_xattn_all = _L2_xattn_setup()
    _L2_xattn_in = {k: v for k, v in _L2_xattn_all.items() if k in ('Wk', 'bk', 'Wv', 'bv', 'Wq', 'bq', 'Woff', 'boff', 'Wo', 'bo')}
    del _L2_xattn_all

    def _L2_ffn_setup():
        import jax, jax.numpy as jnp
        import numpy as np
        SL, BS, HS, FF, E, TOPK = (256, 2, 128, 512, 8, 2)
        key = jax.random.key(seed)
        ks = jax.random.split(key, 6)
        T = SL * BS
        x = jax.random.normal(ks[0], (SL, BS, HS), jnp.float32)
        scores = jax.random.uniform(ks[1], (T, E), jnp.float32)
        expert_weights = jax.random.uniform(ks[2], (T, TOPK), jnp.float32)
        expert_indices = jax.random.randint(ks[3], (T, TOPK), 0, E, jnp.int32)
        w1 = jax.random.normal(ks[4], (E, HS, FF), jnp.float32) * (1.0 / np.sqrt(HS))
        w2 = jax.random.normal(ks[5], (E, FF, HS), jnp.float32) * (1.0 / np.sqrt(FF))
        bias = jnp.zeros((HS,), jnp.float32)
        return dict(x=x, scores=scores, expert_weights=expert_weights, expert_indices=expert_indices, w1=w1, w2=w2, bias=bias)
    _L2_ffn_all = _L2_ffn_setup()
    _L2_ffn_in = {k: v for k, v in _L2_ffn_all.items() if k in ('scores', 'expert_weights', 'expert_indices', 'w1', 'w2', 'bias')}
    del _L2_ffn_all

    def _L3_xattn_setup():
        import jax, jax.numpy as jnp
        import numpy as np
        import math
        D_MODEL = 128
        NUM_HEADS = 16
        D_K = D_MODEL // NUM_HEADS
        B, L = (4, 256)

        def _nan_clamp(x):
            x = jnp.where(jnp.isnan(x), 0.0, x)
            x = jnp.where(jnp.isposinf(x), 10000.0, x)
            x = jnp.where(jnp.isneginf(x), -10000.0, x)
            return x

        def _split_heads(x):
            b, l, _ = x.shape
            return x.reshape(b, l, NUM_HEADS, D_K).transpose(0, 2, 1, 3)
        key = jax.random.key(seed)
        ks = jax.random.split(key, 14)
        s = 1.0 / math.sqrt(D_MODEL)
        return {'Q': jax.random.normal(ks[0], (B, L, D_MODEL), jnp.float32), 'K': jax.random.normal(ks[1], (B, L, D_MODEL), jnp.float32), 'V': jax.random.normal(ks[2], (B, L, D_MODEL), jnp.float32), 'mask': jax.random.randint(ks[3], (B, 1, L, L), 0, 2, jnp.int32), 'attn_bias': jax.random.normal(ks[4], (1, NUM_HEADS, L, L), jnp.float32), 'W_q': jax.random.normal(ks[5], (D_MODEL, D_MODEL), jnp.float32) * s, 'b_q': jax.random.normal(ks[6], (D_MODEL,), jnp.float32) * s, 'W_k': jax.random.normal(ks[7], (D_MODEL, D_MODEL), jnp.float32) * s, 'b_k': jax.random.normal(ks[8], (D_MODEL,), jnp.float32) * s, 'W_v': jax.random.normal(ks[9], (D_MODEL, D_MODEL), jnp.float32) * s, 'b_v': jax.random.normal(ks[10], (D_MODEL,), jnp.float32) * s, 'W_o': jax.random.normal(ks[11], (D_MODEL, D_MODEL), jnp.float32) * s, 'b_o': jax.random.normal(ks[12], (D_MODEL,), jnp.float32) * s}
    _L3_xattn_all = _L3_xattn_setup()
    _L3_xattn_in = {k: v for k, v in _L3_xattn_all.items() if k in ('W_q', 'b_q', 'W_k', 'b_k', 'W_v', 'b_v', 'W_o', 'b_o')}
    del _L3_xattn_all

    def _L3_ffn_setup():
        import jax, jax.numpy as jnp
        import numpy as np
        BLOCK = 32
        W_BITS = 4
        ACT_BITS = 16

        def act_qdq(x):
            qmax = 2.0 ** (ACT_BITS - 1) - 1.0
            scale = jnp.maximum(jnp.max(jnp.abs(x)) / qmax, 1e-12)
            return jnp.clip(jnp.round(x / scale), -qmax - 1.0, qmax) * scale

        def fixed_qdq_u16(x):
            scale = 1.0 / 65536.0
            return jnp.clip(jnp.round(x / scale), 0.0, 65535.0) * scale

        def lpbq_dequant(w):
            O, I = w.shape
            qmax = 2.0 ** (W_BITS - 1) - 1.0
            wb = w.reshape(O, I // BLOCK, BLOCK)
            s = jnp.maximum(jnp.max(jnp.abs(wb), axis=-1, keepdims=True) / qmax, 1e-12)
            wq = jnp.clip(jnp.round(wb / s), -qmax - 1.0, qmax) * s
            return wq.reshape(O, I)
        key = jax.random.key(seed)
        k1, k2, k3, k4 = jax.random.split(key, 4)
        B, S, H, I = (2, 512, 128, 384)
        x = jax.random.normal(k1, (B, S, H), jnp.float32)
        w_gate = jax.random.normal(k2, (I, H), jnp.float32) * 0.02
        w_up = jax.random.normal(k3, (I, H), jnp.float32) * 0.02
        w_down = jax.random.normal(k4, (H, I), jnp.float32) * 0.02
        return {'x': x, 'w_gate': w_gate, 'w_up': w_up, 'w_down': w_down}
    _L3_ffn_all = _L3_ffn_setup()
    _L3_ffn_in = {k: v for k, v in _L3_ffn_all.items() if k in ('w_gate', 'w_up', 'w_down')}
    del _L3_ffn_all
    return {'x': x, 'ctx_1024': ctx_1024, 'fside_1x16xSxS2_0': fside_1x16xSxS2_0, 'mask_BxS2_if0': mask_BxS2_if0, 'mask_Bx1xSxS2_ik1': mask_Bx1xSxS2_ik1, 'L0_xattn_Wq': _L0_xattn_in['Wq'], 'L0_xattn_bq': _L0_xattn_in['bq'], 'L0_xattn_Wk': _L0_xattn_in['Wk'], 'L0_xattn_bk': _L0_xattn_in['bk'], 'L0_xattn_Wv': _L0_xattn_in['Wv'], 'L0_xattn_bv': _L0_xattn_in['bv'], 'L0_xattn_Wo': _L0_xattn_in['Wo'], 'L0_xattn_bo': _L0_xattn_in['bo'], 'L0_ffn_gate_w': _L0_ffn_in['gate_w'], 'L0_ffn_gate_b': _L0_ffn_in['gate_b'], 'L0_ffn_rw1': _L0_ffn_in['rw1'], 'L0_ffn_rb1': _L0_ffn_in['rb1'], 'L0_ffn_rw2': _L0_ffn_in['rw2'], 'L0_ffn_rb2': _L0_ffn_in['rb2'], 'L0_ffn_rw3': _L0_ffn_in['rw3'], 'L0_ffn_rb3': _L0_ffn_in['rb3'], 'L0_ffn_sw1': _L0_ffn_in['sw1'], 'L0_ffn_sb1': _L0_ffn_in['sb1'], 'L0_ffn_sw2': _L0_ffn_in['sw2'], 'L0_ffn_sb2': _L0_ffn_in['sb2'], 'L0_ffn_sw3': _L0_ffn_in['sw3'], 'L0_ffn_sb3': _L0_ffn_in['sb3'], 'L1_xattn_wqg': _L1_xattn_in['wqg'], 'L1_xattn_bqg': _L1_xattn_in['bqg'], 'L1_xattn_wkg': _L1_xattn_in['wkg'], 'L1_xattn_bkg': _L1_xattn_in['bkg'], 'L1_xattn_wvg': _L1_xattn_in['wvg'], 'L1_xattn_bvg': _L1_xattn_in['bvg'], 'L1_xattn_wql': _L1_xattn_in['wql'], 'L1_xattn_bql': _L1_xattn_in['bql'], 'L1_xattn_wkl': _L1_xattn_in['wkl'], 'L1_xattn_bkl': _L1_xattn_in['bkl'], 'L1_xattn_wvl': _L1_xattn_in['wvl'], 'L1_xattn_bvl': _L1_xattn_in['bvl'], 'L1_xattn_wp': _L1_xattn_in['wp'], 'L1_xattn_bp': _L1_xattn_in['bp'], 'L1_ffn_weight_q': _L1_ffn_in['weight_q'], 'L1_ffn_weight_scale': _L1_ffn_in['weight_scale'], 'L1_ffn_bias': _L1_ffn_in['bias'], 'L2_xattn_Wk': _L2_xattn_in['Wk'], 'L2_xattn_bk': _L2_xattn_in['bk'], 'L2_xattn_Wv': _L2_xattn_in['Wv'], 'L2_xattn_bv': _L2_xattn_in['bv'], 'L2_xattn_Wq': _L2_xattn_in['Wq'], 'L2_xattn_bq': _L2_xattn_in['bq'], 'L2_xattn_Woff': _L2_xattn_in['Woff'], 'L2_xattn_boff': _L2_xattn_in['boff'], 'L2_xattn_Wo': _L2_xattn_in['Wo'], 'L2_xattn_bo': _L2_xattn_in['bo'], 'L2_ffn_scores': _L2_ffn_in['scores'], 'L2_ffn_expert_weights': _L2_ffn_in['expert_weights'], 'L2_ffn_expert_indices': _L2_ffn_in['expert_indices'], 'L2_ffn_w1': _L2_ffn_in['w1'], 'L2_ffn_w2': _L2_ffn_in['w2'], 'L2_ffn_bias': _L2_ffn_in['bias'], 'L3_xattn_W_q': _L3_xattn_in['W_q'], 'L3_xattn_b_q': _L3_xattn_in['b_q'], 'L3_xattn_W_k': _L3_xattn_in['W_k'], 'L3_xattn_b_k': _L3_xattn_in['b_k'], 'L3_xattn_W_v': _L3_xattn_in['W_v'], 'L3_xattn_b_v': _L3_xattn_in['b_v'], 'L3_xattn_W_o': _L3_xattn_in['W_o'], 'L3_xattn_b_o': _L3_xattn_in['b_o'], 'L3_ffn_w_gate': _L3_ffn_in['w_gate'], 'L3_ffn_w_up': _L3_ffn_in['w_up'], 'L3_ffn_w_down': _L3_ffn_in['w_down']}

def reference(x, ctx_1024, fside_1x16xSxS2_0, mask_BxS2_if0, mask_Bx1xSxS2_ik1, L0_xattn_Wq, L0_xattn_bq, L0_xattn_Wk, L0_xattn_bk, L0_xattn_Wv, L0_xattn_bv, L0_xattn_Wo, L0_xattn_bo, L0_ffn_gate_w, L0_ffn_gate_b, L0_ffn_rw1, L0_ffn_rb1, L0_ffn_rw2, L0_ffn_rb2, L0_ffn_rw3, L0_ffn_rb3, L0_ffn_sw1, L0_ffn_sb1, L0_ffn_sw2, L0_ffn_sb2, L0_ffn_sw3, L0_ffn_sb3, L1_xattn_wqg, L1_xattn_bqg, L1_xattn_wkg, L1_xattn_bkg, L1_xattn_wvg, L1_xattn_bvg, L1_xattn_wql, L1_xattn_bql, L1_xattn_wkl, L1_xattn_bkl, L1_xattn_wvl, L1_xattn_bvl, L1_xattn_wp, L1_xattn_bp, L1_ffn_weight_q, L1_ffn_weight_scale, L1_ffn_bias, L2_xattn_Wk, L2_xattn_bk, L2_xattn_Wv, L2_xattn_bv, L2_xattn_Wq, L2_xattn_bq, L2_xattn_Woff, L2_xattn_boff, L2_xattn_Wo, L2_xattn_bo, L2_ffn_scores, L2_ffn_expert_weights, L2_ffn_expert_indices, L2_ffn_w1, L2_ffn_w2, L2_ffn_bias, L3_xattn_W_q, L3_xattn_b_q, L3_xattn_W_k, L3_xattn_b_k, L3_xattn_W_v, L3_xattn_b_v, L3_xattn_W_o, L3_xattn_b_o, L3_ffn_w_gate, L3_ffn_w_up, L3_ffn_w_down):
    import jax
    import jax.numpy as jnp

    def _L0_xattn_ref(q, k, v, Wq, bq, Wk, bk, Wv, bv, Wo, bo):
        import jax, jax.numpy as jnp
        import numpy as np
        D_MODEL = 128
        NHEAD = 16
        HEAD_DIM = D_MODEL // NHEAD
        B, S, D = q.shape
        H, Hd = (NHEAD, HEAD_DIM)
        qh = (q @ Wq.T + bq).reshape(B, S, H, Hd).transpose(0, 2, 1, 3)
        kh = (k @ Wk.T + bk).reshape(B, S, H, Hd).transpose(0, 2, 1, 3)
        vh = (v @ Wv.T + bv).reshape(B, S, H, Hd).transpose(0, 2, 1, 3)
        scores = jnp.einsum('bhqd,bhkd->bhqk', qh, kh) / jnp.sqrt(jnp.float32(Hd))
        attn = jax.nn.softmax(scores, axis=-1)
        out = jnp.einsum('bhqk,bhkd->bhqd', attn, vh)
        out = out.transpose(0, 2, 1, 3).reshape(B, S, D)
        return out @ Wo.T + bo

    def _L0_ffn_ref(x, gate_w, gate_b, rw1, rb1, rw2, rb2, rw3, rb3, sw1, sb1, sw2, sb2, sw3, sb3):
        import jax, jax.numpy as jnp
        import numpy as np
        B, T, D, H = (4, 256, 128, 256)
        E, S, K = (8, 2, 2)

        def _swiglu_stacked(x, w1, b1, w2, b2, w3, b3):
            p1 = jnp.einsum('btd,ndh->nbth', x, w1) + b1[:, None, None, :]
            p2 = jnp.einsum('btd,ndh->nbth', x, w2) + b2[:, None, None, :]
            glu = jax.nn.silu(p1) * p2
            return jnp.einsum('nbth,nhd->nbtd', glu, w3) + b3[:, None, None, :]
        scores = jax.nn.softmax(x @ gate_w + gate_b, axis=-1)
        weights, indices = jax.lax.top_k(scores, K)
        routed_all = _swiglu_stacked(x, rw1, rb1, rw2, rb2, rw3, rb3)
        out_bted = jnp.transpose(routed_all, (1, 2, 0, 3))
        gathered = jnp.take_along_axis(out_bted, indices[..., None], axis=2)
        routed = jnp.sum(weights[..., None] * gathered, axis=2)
        shared = _swiglu_stacked(x, sw1, sb1, sw2, sb2, sw3, sb3).mean(axis=0)
        return shared + routed

    def _L1_xattn_ref(q, k, v, wqg, bqg, wkg, bkg, wvg, bvg, wql, bql, wkl, bkl, wvl, bvl, wp, bp):
        import jax, jax.numpy as jnp
        import numpy as np
        N_HEADS = 4
        IN_FEATURES = 128

        def _channel_attention(qm, km, vm, scale):
            b, n, c = qm.shape
            d = c // N_HEADS
            qh = qm.reshape(b, n, N_HEADS, d).transpose(0, 2, 3, 1)
            kh = km.reshape(b, n, N_HEADS, d).transpose(0, 2, 3, 1)
            vh = vm.reshape(b, n, N_HEADS, d).transpose(0, 2, 3, 1)
            scores = jnp.einsum('bhdn,bhen->bhde', qh, kh) * scale
            attn = jax.nn.softmax(scores, axis=-1)
            out = jnp.einsum('bhde,bhen->bhdn', attn, vh)
            return out.transpose(0, 3, 1, 2).reshape(b, n, c)
        scale = IN_FEATURES ** (-0.5)
        att_global = _channel_attention(q * wqg + bqg, k * wkg + bkg, v * wvg + bvg, scale)
        att_local = _channel_attention(q * wql + bql, k * wkl + bkl, v * wvl + bvl, scale)
        att = att_global + att_local
        return 2.0 * att * wp + bp

    def _L1_ffn_ref(x, weight_q, weight_scale, bias):
        import jax, jax.numpy as jnp
        import numpy as np
        B, S, IN, OUT = (4, 1024, 128, 128)
        EPS = 1e-06

        def _xla_quantized_matmul(x2d, weight_q, weight_scale):
            amax = jnp.max(jnp.abs(x2d), axis=-1, keepdims=True)
            x_scale = jnp.maximum(amax, EPS) / 127.0
            x_q = jnp.clip(jnp.round(x2d / x_scale), -128, 127).astype(jnp.int8)
            acc = jax.lax.dot_general(x_q, weight_q, (((1,), (1,)), ((), ())), preferred_element_type=jnp.int32)
            return acc.astype(jnp.float32) * x_scale * weight_scale[None, :]
        orig_shape = x.shape
        x2d = x.reshape(-1, orig_shape[-1])
        out = _xla_quantized_matmul(x2d, weight_q, weight_scale)
        out = out.reshape(*orig_shape[:-1], out.shape[-1])
        out = out + bias
        return out

    def _L2_xattn_ref(k, v, q, mask, Wk, bk, Wv, bv, Wq, bq, Woff, boff, Wo, bo):
        import jax, jax.numpy as jnp
        import numpy as np
        import math
        B, M, D, H, NK = (4, 256, 128, 16, 5)
        HD = D // H

        def _gather_pad0(x, idx):
            Bx, Hx, W, hd = x.shape
            valid = (idx >= 0) & (idx < W)
            idxc = jnp.clip(idx, 0, W - 1).reshape(Bx, Hx, -1)
            g = jnp.take_along_axis(x, idxc[..., None], axis=2)
            g = g.reshape(idx.shape + (hd,))
            return g * valid[..., None].astype(x.dtype)
        Bq, Q, _ = q.shape
        key_len = k.shape[1]
        K = jnp.einsum('bmd,ed->bme', k, Wk) + bk
        V = jnp.einsum('bmd,ed->bme', v, Wv) + bv
        Qp = jnp.einsum('bqd,ed->bqe', q, Wq) + bq
        off = jnp.einsum('bqd,ed->bqe', Qp, Woff) + boff
        off = off.reshape(Bq, Q, H, NK).transpose(0, 2, 1, 3)
        Kh = K.reshape(Bq, key_len, H, HD).transpose(0, 2, 1, 3)
        Vh = V.reshape(Bq, key_len, H, HD).transpose(0, 2, 1, 3)
        Qh = Qp.reshape(Bq, Q, H, HD).transpose(0, 2, 1, 3)
        loc = jnp.arange(Q, dtype=jnp.float32)[:, None]
        left = -NK // 2
        ref = jnp.arange(left, NK + left, dtype=jnp.float32)
        sign_lens = (1 - mask).sum(-1).astype(jnp.float32) - 1.0
        loc_x = jnp.mod(ref + off + loc, sign_lens[:, None, None, None])
        xg = loc_x / (key_len - 1) * 2.0 - 1.0
        ix = ((xg + 1.0) * key_len - 1.0) / 2.0
        x0 = jnp.floor(ix)
        dx = ix - x0
        i0 = x0.astype(jnp.int32)
        i1 = i0 + 1
        w0 = (1.0 - dx)[..., None]
        w1 = dx[..., None]
        sk = 0.5 * (w0 * _gather_pad0(Kh, i0) + w1 * _gather_pad0(Kh, i1))
        sv = 0.5 * (w0 * _gather_pad0(Vh, i0) + w1 * _gather_pad0(Vh, i1))
        scores = jnp.einsum('bhqd,bhqkd->bhqk', Qh / math.sqrt(HD), sk)
        attn = jax.nn.softmax(scores, axis=-1)
        ctx = jnp.einsum('bhqk,bhqkd->bhqd', attn, sv)
        ctx = ctx.transpose(0, 2, 1, 3).reshape(Bq, Q, H * HD)
        return jnp.einsum('bqd,ed->bqe', ctx, Wo) + bo

    def _L2_ffn_ref(x, scores, expert_weights, expert_indices, w1, w2, bias):
        import jax, jax.numpy as jnp
        import numpy as np
        SL, BS, HS, FF, E, TOPK = (256, 2, 128, 512, 8, 2)
        sl, bs, hs = x.shape
        n_exp = w1.shape[0]
        top_k = expert_indices.shape[-1]
        xf = x.reshape(-1, hs)
        flat_idx = expert_indices.reshape(-1)
        flat_w = expert_weights.reshape(-1)
        order = jnp.argsort(flat_idx)
        tok = order // top_k
        tokens_per_expert = jnp.bincount(flat_idx, length=n_exp).astype(jnp.int32)
        xs = xf[tok]
        h = jax.nn.gelu(jax.lax.ragged_dot(xs, w1, tokens_per_expert), approximate=False)
        ys = jax.lax.ragged_dot(h, w2, tokens_per_expert)
        ys = ys * flat_w[order][:, None]
        out = jnp.zeros_like(xf).at[tok].add(ys)
        return out.reshape(sl, bs, hs) + bias

    def _L3_xattn_ref(Q, K, V, mask, attn_bias, W_q, b_q, W_k, b_k, W_v, b_v, W_o, b_o):
        import jax, jax.numpy as jnp
        import numpy as np
        import math
        D_MODEL = 128
        NUM_HEADS = 16
        D_K = D_MODEL // NUM_HEADS
        B, L = (4, 256)

        def _nan_clamp(x):
            x = jnp.where(jnp.isnan(x), 0.0, x)
            x = jnp.where(jnp.isposinf(x), 10000.0, x)
            x = jnp.where(jnp.isneginf(x), -10000.0, x)
            return x

        def _split_heads(x):
            b, l, _ = x.shape
            return x.reshape(b, l, NUM_HEADS, D_K).transpose(0, 2, 1, 3)
        q = _split_heads(Q @ W_q.T + b_q)
        k = _split_heads(K @ W_k.T + b_k)
        v = _split_heads(V @ W_v.T + b_v)
        q = _nan_clamp(q)
        k = _nan_clamp(k)
        v = _nan_clamp(v)
        bias = jnp.clip(_nan_clamp(attn_bias), -10000.0, 10000.0)
        scale = 1.0 / math.sqrt(D_K)
        logits = jnp.einsum('bhqd,bhkd->bhqk', q.astype(jnp.float32), k.astype(jnp.float32)) * scale
        logits = logits + bias.astype(jnp.float32)
        logits = jnp.where(mask == 0, -10000.0, logits)
        probs = jax.nn.softmax(logits, axis=-1)
        probs = jnp.where(jnp.isnan(probs), 0.0, probs)
        out = jnp.einsum('bhqk,bhkd->bhqd', probs, v.astype(jnp.float32)).astype(q.dtype)
        out = out.transpose(0, 2, 1, 3).reshape(Q.shape[0], Q.shape[1], D_MODEL)
        return out @ W_o.T + b_o

    def _L3_ffn_ref(x, w_gate, w_up, w_down):
        import jax, jax.numpy as jnp
        import numpy as np
        BLOCK = 32
        W_BITS = 4
        ACT_BITS = 16

        def act_qdq(x):
            qmax = 2.0 ** (ACT_BITS - 1) - 1.0
            scale = jnp.maximum(jnp.max(jnp.abs(x)) / qmax, 1e-12)
            return jnp.clip(jnp.round(x / scale), -qmax - 1.0, qmax) * scale

        def fixed_qdq_u16(x):
            scale = 1.0 / 65536.0
            return jnp.clip(jnp.round(x / scale), 0.0, 65535.0) * scale

        def lpbq_dequant(w):
            O, I = w.shape
            qmax = 2.0 ** (W_BITS - 1) - 1.0
            wb = w.reshape(O, I // BLOCK, BLOCK)
            s = jnp.maximum(jnp.max(jnp.abs(wb), axis=-1, keepdims=True) / qmax, 1e-12)
            wq = jnp.clip(jnp.round(wb / s), -qmax - 1.0, qmax) * s
            return wq.reshape(O, I)
        x = act_qdq(x)
        up = act_qdq(x @ lpbq_dequant(w_up).T)
        gate = act_qdq(x @ lpbq_dequant(w_gate).T)
        sig = fixed_qdq_u16(jax.nn.sigmoid(gate))
        gate = act_qdq(gate * sig)
        o = act_qdq(gate * up)
        return o @ lpbq_dequant(w_down).T
    x = x + _L0_xattn_ref(_layernorm(x, axis=-1), ctx_1024, ctx_1024, L0_xattn_Wq, L0_xattn_bq, L0_xattn_Wk, L0_xattn_bk, L0_xattn_Wv, L0_xattn_bv, L0_xattn_Wo, L0_xattn_bo)
    x = x + _L0_ffn_ref(_layernorm(x, axis=-1), L0_ffn_gate_w, L0_ffn_gate_b, L0_ffn_rw1, L0_ffn_rb1, L0_ffn_rw2, L0_ffn_rb2, L0_ffn_rw3, L0_ffn_rb3, L0_ffn_sw1, L0_ffn_sb1, L0_ffn_sw2, L0_ffn_sb2, L0_ffn_sw3, L0_ffn_sb3)
    x = x + _L1_xattn_ref(_layernorm(x, axis=-1), ctx_1024, ctx_1024, L1_xattn_wqg, L1_xattn_bqg, L1_xattn_wkg, L1_xattn_bkg, L1_xattn_wvg, L1_xattn_bvg, L1_xattn_wql, L1_xattn_bql, L1_xattn_wkl, L1_xattn_bkl, L1_xattn_wvl, L1_xattn_bvl, L1_xattn_wp, L1_xattn_bp)
    x = x + _L1_ffn_ref(_layernorm(x, axis=-1), L1_ffn_weight_q, L1_ffn_weight_scale, L1_ffn_bias)
    x = x + _L2_xattn_ref(ctx_1024, ctx_1024, _layernorm(x, axis=-1), mask_BxS2_if0, L2_xattn_Wk, L2_xattn_bk, L2_xattn_Wv, L2_xattn_bv, L2_xattn_Wq, L2_xattn_bq, L2_xattn_Woff, L2_xattn_boff, L2_xattn_Wo, L2_xattn_bo)
    x = x + _L2_ffn_ref(_layernorm(x, axis=-1), L2_ffn_scores, L2_ffn_expert_weights, L2_ffn_expert_indices, L2_ffn_w1, L2_ffn_w2, L2_ffn_bias)
    x = x + _L3_xattn_ref(_layernorm(x, axis=-1), ctx_1024, ctx_1024, mask_Bx1xSxS2_ik1, fside_1x16xSxS2_0, L3_xattn_W_q, L3_xattn_b_q, L3_xattn_W_k, L3_xattn_b_k, L3_xattn_W_v, L3_xattn_b_v, L3_xattn_W_o, L3_xattn_b_o)
    x = x + _L3_ffn_ref(_layernorm(x, axis=-1), L3_ffn_w_gate, L3_ffn_w_up, L3_ffn_w_down)
    return x

_drawn_inputs = setup_inputs


def setup_inputs(seed=0):
    import zlib

    import numpy as np

    out = dict(_drawn_inputs(seed))
    spreads = {'L0_xattn_bq': (0.0, 0.313),
     'L0_xattn_bk': (0.0, 2.0),
     'L0_xattn_bv': (0.0, 0.1),
     'L0_xattn_bo': (0.0, 0.1),
     'L0_ffn_gate_b': (0.0, 0.653),
     'L0_ffn_rb1': (0.0, 0.8),
     'L0_ffn_rb2': (0.0, 0.8),
     'L0_ffn_rb3': (0.0, 0.369),
     'L0_ffn_sb1': (0.0, 0.8),
     'L0_ffn_sb2': (0.0, 0.8),
     'L0_ffn_sb3': (0.0, 0.448),
     'L2_xattn_bk': (0.0, 2.0),
     'L2_xattn_bv': (0.0, 0.8),
     'L2_xattn_bq': (0.0, 0.8),
     'L2_xattn_boff': (0.0, 0.8),
     'L2_xattn_bo': (0.0, 0.481),
     'L2_ffn_bias': (0.0, 0.566)}
    factors = {'L0_ffn_gate_w': 4.367,
     'L0_ffn_rw1': 8.0,
     'L0_ffn_rw2': 8.0,
     'L0_ffn_rw3': 8.0,
     'L0_ffn_sw1': 8.0,
     'L0_ffn_sw2': 8.0,
     'L0_ffn_sw3': 8.0,
     'L1_ffn_bias': 34.508,
     'L2_xattn_Wk': 8.0,
     'L2_xattn_Wv': 8.0,
     'L2_xattn_Wq': 8.0,
     'L2_xattn_Woff': 8.0,
     'L2_xattn_Wo': 8.0,
     'L3_xattn_b_q': 8.0,
     'L3_xattn_b_k': 64.0,
     'L3_xattn_b_v': 3.66,
     'L3_xattn_b_o': 4.525,
     'L3_ffn_w_gate': 8.0,
     'L3_ffn_w_up': 8.0,
     'L3_ffn_w_down': 8.0}
    for name, (base, spread) in spreads.items():
        noise = np.random.default_rng([zlib.crc32(name.encode()), seed]).standard_normal(out[name].shape)
        drawn = base * np.exp(spread * noise) if base else spread * noise
        out[name] = jnp.asarray(drawn.astype(out[name].dtype))
    for name, factor in factors.items():
        out[name] = (out[name] * factor).astype(out[name].dtype)
    return out
```

```python
from contextlib import ExitStack

import numpy as np

import concourse.bass as bass
from concourse import mybir

P = 128
B, S, D = 16, 64, 128
T = B * S
NT = T // P
H, HD = 16, 8
NK = 5
NE, NSH, TOPK, FH = 8, 2, 2, 256
FF2, T2 = 512, 512
I3 = 384
LAST = 8
EPS = 1e-5
MAGIC = 12582912.0
F32 = mybir.dt.float32
BF16 = mybir.dt.bfloat16
I32 = mybir.dt.int32
I8 = mybir.dt.int8
ALU = mybir.AluOpType
ACT = mybir.ActivationFunctionType
AX = mybir.AxisListType

ROWS = ["L0_xattn_bv", "L0_xattn_bo", "L1_xattn_wqg", "L1_xattn_wql", "L1_xattn_bqg", "L1_xattn_bql",
        "L1_xattn_wkg", "L1_xattn_wkl", "L1_xattn_bkg", "L1_xattn_bkl", "L1_xattn_wp", "L1_xattn_bp",
        "L1_ffn_weight_scale", "L1_ffn_bias", "L2_xattn_bk", "L2_xattn_bv", "L2_xattn_bo",
        "L2_xattn_bq", "L2_ffn_bias", "L3_xattn_b_v", "L3_xattn_b_o"]
COLS = ["L0_xattn_bq", "L0_xattn_bk", "L1_xattn_wvg", "L1_xattn_bvg", "L1_xattn_wvl", "L1_xattn_bvl",
        "L2_xattn_bq", "L3_xattn_b_q", "L3_xattn_b_k"]
NC_EXP = len(COLS)
MATS = ["L0_xattn_Wq", "L0_xattn_Wk", "L0_xattn_Wv", "L0_xattn_Wo",
        "L2_xattn_Wk", "L2_xattn_Wv", "L2_xattn_Wq", "L2_xattn_Wo",
        "L3_xattn_W_q", "L3_xattn_W_k", "L3_xattn_W_v", "L3_xattn_W_o"]
NQ = NE + NSH

C_ID = 0
C_HM = C_ID + P
C_NEGM = C_HM + 4
C_REF = C_NEGM + 1
C_IOTA = C_REF + S
C_END = C_IOTA + NE


def shape_constants():
    c = np.zeros((P, C_END), np.float32)
    p = np.arange(P)
    c[p, C_ID + p] = 1.0
    for h in range(4):
        c[:, C_HM + h] = (p // HD) % 4 == h
    c[:, C_NEGM] = -(p % S)
    c[:, C_REF:C_REF + S] = ((p % S) % NK - 3)[:, None] + np.arange(S)[None, :]
    c[:, C_IOTA:C_IOTA + NE] = np.arange(NE)
    return c


def row_picks():
    c = np.zeros((P, 26, P), np.float32)
    for b in range(2):
        for r in range(20):
            for part in range(3):
                c[S * b + 20 * part + r, r, S * b:S * b + S] = 1.0
                for g in range(2):
                    c[S * b + 20 * g + r, 20 + 3 * g + part, S * b + 20 * part + r] = 1.0
    return c.reshape(P, 26 * P)


def over(ap, axis, n):
    wide = ap.unsqueeze(axis)
    shape = list(wide.shape)
    shape[axis] = n
    return wide.broadcast_to(shape)


def build(nc, A, out):
    ctx = ExitStack()
    with ctx:
        def sb(name, shape, dt=F32):
            return ctx.enter_context(nc.sbuf_tensor(name, shape, dt))

        def sem(name):
            return ctx.enter_context(nc.semaphore(name))

        V, G, PE, AC = nc.vector, nc.gpsimd, nc.tensor, nc.scalar

        const = sb("const", [P, C_END])
        rows = sb("rows", [P, len(ROWS), D])
        cols = sb("cols", [P, NC_EXP + 4 * NQ + 2])
        mats = sb("mats", [P, len(MATS), D])
        woff = sb("woff", [P, 2, S])
        x_tm = sb("x_tm", [P, NT, D])
        h_tm = sb("h_tm", [P, NT, D])
        h_fm = sb("h_fm", [P, T])
        ctx_fm = sb("ctx_fm", [P, T])
        ctx_tm = sb("ctx_tm", [P, NT, D])
        stats = sb("stats", [P, NT, 6])
        mv = sb("mv", [P, NT, 2])
        rstd = sb("rstd", [P, NT])
        kexp = sb("kexp", [P, B * 4 * S])
        v4 = sb("v4", [P, B * 8 * 32])
        arena = sb("arena", [P, 10240])
        weights = sb("weights", [P, 8192])

        ps = ctx.enter_context(nc.psum_tensor("ps", [P, 8, 512], F32))

        def row(name):
            return rows[:, ROWS.index(name), :]

        def col(name):
            i = COLS.index(name)
            return cols[:, i:i + 1]

        def mat(name):
            return mats[:, MATS.index(name), :]

        ident = const[:, C_ID:C_ID + P]

        dve_chain, act_chain = sem("dve_chain"), sem("act_chain")
        chained = {"dve": 0, "act": 0}

        def dve_link(ins):
            chained["dve"] += 1
            ins.then_inc(dve_chain, 1)
            V.wait_ge(dve_chain, chained["dve"])

        def act_link(ins):
            chained["act"] += 1
            ins.then_inc(act_chain, 1)
            AC.wait_ge(act_chain, chained["act"])

        x_in, const_in, ctxf_in, ctxt_in = sem("x_in"), sem("const_in"), sem("ctxf_in"), sem("ctxt_in")
        rows_in, cols_in, mats_in = sem("rows_in"), sem("cols_in"), sem("mats_in")
        moe0_in, moe0_free = sem("moe0_in"), sem("moe0_free")
        x_done = sem("x_done")
        h_ready = sem("h_ready")
        hf_ready = sem("hf_ready")
        b3 = sb("b3", [NQ, D])
        gate_w = sb("gate_w", [P, NE])
        gate_b = sb("gate_b", [P, NE])
        w1 = weights[:, 0:NQ * FH].rearrange("p (e h) -> p e h", e=NQ)
        w2 = weights[:, NQ * FH:2 * NQ * FH].rearrange("p (e h) -> p e h", e=NQ)
        w3 = weights[:, 2 * NQ * FH:3 * NQ * FH].rearrange("p (e k d) -> p e k d", e=NQ, k=2)

        block = ctx.enter_context(nc.Block())

        @block.sync
        def _(sp):
            sp.dma_start(x_tm[:], A["x"].rearrange("(j p) d -> p j d", p=P)).then_inc(x_in, 16)
            sp.dma_start(const[:], A["const"]).then_inc(const_in, 16)
            sp.dma_start(mats[:], A["mats"]).then_inc(mats_in, 16)
            sp.dma_start(woff[:], A["woff"]).then_inc(mats_in, 16)
            sp.dma_start(w1, A["moe0_w1"]).then_inc(moe0_in, 16)
            sp.dma_start(w2, A["moe0_w2"]).then_inc(moe0_in, 16)
            sp.dma_start(w3, A["moe0_w3"]).then_inc(moe0_in, 16)
            sp.dma_start(b3[:], A["moe0_b3"]).then_inc(moe0_in, 16)
            sp.dma_start(gate_w[:], A["gate_w"]).then_inc(moe0_in, 16)
            sp.dma_start(gate_b[:], A["gate_b"].partition_broadcast(P)).then_inc(moe0_in, 16)

        @block.scalar
        def _(act):
            act.dma_start(ctx_fm[:], A["ctx_fm"]).then_inc(ctxf_in, 16)
            act.dma_start(cols[:], A["cols"]).then_inc(cols_in, 16)
            act.dma_start(rows[:], A["rows"].partition_broadcast(P)).then_inc(rows_in, 16)
            act.dma_start(ctx_tm[:], A["ctx"].rearrange("(j p) d -> p j d", p=P)).then_inc(ctxt_in, 16)

        v4_zero = sem("v4_zero")

        @block.gpsimd
        def _(pool):
            G.memset(v4[:], 0.0).then_inc(v4_zero, 1)

        n_sub, n_fm = [0], [0]
        stat_ready, std_ready, tr_ready = sem("var"), sem("std"), sem("hT")

        def layernorm(feature_major=True):
            n = n_sub[0]
            n_sub[0] += 1
            nf = n_fm[0]

            @block.vector
            def _(dve):
                if n == 0:
                    dve.wait_ge(x_in, 16)
                else:
                    dve.wait_ge(x_done, n)
                for j in range(NT):
                    ins = V.bn_stats(stats[:, j, :], x_tm[:, j, :])
                dve_link(ins)
                for j in range(NT):
                    ins = V.bn_aggr(mv[:, j, :], stats[:, j, :])
                dve_link(ins)
                V.tensor_scalar(rstd[:], mv[:, :, 1], EPS, None, ALU.add).then_inc(stat_ready, 1)
                dve.wait_ge(std_ready, n + 1)
                dve_link(V.reciprocal(rstd[:], rstd[:]))
                for j in range(NT):
                    ins = V.tensor_scalar(h_tm[:, j, :], x_tm[:, j, :], mv[:, j, 0:1], rstd[:, j:j + 1],
                                          ALU.subtract, ALU.mult)
                ins.then_inc(h_ready, 1)

            @block.scalar
            def _(act):
                act.wait_ge(stat_ready, n + 1)
                AC.activation(rstd[:], rstd[:], ACT.Sqrt).then_inc(std_ready, 1)
                if feature_major:
                    for k in range(2):
                        act.wait_ge(tr_ready, 2 * nf + k + 1)
                        AC.activation(h_fm[:, 512 * k:512 * k + 512], ps[:, 4 + k, :], ACT.Copy)\
                            .then_inc(hf_ready, 1)

            if feature_major:
                @block.tensor
                def _(pe):
                    if n == 0:
                        pe.wait_ge(const_in, 16)
                    pe.wait_ge(h_ready, n + 1)
                    for k in range(2):
                        for j in range(4):
                            ins = PE.transpose(ps[:, 4 + k, 128 * j:128 * j + 128], h_tm[:, 4 * k + j, :], ident)
                        ins.then_inc(tr_ready, 1)
                n_fm[0] += 1

        def wait_h_fm(eng):
            eng.wait_ge(hf_ready, 2 * n_fm[0])

        k_fm = sb("k_fm", [P, T])
        q_fm = sb("q_fm", [P, T])
        o_fm = sb("o_fm", [P, T])

        def attention(n, wq, wk, wv, wo, bq, bk, bv, bo, masked):
            s = lambda name: sem(f"a{n}_{name}")
            scale = 1.0 / float(np.sqrt(np.float32(HD)))
            kx = kexp[:].rearrange("p (b h k) -> p b h k", b=B, h=4)
            vx = v4[:].rearrange("p (b c m) -> p b c m", b=B, c=8)
            prob = [arena[:, 1024 * i:1024 * i + 1024] for i in range(2)]
            pT = [arena[:, 2048 + 1024 * i:3072 + 1024 * i] for i in range(2)]
            vdup = arena[:, 4096:4096 + 2048].rearrange("p (i b e) -> p i b e", i=4, b=4)
            mx = arena[:, 6144:6144 + 16]
            sm = arena[:, 6160:6160 + 32].rearrange("p (i h) -> p i h", i=2)
            ri = arena[:, 6208:6208 + 256].rearrange("p (i h d) -> p i h d", i=2, h=H)
            rb = arena[:, 6464:6464 + 128]
            bqs = arena[:, 6592:6593]
            bias = arena[:, 6656:6656 + 1024]
            masks = arena[:, 7680:7680 + 512].bitcast(I32).rearrange("p (j k) -> p j k", j=NT)
            unseen = arena[:, 8192:8192 + 512].bitcast(I32).rearrange("p (j k) -> p j k", j=NT)
            fill = arena[:, 8704:8705]
            tmp = prob[0]
            tmp2 = prob[1]
            nonf = pT[0].bitcast(I32)
            k_ps, k_sb, kx_ready = s("k_ps"), s("k_sb"), s("kx")
            v_ps, v_sb, vx_ready = s("v_ps"), s("v_sb"), s("vx")
            q_ps, q_sb, q_ok = s("q_ps"), s("q_sb"), s("q_ok")
            bq_ok = s("bq")
            sc_ready, sc_free = s("scores"), s("scores_read")
            sub_ready, exp_ready = s("less_max"), s("exp")
            ptT_ready, pt_ready = s("probsT"), s("probsT_sb")
            clean = s("clean")
            ri_ready, o_ready, rb_ready = s("rsum"), s("o_ps"), s("rsum_sb")
            of_ready, y_ready, y_added, bo_added = s("o_fm"), s("y"), s("y_added"), s("bo")
            if masked:
                bias_in = s("bias_in")

                @block.sync
                def _(sp):
                    sp.wait_ge(x_done, n)
                    for b in range(2):
                        sp.dma_start(bias[S * b:S * b + S, :].rearrange("q (h k) -> q h k", h=H),
                                     A["attn_bias"].rearrange("h q k -> q h k")).then_inc(bias_in, 16)
                    sp.dma_start(masks, A["attn_mask"].rearrange("(j p) k -> p j k", p=P))\
                        .then_inc(bias_in, 16)

            def guard_dve(t, width):
                for at in range(0, width, 1024):
                    v = t[:, at:at + 1024]
                    V.tensor_scalar(nonf, v, 0.0, 0.0, ALU.mult, ALU.not_equal)
                    V.tensor_scalar(tmp, v, 0.0, 1e4, ALU.max, ALU.min)
                    dve_link(V.tensor_scalar(tmp2, v, 0.0, -1e4, ALU.min, ALU.max))
                    dve_link(V.tensor_tensor(tmp, tmp, tmp2, ALU.add))
                    dve_link(V.copy_predicated(v, nonf, tmp))

            @block.tensor
            def _(pe):
                if n == 0:
                    pe.wait_ge(ctxf_in, 16)
                    pe.wait_ge(mats_in, 32)
                else:
                    pe.wait_ge(x_done, n)
                for k in range(2):
                    PE.matmul(ps[:, 6 + k, :], mat(wk), ctx_fm[:, 512 * k:512 * k + 512],
                              start=True, stop=True).then_inc(k_ps, 1)
                for g in range(4):
                    if g >= 2:
                        pe.wait_ge(v_sb, g - 1)
                    for b in range(4):
                        for h2 in range(2):
                            ins = PE.matmul(ps[64 * h2:64 * h2 + 64, g % 2, 128 * b:128 * b + 128],
                                            ctx_fm[:, (4 * g + b) * S:(4 * g + b + 1) * S], mat(wv),
                                            start=True, stop=True)
                    ins.then_inc(v_ps, 1)

            @block.scalar
            def _(act):
                if n == 0:
                    act.wait_ge(cols_in, 16)
                for k in range(2):
                    act.wait_ge(k_ps, k + 1)
                    AC.activation(k_fm[:, 512 * k:512 * k + 512], ps[:, 6 + k, :], ACT.Identity,
                                  bias=col(bk)).then_inc(k_sb, 1)

            @block.vector
            def _(dve):
                if n == 0:
                    dve.wait_ge(const_in, 16)
                    dve.wait_ge(cols_in, 16)
                    dve.wait_ge(rows_in, 16)
                else:
                    dve.wait_ge(x_done, n)
                V.tensor_scalar(bqs, col(bq), 1.0 if masked else scale, None, ALU.mult).then_inc(bq_ok, 1)
                if masked:
                    dve.wait_ge(bias_in, 48)
                    V.memset(fill, -1e4)
                    V.tensor_scalar(unseen, masks, 0, None, ALU.is_equal)
                    V.tensor_scalar(tmp, bias, 0.0, 1e4, ALU.max, ALU.min)
                    dve_link(V.tensor_scalar(tmp2, bias, 0.0, -1e4, ALU.min, ALU.max))
                    dve_link(V.tensor_tensor(bias, tmp, tmp2, ALU.add))
                dve.wait_ge(k_sb, 2)
                if masked:
                    guard_dve(k_fm[:], T)
                for k in range(2):
                    src = over(k_fm[:, 512 * k:512 * k + 512].rearrange("p (b k) -> p b k", b=8), 2, 4)
                    hm = over(over(const[:, C_HM:C_HM + 4], 2, S), 1, 8)
                    ins = V.tensor_tensor(kx[:, 8 * k:8 * k + 8], src, hm, ALU.mult)
                ins.then_inc(kx_ready, 1)
                for g in range(4):
                    dve.wait_ge(v_ps, g + 1)
                    V.tensor_tensor(vdup[:, g], ps[:, g % 2, :].rearrange("p (b e) -> p b e", b=4),
                                    over(row(bv), 1, 4), ALU.add).then_inc(v_sb, 1)
                dve.wait_ge(v_sb, 4)
                if masked:
                    guard_dve(vdup.rearrange("p i b e -> p (i b e)"), 2048)
                dve.wait_ge(v4_zero, 2 if masked else 1)
                for h2 in range(2):
                    for par in range(2):
                        r = slice(64 * h2, 64 * h2 + 64)
                        c0 = (par * 2 + h2) * HD
                        for g in range(4):
                            src = vdup[r, g].rearrange("p b (c h d) -> p b c h d", c=4, h=4)[:, :, :, par * 2 + h2, :]
                            dst = vx[r, 4 * g:4 * g + 4].rearrange("p b (c t) m -> p b c t m", t=2)[:, :, :, par, c0:c0 + HD]
                            ins = V.tensor_copy(dst, src)
                ins.then_inc(vx_ready, 1)

            layernorm()

            @block.tensor
            def _(pe):
                wait_h_fm(pe)
                pe.wait_ge(k_sb, 2)
                for k in range(2):
                    PE.matmul(ps[:, 6 + k, :], mat(wq), h_fm[:, 512 * k:512 * k + 512],
                              start=True, stop=True).then_inc(q_ps, 1)

            @block.scalar
            def _(act):
                act.wait_ge(bq_ok, 1)
                for k in range(2):
                    act.wait_ge(q_ps, k + 1)
                    AC.activation(q_fm[:, 512 * k:512 * k + 512], ps[:, 6 + k, :], ACT.Identity,
                                  bias=bqs, scale=1.0 if masked else scale).then_inc(q_sb, 1)

            if masked:
                @block.vector
                def _(dve):
                    dve.wait_ge(q_sb, 2)
                    guard_dve(q_fm[:], T)
                    V.tensor_scalar(q_fm[:], q_fm[:], scale, None, ALU.mult).then_inc(q_ok, 1)

            def scores(j):
                for g in range(4):
                    for b in range(2):
                        ins = PE.matmul(ps[64 * b:64 * b + 64, g, 0:256],
                                        q_fm[32 * g:32 * g + 32, j * P + 64 * b:j * P + 64 * b + 64],
                                        kx[32 * g:32 * g + 32, 2 * j + b].rearrange("p h k -> p (h k)"),
                                        start=True, stop=True)
                ins.then_inc(sc_ready, 1)

            @block.tensor
            def _(pe):
                pe.wait_ge(q_ok if masked else q_sb, 1 if masked else 2)
                pe.wait_ge(kx_ready, 1)
                pe.wait_ge(v_sb, 4)
                scores(0)
                for j in range(NT):
                    if j + 1 < NT:
                        pe.wait_ge(sc_free, j + 1)
                        scores(j + 1)
                    pe.wait_ge(clean if masked else exp_ready, j + 1)
                    if j >= 1:
                        pe.wait_ge(pt_ready, 2 * j)
                    for k in range(2):
                        for c in range(4):
                            ins = PE.transpose(ps[:, 4 + k, 128 * c:128 * c + 128],
                                               prob[j % 2][:, (4 * k + c) * 128:(4 * k + c + 1) * 128], ident)
                        ins.then_inc(ptT_ready, 1)
                    pe.wait_ge(pt_ready, 2 * j + 2)
                    if j == 0:
                        pe.wait_ge(vx_ready, 1)
                    if j >= 1:
                        pe.wait_ge(of_ready, j)
                    for b in range(2):
                        for c in range(8):
                            g = c // 2
                            PE.matmul(ps[32 * g:32 * g + 32, 6, 64 * b:64 * b + 64], vx[:, 2 * j + b, c, :],
                                      pT[j % 2][:, 128 * c + 64 * b:128 * c + 64 * b + 64],
                                      start=(c % 2 == 0), stop=(c % 2 == 1))
                    pe.wait_ge(ri_ready, j + 1)
                    PE.matmul(ps[:, 6, 128:256], ri[:, j % 2].rearrange("p h d -> p (h d)"), ident,
                              start=True, stop=True).then_inc(o_ready, 1)
                    pe.wait_ge(of_ready, j + 1)
                    if j >= 1:
                        pe.wait_ge(y_added, j)
                    PE.matmul(ps[:, 7, 0:128], o_fm[:, j * P:j * P + P], mat(wo), start=True, stop=True)\
                        .then_inc(y_ready, 1)

            @block.scalar
            def _(act):
                for j in range(NT):
                    act.wait_ge(sub_ready, j + 1)
                    AC.activation(prob[j % 2], prob[j % 2], ACT.Exp).then_inc(exp_ready, 1)
                    for k in range(2):
                        act.wait_ge(ptT_ready, 2 * j + k + 1)
                        AC.activation(pT[j % 2][:, 512 * k:512 * k + 512], ps[:, 4 + k, :], ACT.Copy)\
                            .then_inc(pt_ready, 1)
                    act.wait_ge(o_ready, j + 1)
                    if j >= 1:
                        act.wait_ge(of_ready, j)
                    AC.activation(rb, ps[:, 6, 128:256], ACT.Copy).then_inc(rb_ready, 1)

            def softmax_in(j):
                V.wait_ge(sc_ready, j + 1)
                if j >= 2:
                    V.wait_ge(ptT_ready, 2 * (j - 1))
                sc = ps[:, 0:4, 0:256].rearrange("p g (h k) -> p g h k", h=4)
                pr = prob[j % 2].rearrange("p (g h k) -> p g h k", g=4, h=4)
                pr3 = prob[j % 2].rearrange("p (h k) -> p h k", h=H)
                if masked:
                    V.tensor_tensor(pr, sc, bias.rearrange("p (g h k) -> p g h k", g=4, h=4), ALU.add)\
                        .then_inc(sc_free, 1)
                    V.wait_ge(sc_free, j + 1)
                    dve_link(V.copy_predicated(pr3, over(unseen[:, j], 1, H), over(fill.broadcast_to([P, S]), 1, H)))
                    dve_link(V.tensor_reduce(mx, pr3, AX.X, ALU.max))
                    V.tensor_tensor(pr3, pr3, over(mx, 2, S), ALU.subtract).then_inc(sub_ready, 1)
                else:
                    for g in range(4):
                        ins = V.tensor_reduce(mx[:, 4 * g:4 * g + 4], sc[:, g], AX.X, ALU.max)
                    dve_link(ins)
                    for g in range(4):
                        ins = V.tensor_tensor(pr[:, g], sc[:, g], over(mx[:, 4 * g:4 * g + 4], 2, S), ALU.subtract)
                    ins.then_inc(sub_ready, 1)
                    V.wait_ge(sub_ready, j + 1)
                    V.sem_inc(sc_free, 1)

            @block.vector
            def _(dve):
                dve.wait_ge(h_ready, n_sub[0])
                dve_link(V.tensor_tensor(x_tm[:], x_tm[:], over(row(bo), 1, NT), ALU.add))
                softmax_in(0)
                for j in range(NT):
                    dve.wait_ge(exp_ready, j + 1)
                    pr3 = prob[j % 2].rearrange("p (h k) -> p h k", h=H)
                    dve_link(V.tensor_reduce(sm[:, j % 2], pr3, AX.X, ALU.add))
                    dve_link(V.reciprocal(sm[:, j % 2], sm[:, j % 2]))
                    if masked:
                        V.tensor_scalar(prob[j % 2], prob[j % 2], 0.0, None, ALU.max).then_inc(clean, 1)
                        dve_link(V.tensor_scalar(sm[:, j % 2], sm[:, j % 2], 0.0, None, ALU.max))
                    V.tensor_copy(ri[:, j % 2], over(sm[:, j % 2], 2, HD)).then_inc(ri_ready, 1)
                    if j + 1 < NT:
                        softmax_in(j + 1)
                    dve.wait_ge(rb_ready, j + 1)
                    V.tensor_tensor(o_fm[:, j * P:j * P + P], ps[:, 6, 0:128], rb, ALU.mult).then_inc(of_ready, 1)
                    dve.wait_ge(y_ready, j + 1)
                    ins = V.tensor_tensor(x_tm[:, j], x_tm[:, j], ps[:, 7, 0:128], ALU.add)
                    ins.then_inc(y_added, 1)
                dve.wait_ge(y_added, NT)
                V.sem_inc(x_done, 1)

        attention(0, "L0_xattn_Wq", "L0_xattn_Wk", "L0_xattn_Wv", "L0_xattn_Wo", "L0_xattn_bq",
                  "L0_xattn_bk", "L0_xattn_bv", "L0_xattn_bo", False)
        def moe0(n):
            s = lambda name: sem(f"moe0_{name}")
            lg_ps, lg_read, gates_ok, gT_ps, gT_ok = s("logits"), s("logits_read"), s("gates"), s("gatesT"), s("gatesT_sb")
            shifted, powered = s("less_max"), s("exp")
            by_ps, by_read = s("bias_ps"), s("bias_added")
            up_ps, silu_ok, glu_ok, y_ps, y_added = s("up_ps"), s("silu"), s("glu"), s("y_ps"), s("y_added")
            lin_ps = s("lin_ps")
            lg = arena[:, 0:64].rearrange("p (j e) -> p j e", j=NT)
            pr = arena[:, 64:128].rearrange("p (j e) -> p j e", j=NT)
            t1 = arena[:, 128:192].rearrange("p (j e) -> p j e", j=NT)
            t2 = arena[:, 192:256].rearrange("p (j e) -> p j e", j=NT)
            first = arena[:, 256:320].rearrange("p (j e) -> p j e", j=NT)
            m8 = arena[:, 320:328]
            back = arena[:, 328:336]
            gates = arena[:, 336:336 + NT * NQ].rearrange("p (j e) -> p j e", j=NT)
            gT = arena[0:NQ, 512:512 + T]
            silu = arena[:, 2048:2048 + 1024].rearrange("p (k t) -> p k t", k=2)
            glu = arena[:, 4096:4096 + 2048].rearrange("p (i k t) -> p i k t", i=2, k=2)
            units = [(e, half) for e in range(NQ) for half in range(2)]

            def bias_col(which, e, k):
                i = NC_EXP + which * 2 * NQ + 2 * e + k
                return cols[:, i:i + 1]

            @block.tensor
            def _(pe):
                pe.wait_ge(moe0_in, 96)
                wait_h_fm(pe)
                for j in range(NT):
                    ins = PE.matmul(ps[:, 6, NE * j:NE * j + NE], h_fm[:, j * P:j * P + P], gate_w[:],
                                    start=True, stop=True)
                ins.then_inc(lg_ps, 1)

            @block.scalar
            def _(act):
                act.wait_ge(shifted, 1)
                AC.activation(pr, t1, ACT.Exp).then_inc(powered, 1)

            def pick_first(src, dst):
                dve_link(V.tensor_reduce(m8, src, AX.X, ALU.max))
                dve_link(V.tensor_tensor(t2, src, over(m8, 2, NE), ALU.is_equal))
                dve_link(V.tensor_tensor(t2, t2, over(back, 1, NT), ALU.mult))
                dve_link(V.tensor_reduce(m8, t2, AX.X, ALU.max))
                dve_link(V.tensor_tensor(dst, t2, over(m8, 2, NE), ALU.is_equal))

            @block.vector
            def _(dve):
                V.tensor_scalar(back, const[:, C_IOTA:C_IOTA + NE], -1.0, float(NE), ALU.mult, ALU.add)
                V.memset(gates, 1.0 / NSH)
                dve.wait_ge(moe0_in, 96)
                dve.wait_ge(lg_ps, 1)
                dve_link(V.tensor_tensor(lg, ps[:, 6, 0:64].rearrange("p (j e) -> p j e", j=NT),
                                         over(gate_b[:], 1, NT), ALU.add))
                dve_link(V.tensor_reduce(m8, lg, AX.X, ALU.max))
                V.tensor_tensor(t1, lg, over(m8, 2, NE), ALU.subtract).then_inc(shifted, 1)
                dve.wait_ge(powered, 1)
                dve_link(V.tensor_reduce(m8, pr, AX.X, ALU.add))
                dve_link(V.reciprocal(m8, m8))
                dve_link(V.tensor_tensor(pr, pr, over(m8, 2, NE), ALU.mult))
                pick_first(pr, first)
                dve_link(V.scalar_tensor_tensor(out=t1, in0=first, scalar=-2.0, in1=pr, op0=ALU.mult, op1=ALU.add))
                dve_link(V.tensor_tensor(lg, first, pr, ALU.mult))
                pick_first(t1, first)
                dve_link(V.tensor_tensor(first, first, pr, ALU.mult))
                V.tensor_tensor(gates[:, :, 0:NE], lg, first, ALU.add).then_inc(gates_ok, 1)

            @block.tensor
            def _(pe):
                def up(u):
                    e, half = units[u]
                    t = slice(512 * half, 512 * half + 512)
                    for k in range(2):
                        if u >= 1:
                            pe.wait_ge(silu_ok, 2 * (u - 1) + k + 1)
                        PE.matmul(ps[:, k, :], w1[:, e, P * k:P * k + P], h_fm[:, t], start=True, stop=True)\
                            .then_inc(up_ps, 1)
                    for k in range(2):
                        if u >= 1:
                            pe.wait_ge(glu_ok, 2 * (u - 1) + k + 1)
                        PE.matmul(ps[:, 2 + k, :], w2[:, e, P * k:P * k + P], h_fm[:, t], start=True, stop=True)\
                            .then_inc(lin_ps, 1)

                def down(u):
                    e, half = units[u]
                    pe.wait_ge(glu_ok, 2 * u + 2)
                    if u >= 2:
                        pe.wait_ge(y_added, u - 1)
                    for t in range(4):
                        for k in range(2):
                            ins = PE.matmul(ps[:, 4 + u % 2, P * t:P * t + P], glu[:, u % 2, k, P * t:P * t + P],
                                            w3[:, e, k, :], start=(k == 0), stop=(k == 1))
                    ins.then_inc(y_ps, 1)

                up(0)
                up(1)
                for u in range(len(units)):
                    if u >= 1 and u + 1 < len(units):
                        up(u + 1)
                    if u == 1:
                        pe.wait_ge(gates_ok, 1)
                        for k in range(2):
                            for j in range(4):
                                ins = PE.transpose(ps[0:NQ, 6 + k, P * j:P * j + P], gates[:, 4 * k + j, :], ident)
                            ins.then_inc(gT_ps, 1)
                        pe.wait_ge(gT_ok, 2)
                        for k in range(2):
                            for j in range(4):
                                ins = PE.matmul(ps[:, 6 + k, P * j:P * j + P],
                                                gT[:, (4 * k + j) * P:(4 * k + j + 1) * P], b3[:], start=True, stop=True)
                            ins.then_inc(by_ps, 1)
                    down(u)

            @block.scalar
            def _(act):
                for u, (e, half) in enumerate(units):
                    for k in range(2):
                        act.wait_ge(up_ps, 2 * u + k + 1)
                        if u >= 1:
                            act.wait_ge(glu_ok, 2 * (u - 1) + k + 1)
                        AC.activation(silu[:, k, :], ps[:, k, :], ACT.Silu, bias=bias_col(0, e, k)).then_inc(silu_ok, 1)
                    if u == 1:
                        for k in range(2):
                            act.wait_ge(gT_ps, k + 1)
                            AC.activation(gT[:, 512 * k:512 * k + 512], ps[0:NQ, 6 + k, :], ACT.Copy).then_inc(gT_ok, 1)

            @block.vector
            def _(dve):
                dve.wait_ge(gates_ok, 1)

                def accumulate(u):
                    e, half = units[u]
                    dve.wait_ge(y_ps, u + 1)
                    if u >= 2:
                        dve.wait_ge(y_added, u - 1)
                    for t in range(4):
                        j = 4 * half + t
                        ins = V.scalar_tensor_tensor(out=x_tm[:, j], in0=ps[:, 4 + u % 2, P * t:P * t + P],
                                                     scalar=gates[:, j, e:e + 1], in1=x_tm[:, j],
                                                     op0=ALU.mult, op1=ALU.add)
                    ins.then_inc(y_added, 1)

                for u, (e, half) in enumerate(units):
                    for k in range(2):
                        dve.wait_ge(lin_ps, 2 * u + k + 1)
                        dve.wait_ge(silu_ok, 2 * u + k + 1)
                        if u >= 2:
                            dve.wait_ge(y_ps, u - 1)
                        V.scalar_tensor_tensor(out=glu[:, u % 2, k, :], in0=ps[:, 2 + k, :], scalar=bias_col(1, e, k),
                                               in1=silu[:, k, :], op0=ALU.add, op1=ALU.mult).then_inc(glu_ok, 1)
                    if u == 2:
                        for k in range(2):
                            dve.wait_ge(by_ps, k + 1)
                            dve_link(V.tensor_tensor(x_tm[:, 4 * k:4 * k + 4], x_tm[:, 4 * k:4 * k + 4],
                                                     ps[:, 6 + k, :].rearrange("p (j d) -> p j d", j=4), ALU.add))
                    if u >= 2:
                        accumulate(u - 2)
                accumulate(len(units) - 2)
                accumulate(len(units) - 1)
                dve.wait_ge(y_added, len(units))
                V.sem_inc(x_done, 1)

        if LAST >= 2:
            layernorm()
            moe0(1)

        def channel_attention(n):
            s = lambda name: sem(f"chan_{name}")
            q_ok, kg_ok, vg_ok, s_ps, sub_ok, e_ok, n_ok, ab_ok, y_ps = (
                s("q"), s("k"), s("v"), s("scores"), s("less_max"), s("exp"), s("attn"), s("attnT"), s("y"))
            zeroed = s("zeroed")
            sets = 2
            qa = arena[:, 0:2048].rearrange("p (s j c) -> p s j c", s=2, j=NT)
            ka = arena[:, 2048:4096].rearrange("p (s j c) -> p s j c", s=2, j=NT)
            va = arena[:, 4096:6144].rearrange("p (s t) -> p s t", s=2)
            at = arena[:, 6144:7168].rearrange("p (m e) -> p m e", e=32)
            m32 = arena[:, 7168:7200]
            att = arena[:, 7424:8448].rearrange("p (j c) -> p j c", j=NT)
            ab = kexp[:].rearrange("p (m c) -> p m c", c=P)

            @block.gpsimd
            def _(pool):
                pool.wait_ge(x_done, 1)
                G.memset(kexp[:], 0.0).then_inc(zeroed, 1)
                pool.wait_ge(x_done, n)
                pool.wait_ge(ctxt_in, 16)
                for i, name in enumerate(("g", "l")):
                    G.tensor_tensor(ka[:, i], ctx_tm[:], over(row(f"L1_xattn_wk{name}"), 1, NT), ALU.mult)\
                        .then_inc(kg_ok, 1)
                    pool.wait_ge(kg_ok, 2 * i + 1)
                    G.tensor_tensor(ka[:, i], ka[:, i], over(row(f"L1_xattn_bk{name}"), 1, NT), ALU.add)\
                        .then_inc(kg_ok, 1)

            @block.scalar
            def _(act):
                act.wait_ge(x_done, n)
                for i, name in enumerate(("g", "l")):
                    AC.activation(va[:, i], ctx_fm[:], ACT.Identity, bias=col(f"L1_xattn_bv{name}"),
                                  scale=col(f"L1_xattn_wv{name}")).then_inc(vg_ok, 1)

            layernorm(feature_major=False)

            @block.vector
            def _(dve):
                dve.wait_ge(h_ready, n_sub[0])
                for i, name in enumerate(("g", "l")):
                    dve_link(V.tensor_tensor(qa[:, i], h_tm[:], over(row(f"L1_xattn_wq{name}"), 1, NT), ALU.mult))
                    V.tensor_tensor(qa[:, i], qa[:, i], over(row(f"L1_xattn_bq{name}"), 1, NT), ALU.add)\
                        .then_inc(q_ok, 1)
                dve_link(V.tensor_tensor(x_tm[:], x_tm[:], over(row("L1_xattn_bp"), 1, NT), ALU.add))

            @block.tensor
            def _(pe):
                for i in range(sets):
                    pe.wait_ge(kg_ok, 2 * i + 2)
                    pe.wait_ge(q_ok, i + 1)
                    for b in range(B):
                        r = slice(S * (b % 2), S * (b % 2) + S)
                        for h in range(4):
                            c = slice(32 * h, 32 * h + 32)
                            ins = PE.matmul(ps[c, 2 * i + b % 2, 32 * (b // 2):32 * (b // 2) + 32], qa[r, i, b // 2, c], ka[r, i, b // 2, c],
                                            start=True, stop=True)
                    ins.then_inc(s_ps, 1)
                pe.wait_ge(vg_ok, 2)
                pe.wait_ge(ab_ok, 1)
                for j in range(NT):
                    for half in range(2):
                        b = 2 * j + half
                        for i in range(sets):
                            ins = PE.matmul(ps[S * half:S * half + S, 4 + j // 4, P * (j % 4):P * (j % 4) + P],
                                            va[:, i, S * b:S * b + S], ab[:, B * i + NT * half + j, :],
                                            start=(i == 0), stop=(i == 1))
                    if j % 4 == 3:
                        ins.then_inc(y_ps, 1)

            @block.vector
            def _(dve):
                for i in range(sets):
                    mi = slice(B * i, B * i + B)
                    dve.wait_ge(s_ps, i + 1)
                    sc = ps[:, 2 * i:2 * i + 2, 0:256].rearrange("p b (m e) -> p b m e", e=32)
                    pair = lambda v: v.rearrange("p (b m) -> p b m", b=2)
                    dve_link(V.tensor_reduce(pair(m32[:, mi]), sc, AX.X, ALU.max))
                    V.tensor_tensor(at[:, mi].rearrange("p (b m) e -> p b m e", b=2), sc,
                                    over(pair(m32[:, mi]), 3, 32), ALU.subtract).then_inc(sub_ok, 1)
                for i in range(sets):
                    mi = slice(B * i, B * i + B)
                    dve.wait_ge(e_ok, i + 1)
                    dve_link(V.tensor_reduce(m32[:, mi], at[:, mi], AX.X, ALU.add))
                    dve_link(V.reciprocal(m32[:, mi], m32[:, mi]))
                    dve_link(V.tensor_tensor(at[:, mi], at[:, mi], over(m32[:, mi], 2, 32), ALU.mult))
                dve.wait_ge(zeroed, 1)
                for h in range(4):
                    c = slice(32 * h, 32 * h + 32)
                    ins = V.transpose(ab[c, :, c], at[c])
                ins.then_inc(ab_ok, 1)
                for k in range(2):
                    dve.wait_ge(y_ps, k + 1)
                    dve_link(V.scalar_tensor_tensor(out=att[:, 4 * k:4 * k + 4],
                                                    in0=ps[:, 4 + k, :].rearrange("p (j c) -> p j c", j=4), scalar=2.0,
                                                    in1=over(row("L1_xattn_wp"), 1, 4), op0=ALU.mult, op1=ALU.mult))
                    ins = V.tensor_tensor(x_tm[:, 4 * k:4 * k + 4], x_tm[:, 4 * k:4 * k + 4], att[:, 4 * k:4 * k + 4],
                                          ALU.add)
                    dve_link(ins)
                V.sem_inc(x_done, 1)

            @block.scalar
            def _(act):
                for i in range(sets):
                    act.wait_ge(sub_ok, i + 1)
                    AC.activation(at[:, B * i:B * i + B], at[:, B * i:B * i + B], ACT.Exp,
                                  scale=float(D) ** -0.5).then_inc(e_ok, 1)

        if LAST >= 3:
            channel_attention(2)

        wq8_in = sem("wq8_in")
        wq8 = sb("wq8", [P, P], I32)
        wq8b = sb("wq8b", [P, P], BF16)
        ident_b = sb("ident_b", [P, P], BF16)

        def int8_linear(n):
            s = lambda name: sem(f"int8_{name}")
            xq_ok, xT_ps, xT_ok, y_ps, w_ok = s("x"), s("xT_ps"), s("xT"), s("y"), s("w")
            am = arena[:, 0:8]
            xs = arena[:, 8:16]
            inv = arena[:, 16:24]
            t = arena[:, 1024:2048].rearrange("p (j c) -> p j c", j=NT)
            y = arena[:, 2048:3072].rearrange("p (j c) -> p j c", j=NT)
            xq = arena[:, 3072:3584].bitcast(BF16).rearrange("p (j c) -> p j c", j=NT)
            xT = arena[:, 3584:4096].bitcast(BF16)

            @block.sync
            def _(sp):
                sp.dma_start(wq8[:], A["wq8"]).then_inc(wq8_in, 16)

            layernorm(feature_major=False)

            @block.vector
            def _(dve):
                dve.wait_ge(wq8_in, 16)
                V.tensor_copy(wq8b[:], wq8[:]).then_inc(w_ok, 1)
                V.tensor_copy(ident_b[:], ident).then_inc(w_ok, 1)
                dve.wait_ge(h_ready, n_sub[0])
                dve_link(V.tensor_reduce(am, h_tm[:], AX.X, ALU.max, apply_absolute_value=True))
                dve_link(V.tensor_scalar(xs, am, 1e-6, 1.0 / 127.0, ALU.max, ALU.mult))
                dve_link(V.reciprocal(inv, xs))
                dve_link(V.tensor_tensor(t, h_tm[:], over(inv, 2, D), ALU.mult))
                dve_link(V.tensor_scalar(t, t, MAGIC, -MAGIC, ALU.add, ALU.add))
                V.tensor_scalar(xq, t, -128.0, 127.0, ALU.max, ALU.min).then_inc(xq_ok, 1)
                dve_link(V.tensor_tensor(x_tm[:], x_tm[:], over(row("L1_ffn_bias"), 1, NT), ALU.add))
                for k in range(2):
                    r = slice(4 * k, 4 * k + 4)
                    dve.wait_ge(y_ps, k + 1)
                    dve_link(V.tensor_tensor(y[:, r], ps[:, 2 + k, :].rearrange("p (j c) -> p j c", j=4),
                                             over(xs[:, r], 2, D), ALU.mult))
                    dve_link(V.tensor_tensor(y[:, r], y[:, r], over(row("L1_ffn_weight_scale"), 1, 4), ALU.mult))
                    dve_link(V.tensor_tensor(x_tm[:, r], x_tm[:, r], y[:, r], ALU.add))
                V.sem_inc(x_done, 1)

            @block.tensor
            def _(pe):
                pe.wait_ge(w_ok, 2)
                pe.wait_ge(xq_ok, 1)
                tp = ps[:, 0, :].bitcast(BF16)
                for j in range(NT):
                    ins = PE.transpose(tp[:, P * j:P * j + P], xq[:, j], ident_b[:])
                ins.then_inc(xT_ps, 1)
                pe.wait_ge(xT_ok, 1)
                for k in range(2):
                    for j in range(4):
                        i = 4 * k + j
                        ins = PE.matmul(ps[:, 2 + k, P * j:P * j + P], xT[:, P * i:P * i + P], wq8b[:],
                                        start=True, stop=True)
                    ins.then_inc(y_ps, 1)

            @block.scalar
            def _(act):
                act.wait_ge(xT_ps, 1)
                AC.activation(xT, ps[:, 0, :].bitcast(BF16), ACT.Copy).then_inc(xT_ok, 1)

        if LAST >= 4:
            int8_linear(3)

        mask_sb = sb("mask_sb", [P, NT, S], I32)
        picks_b = sb("picks_b", [P, 26, P], BF16)
        l2buf = sb("l2buf", [P, 8192])
        mask_in, picks_in, picks_ok = sem("mask_in"), sem("picks_in"), sem("picks_ok")

        def deformable(n):
            s = lambda name: sem(f"def_{name}")
            kv_zero, kv_ps, kv_ok = s("kv_zero"), s("kv_ps"), s("kv")
            q_ps, q_sb, qt_ps, qt_ok, qx_ok = s("q_ps"), s("q_sb"), s("qt_ps"), s("qt"), s("qx")
            off_ps, parts_ok, mv_ps, ix_ok = s("off_ps"), s("parts"), s("moved_ps"), s("ix")
            bc_ps, abs_ok, hat_ok, smp_ps = s("bc_ps"), s("abs"), s("hat"), s("sampled_ps")
            v_ok, prod_ok, sc_ok, e_ok, c_ok, cT_ps, cT_ok, y_ps = (
                s("sv"), s("prod"), s("scores"), s("exp"), s("ctx"), s("ctxT_ps"), s("ctxT"), s("y"))
            off_sb = s("off_sb")
            kv = kexp[:].rearrange("p (j h v b d) -> p j h v b d", j=NT, h=H, v=2, b=2)
            kvc = kexp[:].rearrange("p (j h m) -> p j h m", j=NT, h=H)
            hats = arena[:].rearrange("p (i r c) -> p i r c", i=2, r=20)
            sign = v4[:, 0:8]
            inv = v4[:, 8:16]
            msum = v4[:, 16:24]
            qt = v4[:, 64:1088].rearrange("p (i h b d) -> p i h b d", i=4, h=H, b=2)
            cx = v4[:, 1088:2112].rearrange("p (i b c) -> p i b c", i=4, b=2)
            prod = v4[:, 2112:2752].rearrange("p (i r c) -> p i r c", i=2, c=16)
            sc = v4[:, 2752:2752 + 320].rearrange("p (i r b) -> p i r b", i=2, b=2)
            mx = v4[:, 3072:3104]
            rs = v4[:, 3104:3136]
            off = l2buf[:, 0:1024].rearrange("p (g c) -> p g c", g=2)
            t1 = l2buf[:, 1024:2048].rearrange("p (g c) -> p g c", g=2)
            t2 = l2buf[:, 2048:3072].rearrange("p (g c) -> p g c", g=2)
            parts = l2buf[:, 3072:4608].bitcast(BF16).rearrange("p (i g c) -> p i g c", i=3, g=2)
            ixm = l2buf[:, 4608:5632].bitcast(BF16).rearrange("p (g c) -> p g c", g=4)
            qx = l2buf[:, 0:2560].rearrange("p (i r c) -> p i r c", i=2, c=16)
            sv = l2buf[:, 5632:8192].rearrange("p (i r c) -> p i r c", i=2, c=16)
            units = [(hg, half) for hg in range(4) for half in range(2)]
            qscale = -0.5 / float(np.sqrt(HD))

            @block.gpsimd
            def _(pool):
                pool.wait_ge(x_done, 3)
                G.memset(kexp[:], 0.0).then_inc(kv_zero, 1)

            @block.tensor
            def _(pe):
                pe.wait_ge(x_done, n)
                for j in range(NT):
                    wkv = mats[:, MATS.index("L2_xattn_Wk"):MATS.index("L2_xattn_Wk") + 2, :].rearrange("p a b -> p (a b)")
                    PE.matmul(ps[:, j // 2, 256 * (j % 2):256 * (j % 2) + 256], ctx_fm[:, P * j:P * j + P],
                              wkv, start=True, stop=True).then_inc(kv_ps, 1)

            layernorm()

            @block.vector
            def _(dve):
                dve.wait_ge(mask_in, 32)
                dve_link(V.tensor_reduce(msum, mask_sb[:], AX.X, ALU.add))
                dve_link(V.tensor_scalar(sign, msum, -1.0, float(S - 1), ALU.mult, ALU.add))
                dve_link(V.reciprocal(inv, sign))
                dve.wait_ge(kv_zero, 1)
                i = ROWS.index("L2_xattn_bk")
                for bank in range(4):
                    dve.wait_ge(kv_ps, 2 * bank + 2)
                    for b in range(2):
                        r = slice(S * b, S * b + S)
                        for v in range(2):
                            src = ps[r, bank, :].rearrange("p (j v h d) -> p j v h d", j=2, v=2, h=H)[:, :, v]
                            bias = over(rows[r, i + v, :].rearrange("p (h d) -> p h d", h=H), 1, 2)
                            ins = V.tensor_tensor(kv[r, 2 * bank:2 * bank + 2, :, v, b, :], src, bias, ALU.add)
                ins.then_inc(kv_ok, 1)
                dve_link(V.tensor_tensor(x_tm[:], x_tm[:], over(row("L2_xattn_bo"), 1, NT), ALU.add))

            @block.tensor
            def _(pe):
                wait_h_fm(pe)
                for k in range(2):
                    PE.matmul(ps[:, 6 + k, :], mat("L2_xattn_Wq"), h_fm[:, 512 * k:512 * k + 512],
                              start=True, stop=True).then_inc(q_ps, 1)
                pe.wait_ge(kv_ok, 1)
                pe.wait_ge(q_sb, 2)
                qv = q_fm[:].rearrange("p (j b q) -> p j b q", j=NT, b=2)
                for g in range(2):
                    for b in range(2):
                        ins = PE.matmul(ps[S * b:S * b + S, 2 + g, :], woff[:, g, :], qv[:, :, b, :], start=True, stop=True)
                    ins.then_inc(off_ps, 1)
                for j in range(NT):
                    for b in range(2):
                        c = (j // 2) * 256 + P * b
                        ins = PE.matmul(ps[S * (j % 2):S * (j % 2) + S, c // 512, c % 512:c % 512 + P],
                                        h_fm[:, P * j + S * b:P * j + S * b + S], mat("L2_xattn_Wq"), start=True, stop=True)
                ins.then_inc(qt_ps, 1)
                pe.wait_ge(parts_ok, 1)
                pe.wait_ge(qt_ok, 1)
                for hg in range(4):
                    g = hg // 2
                    for i in range(3):
                        ins = PE.matmul(ps[:, 4 + hg, :], picks_b[:, 20 + 3 * (hg % 2) + i, :], parts[:, i, g, :],
                                        start=(i == 0), stop=(i == 2))
                    ins.then_inc(mv_ps, 1)

            @block.scalar
            def _(act):
                for k in range(2):
                    act.wait_ge(q_ps, k + 1)
                    AC.activation(q_fm[:, 512 * k:512 * k + 512], ps[:, 6 + k, :], ACT.Identity,
                                  bias=col("L2_xattn_bq")).then_inc(q_sb, 1)
                for g in range(2):
                    act.wait_ge(off_ps, g + 1)
                    AC.activation(off[:, g, :], ps[:, 2 + g, :], ACT.Identity,
                                  bias=cols[:, NC_EXP + 4 * NQ + g:NC_EXP + 4 * NQ + g + 1]).then_inc(off_sb, 1)
                for hg in range(4):
                    act.wait_ge(mv_ps, hg + 1)
                    AC.activation(ixm[:, hg, :], ps[:, 4 + hg, :], ACT.Copy).then_inc(ix_ok, 1)

            @block.vector
            def _(dve):
                def jq(v, g):
                    return v[:, g, :].rearrange("p (j q) -> p j q", j=NT)

                for g in range(2):
                    dve.wait_ge(off_sb, g + 1)
                    ref = over(const[:, C_REF:C_REF + S], 1, NT)
                    sg, iv = over(sign, 2, S), over(inv, 2, S)
                    dve_link(V.tensor_tensor(jq(off, g), jq(off, g), ref, ALU.add))
                    dve_link(V.tensor_tensor(jq(t1, g), jq(off, g), iv, ALU.mult))
                    dve_link(V.tensor_scalar(t1[:, g], t1[:, g], MAGIC, -MAGIC, ALU.add, ALU.add))
                    dve_link(V.tensor_tensor(jq(t1, g), jq(t1, g), sg, ALU.mult))
                    dve_link(V.tensor_tensor(off[:, g], off[:, g], t1[:, g], ALU.subtract))
                    dve_link(V.tensor_tensor(jq(t1, g), jq(off, g), iv, ALU.mult))
                    dve_link(V.tensor_scalar(t1[:, g], t1[:, g], 0.0, None, ALU.is_lt))
                    dve_link(V.tensor_tensor(jq(t1, g), jq(t1, g), sg, ALU.mult))
                    dve_link(V.tensor_tensor(off[:, g], off[:, g], t1[:, g], ALU.add))
                    dve_link(V.tensor_scalar(off[:, g], off[:, g], float(S) / (S - 1), -0.5, ALU.mult, ALU.add))
                    dve_link(V.tensor_copy(parts[:, 0, g], off[:, g]))
                    dve_link(V.tensor_tensor(t1[:, g], off[:, g], parts[:, 0, g], ALU.subtract))
                    dve_link(V.tensor_copy(parts[:, 1, g], t1[:, g]))
                    ins = V.tensor_tensor(parts[:, 2, g], t1[:, g], parts[:, 1, g], ALU.subtract)
                ins.then_inc(parts_ok, 1)
                dve.wait_ge(qt_ps, 1)
                for c in range(4):
                    src = ps[:, c // 2, 256 * (c % 2):256 * (c % 2) + 256].rearrange("p (b h d) -> p h b d", b=2, h=H)
                    bias = over(row("L2_xattn_bq").rearrange("p (h d) -> p h d", h=H), 2, 2)
                    ins = V.tensor_tensor(qt[:, c], src, bias, ALU.add)
                ins.then_inc(qt_ok, 1)

            def half_buf(hg, half):
                return hats[:, (2 * hg + half) % 2]

            @block.tensor
            def _(pe):
                def broadcast(u):
                    hg, half = units[u]
                    for c in range(10):
                        m = 10 * u + c
                        if m >= 4:
                            pe.wait_ge(abs_ok, m - 3)
                        for i in range(2):
                            ins = PE.matmul(ps[:, m % 4, 256 * i:256 * i + 256], picks_b[:, 2 * c + i, :],
                                            ixm[:, hg, 256 * half:256 * half + 256], start=True, stop=True)
                        ins.then_inc(bc_ps, 1)

                def sample(u):
                    hg, half = units[u]
                    pe.wait_ge(hat_ok, 10 * (u + 1))
                    for i in range(2):
                        w = 2 * u + i
                        if w >= 2:
                            pe.wait_ge(v_ok, w - 1)
                            pe.wait_ge(prod_ok, w - 1)
                        for par in range(2):
                            j = 4 * half + 2 * i + par
                            for r in range(20):
                                hl = r // NK
                                ins = PE.matmul(ps[S * par:S * par + S, 4 + 2 * (w % 2) + r // 10,
                                                   32 * (r % 10):32 * (r % 10) + 32],
                                                hats[:, u % 2, r, S * (2 * i + par):S * (2 * i + par) + S],
                                                kvc[:, j, 4 * hg + hl, :], start=True, stop=True)
                        ins.then_inc(smp_ps, 1)

                pe.wait_ge(ix_ok, 4)
                broadcast(0)
                for u in range(len(units)):
                    if u + 1 < len(units):
                        broadcast(u + 1)
                    sample(u)
                pe.wait_ge(c_ok, 4)
                for jp in range(4):
                    for b in range(2):
                        ins = PE.transpose(ps[:, jp // 2, 256 * (jp % 2) + P * b:256 * (jp % 2) + P * b + P],
                                           cx[:, jp, b, :], ident)
                    if jp % 2 == 1:
                        ins.then_inc(cT_ps, 1)
                for k in range(2):
                    pe.wait_ge(cT_ok, k + 1)
                    for i in range(4):
                        j = 4 * k + i
                        ins = PE.matmul(ps[:, 2 + k, P * i:P * i + P], o_fm[:, P * j:P * j + P], mat("L2_xattn_Wo"),
                                        start=True, stop=True)
                    ins.then_inc(y_ps, 1)

            @block.scalar
            def _(act):
                act.wait_ge(qt_ok, 1)

                def spread_q(hg):
                    if hg >= 2:
                        act.wait_ge(prod_ok, 4 * (hg - 1))
                    for jp in range(4):
                        src = over(qt[:, jp, 4 * hg:4 * hg + 4].rearrange("p h b d -> p h (b d)"), 2, NK)
                        dst = qx[:, hg % 2, 20 * jp:20 * jp + 20].rearrange("p (h k) c -> p h k c", h=4)
                        ins = AC.activation(dst, src, ACT.Copy, scale=qscale)
                    ins.then_inc(qx_ok, 1)

                def absolute(u):
                    for c in range(10):
                        m = 10 * u + c
                        act.wait_ge(bc_ps, m + 1)
                        if u >= 2 and c == 0:
                            act.wait_ge(smp_ps, 2 * (u - 1))
                        AC.activation(hats[:, u % 2, 2 * c:2 * c + 2, :].rearrange("p r c -> p (r c)"), ps[:, m % 4, :],
                                      ACT.Abs, bias=const[:, C_NEGM:C_NEGM + 1]).then_inc(abs_ok, 1)

                absolute(0)
                spread_q(0)
                for u, (hg, half) in enumerate(units):
                    if u + 1 < len(units):
                        absolute(u + 1)
                    if half == 0 and hg + 1 < 4:
                        spread_q(hg + 1)
                    for i in range(2):
                        w = 2 * u + i
                        act.wait_ge(prod_ok, w + 1)
                        if w % 4 == 0 and hg >= 2:
                            act.wait_ge(c_ok, hg - 1)
                        jp = 2 * half + i
                        src = ps[:, 4 + 2 * (w % 2):6 + 2 * (w % 2), 0:320].rearrange("p k (r c) -> p k r c", c=32)[:, :, :, 16:32]
                        dst = sv[:, hg % 2, 20 * jp:20 * jp + 20].rearrange("p (k r) c -> p k r c", k=2)
                        AC.activation(dst, src, ACT.Copy).then_inc(v_ok, 1)
                    if half == 1:
                        act.wait_ge(sc_ok, hg + 1)
                        AC.activation(sc[:, hg % 2], sc[:, hg % 2], ACT.Exp).then_inc(e_ok, 1)
                for k in range(2):
                    act.wait_ge(cT_ps, k + 1)
                    dst = o_fm[:, 512 * k:512 * k + 512].rearrange("p (i t b q) -> p i t b q", i=2, t=2, b=2)
                    src = ps[:, k, :].rearrange("p (i b t q) -> p i t b q", i=2, b=2, t=2)
                    for i in range(2):
                        ins = AC.activation(dst[:, i], src[:, i], ACT.Copy)
                    ins.then_inc(cT_ok, 1)

            @block.vector
            def _(dve):
                def hat(u):
                    for c in range(10):
                        dve.wait_ge(abs_ok, 10 * u + c + 1)
                        v = hats[:, u % 2, 2 * c:2 * c + 2, :].rearrange("p r c -> p (r c)")
                        V.tensor_scalar(v, v, 1.0, -1.0, ALU.min, ALU.add).then_inc(hat_ok, 1)

                def softmax(hg):
                    v = sc[:, hg % 2].rearrange("p (a k) b -> p a b k", k=NK)
                    ab = lambda t: t.rearrange("p (a b) -> p a b", b=2)
                    dve_link(V.tensor_reduce(ab(mx), v, AX.X, ALU.max))
                    V.tensor_tensor(v, v, over(ab(mx), 3, NK), ALU.subtract).then_inc(sc_ok, 1)

                def context(hg):
                    v = sc[:, hg % 2].rearrange("p (a k) b -> p a b k", k=NK)
                    ab = lambda t: t.rearrange("p (a b) -> p a b", b=2)
                    dve.wait_ge(e_ok, hg + 1)
                    dve_link(V.tensor_reduce(ab(rs), v, AX.X, ALU.add))
                    dve_link(V.reciprocal(rs, rs))
                    dve_link(V.tensor_scalar(rs, rs, -0.5, None, ALU.mult))
                    dve_link(V.tensor_tensor(v, v, over(ab(rs), 3, NK), ALU.mult))
                    dve.wait_ge(v_ok, 4 * hg + 4)
                    values = sv[:, hg % 2].rearrange("p r (b d) -> p (r b) d", b=2)
                    dve_link(V.tensor_tensor(values, values, over(sc[:, hg % 2].rearrange("p r b -> p (r b)"), 2, HD), ALU.mult))
                    for b in range(2):
                        src = sv[:, hg % 2].rearrange("p (a k) (b d) -> p a b d k", k=NK, b=2)[:, :, b]
                        dst = cx[:, :, b, 32 * hg:32 * hg + 32].rearrange("p i (h d) -> p i h d", h=4)
                        ins = V.tensor_reduce(dst, src, AX.X, ALU.add)
                    ins.then_inc(c_ok, 1)

                hat(0)
                for u, (hg, half) in enumerate(units):
                    if u + 1 < len(units):
                        hat(u + 1)
                    if half == 0 and hg >= 1:
                        context(hg - 1)
                    for i in range(2):
                        w = 2 * u + i
                        jp = 2 * half + i
                        dve.wait_ge(smp_ps, w + 1)
                        if half == 0 and i == 0:
                            dve.wait_ge(qx_ok, hg + 1)
                        src = ps[:, 4 + 2 * (w % 2):6 + 2 * (w % 2), 0:320].rearrange("p k (r c) -> p k r c", c=32)[:, :, :, 0:16]
                        pr = prod[:, i]
                        V.tensor_tensor(pr.rearrange("p (k r) c -> p k r c", k=2), src,
                                        qx[:, hg % 2, 20 * jp:20 * jp + 20].rearrange("p (k r) c -> p k r c", k=2),
                                        ALU.mult).then_inc(prod_ok, 1)
                        dve.wait_ge(prod_ok, w + 1)
                        dve_link(V.tensor_reduce(sc[:, hg % 2, 20 * jp:20 * jp + 20, :],
                                                 pr.rearrange("p r (b d) -> p r b d", b=2), AX.X, ALU.add))
                    if half == 1:
                        softmax(hg)
                context(3)
                for k in range(2):
                    dve.wait_ge(y_ps, k + 1)
                    dve_link(V.tensor_tensor(x_tm[:, 4 * k:4 * k + 4], x_tm[:, 4 * k:4 * k + 4],
                                             ps[:, 2 + k, :].rearrange("p (j d) -> p j d", j=4), ALU.add))
                V.sem_inc(x_done, 1)

        if LAST >= 5:
            @block.sync
            def _(sp):
                for b in range(2):
                    sp.dma_start(mask_sb[S * b:S * b + S],
                                 A["mask"].rearrange("(j b) s -> b j s", b=2)[b].partition_broadcast(S)).then_inc(mask_in, 16)
                sp.wait_ge(x_done, 4)
                sp.dma_start(arena[:, 0:26 * P], A["picks"]).then_inc(picks_in, 16)

            @block.scalar
            def _(act):
                act.wait_ge(picks_in, 16)
                AC.activation(picks_b[:].rearrange("p a b -> p (a b)"), arena[:, 0:26 * P], ACT.Copy).then_inc(picks_ok, 1)

            @block.tensor
            def _(pe):
                pe.wait_ge(picks_ok, 1)

            deformable(4)

        moe2_in = sem("moe2_in")
        m2w1 = weights[:, 0:4096].rearrange("p (e f) -> p e f", e=NE)
        m2w2 = weights[:, 4096:8192].rearrange("p (e k d) -> p e k d", e=NE, k=4)
        idx = sb("idx", [P, 4, TOPK], I32)
        gw = sb("gw", [P, 4, TOPK])

        def moe2(n):
            s = lambda name: sem(f"moe2_{name}")
            up_ps, g_ok, y_ps, y_added, gates_ok = s("up_ps"), s("gelu"), s("y"), s("y_added"), s("gates")
            hid = arena[:, 0:4096].rearrange("p (i k t) -> p i k t", i=2, k=4)
            idf = arena[:, 4096:4104].rearrange("p (j k) -> p j k", j=4)
            g2 = arena[:, 4128:4192].rearrange("p (j k e) -> p j k e", j=4, k=2)
            gates = arena[:, 4192:4224].rearrange("p (j e) -> p j e", j=4)

            layernorm()

            @block.vector
            def _(dve):
                dve.wait_ge(moe2_in, 64)
                dve_link(V.tensor_copy(idf, idx[:]))
                for k in range(TOPK):
                    eq = over(idf[:, :, k], 2, NE)
                    ins = V.tensor_tensor(g2[:, :, k, :], eq, over(const[:, C_IOTA:C_IOTA + NE], 1, 4), ALU.is_equal)
                dve_link(ins)
                for k in range(TOPK):
                    ins = V.tensor_tensor(g2[:, :, k, :], g2[:, :, k, :], over(gw[:, :, k], 2, NE), ALU.mult)
                dve_link(ins)
                dve_link(V.tensor_tensor(gates, g2[:, :, 0, :], g2[:, :, 1, :], ALU.add))
                dve_link(V.tensor_tensor(x_tm[:], x_tm[:], over(row("L2_ffn_bias"), 1, NT), ALU.add))

                for e in range(NE):
                    dve.wait_ge(y_ps, e + 1)
                    if e >= 1:
                        dve.wait_ge(y_added, e)
                    for j in range(4):
                        ins = V.scalar_tensor_tensor(out=x_tm[:, j], in0=ps[:, 4 + e % 2, P * j:P * j + P],
                                                     scalar=gates[:, j, e:e + 1], in1=x_tm[:, j],
                                                     op0=ALU.mult, op1=ALU.add)
                    ins.then_inc(y_added, 1)
                dve.wait_ge(y_added, NE)
                V.sem_inc(x_done, 1)

            @block.tensor
            def _(pe):
                wait_h_fm(pe)
                pe.wait_ge(moe2_in, 64)

                def up(e):
                    for k in range(4):
                        if e >= 1:
                            pe.wait_ge(g_ok, 4 * (e - 1) + k + 1)
                        PE.matmul(ps[:, k, :], m2w1[:, e, P * k:P * k + P], h_fm[:, 0:T2], start=True, stop=True)\
                            .then_inc(up_ps, 1)

                def down(e):
                    pe.wait_ge(g_ok, 4 * e + 4)
                    if e >= 2:
                        pe.wait_ge(y_added, e - 1)
                    for j in range(4):
                        for k in range(4):
                            ins = PE.matmul(ps[:, 4 + e % 2, P * j:P * j + P], hid[:, e % 2, k, P * j:P * j + P],
                                            m2w2[:, e, k, :], start=(k == 0), stop=(k == 3))
                    ins.then_inc(y_ps, 1)

                up(0)
                for e in range(NE):
                    if e + 1 < NE:
                        up(e + 1)
                    down(e)

            @block.scalar
            def _(act):
                for e in range(NE):
                    if e >= 2:
                        act.wait_ge(y_ps, e - 1)
                    for k in range(4):
                        act.wait_ge(up_ps, 4 * e + k + 1)
                        AC.activation(hid[:, e % 2, k, :], ps[:, k, :], ACT.Gelu).then_inc(g_ok, 1)

        if LAST >= 6:
            @block.sync
            def _(sp):
                sp.wait_ge(x_done, 2)
                sp.dma_start(m2w1, A["moe2_w1"]).then_inc(moe2_in, 16)
                sp.dma_start(m2w2, A["moe2_w2"]).then_inc(moe2_in, 16)
                sp.dma_start(idx[:], A["moe2_idx"]).then_inc(moe2_in, 16)
                sp.dma_start(gw[:], A["moe2_gw"]).then_inc(moe2_in, 16)
            moe2(5)

        if LAST >= 7:
            @block.gpsimd
            def _(pool):
                pool.wait_ge(x_done, 5)
                G.memset(v4[:], 0.0).then_inc(v4_zero, 1)

            attention(6, "L3_xattn_W_q", "L3_xattn_W_k", "L3_xattn_W_v", "L3_xattn_W_o", "L3_xattn_b_q",
                      "L3_xattn_b_k", "L3_xattn_b_v", "L3_xattn_b_o", True)

        ffn3_in = sem("ffn3_in")
        wn = weights[:, 0:9 * P].rearrange("p (c k) -> p c k", c=9)
        wT = weights[:, 9 * P:18 * P].rearrange("p (c k) -> p c k", c=9)

        def ffn3(n):
            s = lambda name: sem(f"ffn3_{name}")
            wq_ok, wT_ps, wT_ok = s("wq"), s("wT_ps"), s("wT")
            col_ok, row_ps, top_ok, all_ps = s("max_cols"), s("max_row"), s("max_top"), s("max_all")
            x_ok, mm_ps, mm_sb, sig_in, sig_ok, o_ok, y_ps = (
                s("x"), s("up_ps"), s("up_sb"), s("gate"), s("sigmoid"), s("o"), s("y"))
            up = arena[:, 0:3072]
            gate = arena[:, 3072:6144]
            sig = arena[:, 6144:9216]
            wam = arena[:, 9216:9252]
            wsc = arena[:, 9252:9288]
            winv = arena[:, 9288:9324]
            cm = arena[:, 9324:9340]
            m1 = arena[:, 9340:9341]
            top = arena[0:1, 9341:9342]
            amax = arena[:, 9342:9343]
            scl = arena[:, 9344:9350]
            inv = arena[:, 9350:9356]
            ones = arena[0:1, 9360:9488]
            blocks = wn.rearrange("p c (g i) -> p (c g) i", i=32)
            n_max = [0]

            @block.vector
            def _(dve):
                dve.wait_ge(ffn3_in, 48)
                V.memset(ones, 1.0)
                dve_link(V.tensor_reduce(wam, blocks, AX.X, ALU.max, apply_absolute_value=True))
                dve_link(V.tensor_scalar(wsc, wam, 1.0 / 7.0, 1e-12, ALU.mult, ALU.max))
                dve_link(V.reciprocal(winv, wsc))
                dve_link(V.tensor_tensor(blocks, blocks, over(winv, 2, 32), ALU.mult))
                dve_link(V.tensor_scalar(blocks, blocks, MAGIC, -MAGIC, ALU.add, ALU.add))
                dve_link(V.tensor_scalar(blocks, blocks, -8.0, 7.0, ALU.max, ALU.min))
                V.tensor_tensor(blocks, blocks, over(wsc, 2, 32), ALU.mult).then_inc(wq_ok, 1)

            @block.tensor
            def _(pe):
                pe.wait_ge(x_done, n)
                pe.wait_ge(wq_ok, 1)
                for k, c0, c1 in ((0, 0, 4), (1, 4, 8), (2, 8, 9)):
                    for c in range(c0, c1):
                        ins = PE.transpose(ps[:, k, P * (c - c0):P * (c - c0) + P], wn[:, c, :], ident)
                    ins.then_inc(wT_ps, 1)

            @block.scalar
            def _(act):
                for k, c0, c1 in ((0, 0, 4), (1, 4, 8), (2, 8, 9)):
                    act.wait_ge(wT_ps, k + 1)
                    AC.activation(wT[:, c0:c1, :].rearrange("p c k -> p (c k)"), ps[:, k, 0:P * (c1 - c0)], ACT.Copy)\
                        .then_inc(wT_ok, 1)

            layernorm()

            def all_max(i):
                m = n_max[0]
                n_max[0] += 1

                @block.tensor
                def _(pe):
                    pe.wait_ge(col_ok, m + 1)
                    PE.transpose(ps[0:1, 6, 0:P], m1, ident).then_inc(row_ps, 1)
                    pe.wait_ge(top_ok, m + 1)
                    PE.matmul(ps[:, 7, 0:1], ones, top, start=True, stop=True).then_inc(all_ps, 1)

                @block.vector
                def _(dve):
                    dve.wait_ge(row_ps, m + 1)
                    V.tensor_reduce(top, ps[0:1, 6, 0:P], AX.X, ALU.max).then_inc(top_ok, 1)
                    dve.wait_ge(all_ps, m + 1)
                    dve_link(V.tensor_scalar(scl[:, i:i + 1], ps[:, 7, 0:1], 1.0 / 32767.0, 1e-12, ALU.mult, ALU.max))
                    dve_link(V.reciprocal(inv[:, i:i + 1], scl[:, i:i + 1]))

            def quantise(v, i):
                dve_link(V.tensor_scalar(v, v, inv[:, i:i + 1], MAGIC, ALU.mult, ALU.add))
                dve_link(V.tensor_scalar(v, v, -MAGIC, 32767.0, ALU.add, ALU.min))
                return V.tensor_scalar(v, v, -32768.0, scl[:, i:i + 1], ALU.max, ALU.mult)

            @block.vector
            def _(dve):
                dve.wait_ge(h_ready, n_sub[0])
                V.tensor_reduce(m1, h_tm[:].rearrange("p j d -> p (j d)"), AX.X, ALU.max, apply_absolute_value=True)\
                    .then_inc(col_ok, 1)

            all_max(0)

            @block.vector
            def _(dve):
                wait_h_fm(dve)
                quantise(h_fm[:], 0).then_inc(x_ok, 1)

            @block.tensor
            def _(pe):
                pe.wait_ge(x_ok, 1)
                pe.wait_ge(wT_ok, 3)
                for i, c0 in ((0, 3), (1, 0)):
                    for c in range(3):
                        for k in range(2):
                            m = 6 * i + 2 * c + k
                            if m >= 4:
                                pe.wait_ge(mm_sb, m - 3)
                            PE.matmul(ps[:, m % 4, :], wT[:, c0 + c, :], h_fm[:, 512 * k:512 * k + 512],
                                      start=True, stop=True).then_inc(mm_ps, 1)

            @block.scalar
            def _(act):
                for m in range(12):
                    act.wait_ge(mm_ps, m + 1)
                    at = 512 * (m % 6)
                    dst = (up if m < 6 else gate)[:, at:at + 512]
                    AC.activation(dst, ps[:, m % 4, :], ACT.Copy).then_inc(mm_sb, 1)

            for i, v in enumerate((up, gate)):
                @block.vector
                def _(dve):
                    for c in range(6):
                        dve.wait_ge(mm_sb, 6 * i + c + 1)
                        ins = V.tensor_reduce(cm[:, c:c + 1], v[:, 512 * c:512 * c + 512], AX.X, ALU.max,
                                              apply_absolute_value=True)
                    dve_link(ins)
                    V.tensor_reduce(m1, cm[:, 0:6], AX.X, ALU.max).then_inc(col_ok, 1)

                all_max(1 + i)

                @block.vector
                def _(dve):
                    for c in range(3):
                        ins = quantise(v[:, 1024 * c:1024 * c + 1024], 1 + i)
                        if i == 1:
                            ins.then_inc(sig_in, 1)
                        else:
                            dve_link(ins)

            @block.scalar
            def _(act):
                for c in range(3):
                    act.wait_ge(sig_in, c + 1)
                    AC.activation(sig[:, 1024 * c:1024 * c + 1024], gate[:, 1024 * c:1024 * c + 1024], ACT.Sigmoid)\
                        .then_inc(sig_ok, 1)

            @block.vector
            def _(dve):
                for c in range(3):
                    dve.wait_ge(sig_ok, c + 1)
                    v, g = sig[:, 1024 * c:1024 * c + 1024], gate[:, 1024 * c:1024 * c + 1024]
                    dve_link(V.tensor_scalar(v, v, 65536.0, MAGIC, ALU.mult, ALU.add))
                    dve_link(V.tensor_scalar(v, v, -MAGIC, 65535.0, ALU.add, ALU.min))
                    dve_link(V.tensor_scalar(v, v, 0.0, 1.0 / 65536.0, ALU.max, ALU.mult))
                    dve_link(V.tensor_tensor(g, g, v, ALU.mult))
                V.tensor_reduce(m1, gate, AX.X, ALU.max, apply_absolute_value=True).then_inc(col_ok, 1)

            all_max(3)

            @block.vector
            def _(dve):
                for c in range(3):
                    g, u = gate[:, 1024 * c:1024 * c + 1024], up[:, 1024 * c:1024 * c + 1024]
                    dve_link(quantise(g, 3))
                    dve_link(V.tensor_tensor(u, g, u, ALU.mult))
                V.tensor_reduce(m1, up, AX.X, ALU.max, apply_absolute_value=True).then_inc(col_ok, 1)

            all_max(4)

            @block.vector
            def _(dve):
                for c in range(3):
                    quantise(up[:, 1024 * c:1024 * c + 1024], 4).then_inc(o_ok, 1)
                for k in range(2):
                    dve.wait_ge(y_ps, k + 1)
                    dve_link(V.tensor_tensor(x_tm[:, 4 * k:4 * k + 4], x_tm[:, 4 * k:4 * k + 4],
                                             ps[:, k, :].rearrange("p (j d) -> p j d", j=4), ALU.add))
                V.sem_inc(x_done, 1)

            @block.tensor
            def _(pe):
                pe.wait_ge(o_ok, 3)
                for k in range(2):
                    for j in range(4 * k, 4 * k + 4):
                        for c in range(3):
                            ins = PE.matmul(ps[:, k, P * (j % 4):P * (j % 4) + P],
                                            up[:, 1024 * c + P * j:1024 * c + P * j + P], wT[:, 6 + c, :],
                                            start=(c == 0), stop=(c == 2))
                    ins.then_inc(y_ps, 1)

        if LAST >= 8:
            @block.sync
            def _(sp):
                sp.wait_ge(x_done, 6)
                for i, name in enumerate(("w_gate", "w_up")):
                    sp.dma_start(wn[:, 3 * i:3 * i + 3, :], A[name].rearrange("(c p) i -> p c i", p=P)).then_inc(ffn3_in, 16)
                sp.dma_start(wn[:, 6:9, :], A["w_down"].rearrange("p (c i) -> p c i", c=3)).then_inc(ffn3_in, 16)
            ffn3(7)


        out_done = sem("out_done")

        @block.sync
        def _(sp):
            sp.wait_ge(x_done, LAST)
            if LAST < 8:
                for sm_, n_ in ((ctxt_in, 16),):
                    sp.wait_ge(sm_, n_)
            sp.dma_start(out.rearrange("(j p) d -> p j d", p=P), x_tm[:]).then_inc(out_done, 16)
            sp.wait_ge(out_done, 16)


def kernel(**inputs):
    import concourse.bacc as _bacc
    from concourse.bass_utils import run_bass_kernel_spmd as _run

    a = {k: np.asarray(v) for k, v in inputs.items()}

    def T_(m):
        return np.ascontiguousarray(m.T)

    def split(w, k):
        e, f, n = w.shape
        w = w.reshape(e, k, f // k, n).transpose(2, 0, 1, 3)
        return np.ascontiguousarray(w.reshape(f // k, e, n) if k == 1 else w)

    experts = {i: np.concatenate([a[f"L0_ffn_rw{i}"], a[f"L0_ffn_sw{i}"]]) for i in (1, 2, 3)}
    biases = {i: np.concatenate([a[f"L0_ffn_rb{i}"], a[f"L0_ffn_sb{i}"]]) for i in (1, 2, 3)}
    woff = np.zeros((P, 2, S), np.float32)
    boff = np.zeros((2, S, 2), np.float32)
    for g in range(2):
        woff[:, g, :40] = a["L2_xattn_Woff"][40 * g:40 * g + 40].T
        boff[:, :40, g] = a["L2_xattn_boff"][40 * g:40 * g + 40]
    cols = np.concatenate(
        [np.stack([a[n] for n in COLS], 1)]
        + [biases[i].reshape(NQ, 2, P).transpose(2, 0, 1).reshape(P, 2 * NQ) for i in (1, 2)]
        + [boff.reshape(P, 2)], 1)
    send = {
        "x": a["x"].reshape(T, D),
        "ctx": a["ctx_1024"].reshape(T, D),
        "ctx_fm": T_(a["ctx_1024"].reshape(T, D)),
        "const": shape_constants(), "picks": row_picks(),
        "rows": np.stack([a[n] for n in ROWS]),
        "cols": cols,
        "mats": np.ascontiguousarray(np.stack([a[n].T for n in MATS], 1)),
        "woff": woff,
        "moe0_w1": split(experts[1], 1), "moe0_w2": split(experts[2], 1), "moe0_w3": split(experts[3], 2),
        "moe0_b3": biases[3],
        "gate_w": a["L0_ffn_gate_w"], "gate_b": a["L0_ffn_gate_b"],
        "mask": a["mask_BxS2_if0"],
        "attn_bias": a["fside_1x16xSxS2_0"][0],
        "attn_mask": a["mask_Bx1xSxS2_ik1"].reshape(T, S),
        "wq8": T_(a["L1_ffn_weight_q"]).astype(np.int32),
        "moe2_w1": split(a["L2_ffn_w1"], 1), "moe2_w2": split(a["L2_ffn_w2"], 4),
        "moe2_idx": np.ascontiguousarray(a["L2_ffn_expert_indices"].reshape(4, P, 2).transpose(1, 0, 2)),
        "moe2_gw": np.ascontiguousarray(a["L2_ffn_expert_weights"].reshape(4, P, 2).transpose(1, 0, 2)),
        "w_gate": a["L3_ffn_w_gate"], "w_up": a["L3_ffn_w_up"], "w_down": a["L3_ffn_w_down"],
    }
    nc = _bacc.Bacc("TRN2", target_bir_lowering=False, num_devices=1)
    arrays, A = {}, {}
    for name, v in send.items():
        v = np.ascontiguousarray(v)
        arrays[f"in_{name}"] = v
        A[name] = nc.dram_tensor(f"in_{name}", v.shape, mybir.dt.from_np(v.dtype), kind="ExternalInput").ap()
    out = nc.dram_tensor("out_x", (T, D), F32, kind="ExternalOutput").ap()
    build(nc, A, out)
    r = _run(nc, [arrays], core_ids=[0])
    return r.results[0]["out_x"].reshape(B, S, D)
```

```python
from contextlib import ExitStack

import numpy as np

import concourse.bass as bass
from concourse import mybir

P = 128
B, S, D = 16, 64, 128
T = B * S
NT = T // P
H, HD = 16, 8
NK = 5
NE, NSH, TOPK, FH = 8, 2, 2, 256
FF2, T2 = 512, 512
I3 = 384
LAST = 8
EPS = 1e-5
MAGIC = 12582912.0
F32 = mybir.dt.float32
BF16 = mybir.dt.bfloat16
I32 = mybir.dt.int32
I8 = mybir.dt.int8
ALU = mybir.AluOpType
ACT = mybir.ActivationFunctionType
AX = mybir.AxisListType

ROWS = ["L0_xattn_bv", "L0_xattn_bo", "L1_xattn_wqg", "L1_xattn_wql", "L1_xattn_bqg", "L1_xattn_bql",
        "L1_xattn_wkg", "L1_xattn_wkl", "L1_xattn_bkg", "L1_xattn_bkl", "L1_xattn_wp", "L1_xattn_bp",
        "L1_ffn_weight_scale", "L1_ffn_bias", "L2_xattn_bk", "L2_xattn_bv", "L2_xattn_bo",
        "L2_xattn_bq", "L2_ffn_bias", "L3_xattn_b_v", "L3_xattn_b_o"]
COLS = ["L0_xattn_bq", "L0_xattn_bk", "L1_xattn_wvg", "L1_xattn_bvg", "L1_xattn_wvl", "L1_xattn_bvl",
        "L2_xattn_bq", "L3_xattn_b_q", "L3_xattn_b_k"]
NC_EXP = len(COLS)
MATS = ["L0_xattn_Wq", "L0_xattn_Wk", "L0_xattn_Wv", "L0_xattn_Wo",
        "L2_xattn_Wk", "L2_xattn_Wv", "L2_xattn_Wq", "L2_xattn_Wo",
        "L3_xattn_W_q", "L3_xattn_W_k", "L3_xattn_W_v", "L3_xattn_W_o"]
NQ = NE + NSH

C_ID = 0
C_HM = C_ID + P
C_NEGM = C_HM + 4
C_REF = C_NEGM + 1
C_IOTA = C_REF + S
C_ONES = C_IOTA + NE
C_END = C_ONES + 64


def shape_constants():
    c = np.zeros((P, C_END), np.float32)
    p = np.arange(P)
    c[p, C_ID + p] = 1.0
    for h in range(4):
        c[:, C_HM + h] = (p // HD) % 4 == h
    c[:, C_NEGM] = -(p % S)
    c[:, C_REF:C_REF + S] = ((p % S) % NK - 3)[:, None] + np.arange(S)[None, :]
    c[:, C_IOTA:C_IOTA + NE] = np.arange(NE)
    ones = c[:, C_ONES:C_ONES + 64].reshape(P, 2, 4, HD)
    for par in range(2):
        for h2 in range(2):
            ones[S * h2:S * h2 + S, par, 2 * par + h2] = 1.0
    c[:, C_ONES:C_ONES + 64] = ones.reshape(P, 64)
    return c


def row_picks():
    c = np.zeros((P, 26, P), np.float32)
    for b in range(2):
        for r in range(20):
            for part in range(3):
                c[S * b + 20 * part + r, r, S * b:S * b + S] = 1.0
                for g in range(2):
                    c[S * b + 20 * g + r, 20 + 3 * g + part, S * b + 20 * part + r] = 1.0
    return c.reshape(P, 26 * P)


def over(ap, axis, n):
    wide = ap.unsqueeze(axis)
    shape = list(wide.shape)
    shape[axis] = n
    return wide.broadcast_to(shape)


def build(nc, A, out):
    ctx = ExitStack()
    with ctx:
        def sb(name, shape, dt=F32):
            return ctx.enter_context(nc.sbuf_tensor(name, shape, dt))

        def sem(name):
            return ctx.enter_context(nc.semaphore(name))

        V, G, PE, AC = nc.vector, nc.gpsimd, nc.tensor, nc.scalar

        const = sb("const", [P, C_END])
        rows = sb("rows", [P, len(ROWS), D])
        cols = sb("cols", [P, NC_EXP + 4 * NQ + 2])
        mats = sb("mats", [P, len(MATS), D])
        woff = sb("woff", [P, 2, S])
        x_tm = sb("x_tm", [P, NT, D])
        h_tm = sb("h_tm", [P, NT, D])
        h_fm = sb("h_fm", [P, T])
        ctx_fm = sb("ctx_fm", [P, T])
        ctx_tm = sb("ctx_tm", [P, NT, D])
        stats = sb("stats", [P, NT, 6])
        mv = sb("mv", [P, NT, 2])
        rstd = sb("rstd", [P, NT])
        kexp = sb("kexp", [P, B * 4 * S])
        v4 = sb("v4", [P, B * 8 * 32])
        arena = sb("arena", [P, 10240])
        weights = sb("weights", [P, 8192])

        ps = ctx.enter_context(nc.psum_tensor("ps", [P, 8, 512], F32))

        def row(name):
            return rows[:, ROWS.index(name), :]

        def col(name):
            i = COLS.index(name)
            return cols[:, i:i + 1]

        def mat(name):
            return mats[:, MATS.index(name), :]

        ident = const[:, C_ID:C_ID + P]

        dve_chain, pool_chain = sem("dve_chain"), sem("pool_chain")
        chained = {"dve": 0, "pool": 0}

        def dve_link(ins):
            chained["dve"] += 1
            ins.then_inc(dve_chain, 1)
            V.wait_ge(dve_chain, chained["dve"])

        def dve_mark(ins):
            chained["dve"] += 1
            ins.then_inc(dve_chain, 1)
            return chained["dve"]

        def pool_link(ins):
            chained["pool"] += 1
            ins.then_inc(pool_chain, 1)
            G.wait_ge(pool_chain, chained["pool"])

        x_in, const_in, ctxf_in, ctxt_in = sem("x_in"), sem("const_in"), sem("ctxf_in"), sem("ctxt_in")
        rows_in, cols_in, mats_in = sem("rows_in"), sem("cols_in"), sem("mats_in")
        moe0_in = sem("moe0_in")
        x_done = sem("x_done")
        hf_ready = sem("hf_ready")
        b3 = sb("b3", [NQ, D])
        gate_w = sb("gate_w", [P, NE])
        gate_b = sb("gate_b", [P, NE])
        w1 = weights[:, 0:NQ * FH].rearrange("p (e h) -> p e h", e=NQ)
        w2 = weights[:, NQ * FH:2 * NQ * FH].rearrange("p (e h) -> p e h", e=NQ)
        w3 = weights[:, 2 * NQ * FH:3 * NQ * FH].rearrange("p (e k d) -> p e k d", e=NQ, k=2)

        block = ctx.enter_context(nc.Block())

        first_mats = 4
        mats0_in = sem("mats0_in")

        @block.sync
        def _(sp):
            sp.dma_start(mats[:, 0:first_mats], A["mats"][:, 0:first_mats]).then_inc(mats0_in, 16)
            sp.dma_start(x_tm[:], A["x"].rearrange("(j p) d -> p j d", p=P)).then_inc(x_in, 16)
            sp.dma_start(const[:], A["const"]).then_inc(const_in, 16)
            sp.dma_start(w1, A["moe0_w1"]).then_inc(moe0_in, 16)
            sp.dma_start(w2, A["moe0_w2"]).then_inc(moe0_in, 16)
            sp.dma_start(w3, A["moe0_w3"]).then_inc(moe0_in, 16)
            sp.dma_start(b3[:], A["moe0_b3"]).then_inc(moe0_in, 16)
            sp.dma_start(gate_w[:], A["gate_w"]).then_inc(moe0_in, 16)
            sp.dma_start(gate_b[:], A["gate_b"].partition_broadcast(P)).then_inc(moe0_in, 16)
            sp.dma_start(mats[:, first_mats:], A["mats"][:, first_mats:]).then_inc(mats_in, 16)
            sp.dma_start(woff[:], A["woff"]).then_inc(mats_in, 16)

        @block.scalar
        def _(act):
            act.dma_start(ctx_fm[:], A["ctx_fm"]).then_inc(ctxf_in, 16)
            act.dma_start(cols[:], A["cols"]).then_inc(cols_in, 16)
            act.dma_start(rows[:], A["rows"].partition_broadcast(P)).then_inc(rows_in, 16)
            act.dma_start(ctx_tm[:], A["ctx"].rearrange("(j p) d -> p j d", p=P)).then_inc(ctxt_in, 16)

        cleared = sem("cleared")
        V4_CLEAR, KV_CLEAR, AB_CLEAR, V4_CLEAR_AGAIN = 1, 2, 3, 4

        @block.gpsimd
        def _(pool):
            G.memset(v4[:], 0.0).then_inc(cleared, 1)

        n_sub, n_fm = [0], [0]
        stat_ready, std_ready, tr_ready = sem("var"), sem("std"), sem("hT")
        shift_ready, h_first, h_rest = sem("shift"), sem("h_first"), sem("h_rest")
        shift = sb("shift", [P, NT])
        ON_DVE = 5

        def tile_stats(j):
            return V.bn_stats(stats[:, j, :], x_tm[:, j, :])

        def layernorm(feature_major=True):
            n = n_sub[0]
            n_sub[0] += 1
            nf = n_fm[0]

            @block.vector
            def _(dve):
                if n == 0:
                    dve.wait_ge(x_in, 16)
                    for j in range(NT):
                        ins = tile_stats(j)
                    dve_link(ins)
                for j in range(NT):
                    ins = V.bn_aggr(mv[:, j, :], stats[:, j, :])
                dve_link(ins)
                V.tensor_scalar(rstd[:], mv[:, :, 1], EPS, None, ALU.add).then_inc(stat_ready, 1)
                dve.wait_ge(std_ready, n + 1)
                dve_link(V.reciprocal(rstd[:], rstd[:]))
                V.scalar_tensor_tensor(out=shift[:], in0=mv[:, :, 0], scalar=-1.0, in1=rstd[:],
                                       op0=ALU.mult, op1=ALU.mult).then_inc(shift_ready, 1)
                for j in range(ON_DVE):
                    ins = V.tensor_scalar(h_tm[:, j, :], x_tm[:, j, :], mv[:, j, 0:1], rstd[:, j:j + 1],
                                          ALU.subtract, ALU.mult)
                    if j == 3:
                        ins.then_inc(h_first, 1)
                ins.then_inc(h_rest, 1)

            @block.scalar
            def _(act):
                act.wait_ge(stat_ready, n + 1)
                AC.activation(rstd[:], rstd[:], ACT.Sqrt).then_inc(std_ready, 1)
                act.wait_ge(shift_ready, n + 1)
                for j in range(ON_DVE, NT):
                    ins = AC.activation(h_tm[:, j, :], x_tm[:, j, :], ACT.Identity, bias=shift[:, j:j + 1],
                                        scale=rstd[:, j:j + 1])
                ins.then_inc(h_rest, 1)
                if feature_major:
                    for k in range(2):
                        act.wait_ge(tr_ready, 2 * nf + k + 1)
                        AC.activation(h_fm[:, 512 * k:512 * k + 512], ps[:, 4 + k, :], ACT.Copy)\
                            .then_inc(hf_ready, 1)

            if feature_major:
                @block.tensor
                def _(pe):
                    if n == 0:
                        pe.wait_ge(const_in, 16)
                    for k in range(2):
                        if k == 0:
                            pe.wait_ge(h_first, n + 1)
                        else:
                            pe.wait_ge(h_rest, 2 * n + 2)
                        for j in range(4):
                            ins = PE.transpose(ps[:, 4 + k, 128 * j:128 * j + 128], h_tm[:, 4 * k + j, :], ident)
                        ins.then_inc(tr_ready, 1)
                n_fm[0] += 1

        def all_stats(tiles=range(NT)):
            for j in tiles:
                ins = tile_stats(j)
            dve_link(ins)

        def wait_h_tm(eng):
            eng.wait_ge(h_first, n_sub[0])
            eng.wait_ge(h_rest, 2 * n_sub[0])

        def wait_h_fm(eng):
            eng.wait_ge(hf_ready, 2 * n_fm[0])

        k_fm = sb("k_fm", [P, T])
        q_fm = sb("q_fm", [P, T])
        o_fm = sb("o_fm", [P, T])

        SCALE = 1.0 / float(np.sqrt(np.float32(HD)))
        kx = kexp[:].rearrange("p (b h k) -> p b h k", b=B, h=4)
        vx = v4[:].rearrange("p (b c m) -> p b c m", b=B, c=8)
        l2buf = sb("l2buf", [P, 8192])
        bqs = sb("bqs", [P, 2])
        bias = arena[:, 8192:9216]
        masks = arena[:, 9216:9728].bitcast(I32).rearrange("p (j k) -> p j k", j=NT)
        seen = arena[:, 9728:10240].rearrange("p (j k) -> p j k", j=NT)
        seen_bias = l2buf[:].rearrange("p (j h k) -> p j h k", j=NT, h=H)

        def keys_values(n, layer, wk, wv, bq, bk, bv, masked, work, banks, ready, before_dve=None):
            s = lambda name: sem(f"{layer}_{name}")
            k_ps, k_sb, kx_ready = s("k_ps"), s("k_sb"), s("kx")
            v_ps, v_sb, vx_ready, bq_ok = s("v_ps"), s("v_sb"), s("vx"), s("bq")
            vdup = work[:, 0:2048].rearrange("p (i b e) -> p i b e", i=4, b=4)
            nb = len(banks)

            def guard(t, width, scratch):
                tmp, tmp2, nonf = scratch[:, 0:1024], scratch[:, 1024:2048], scratch[:, 2048:3072].bitcast(I32)
                for at in range(0, width, 1024):
                    v = t[:, at:at + 1024]
                    V.tensor_scalar(nonf, v, 0.0, 0.0, ALU.mult, ALU.not_equal)
                    V.tensor_scalar(tmp, v, 0.0, 1e4, ALU.max, ALU.min)
                    dve_link(V.tensor_scalar(tmp2, v, 0.0, -1e4, ALU.min, ALU.max))
                    dve_link(V.tensor_tensor(tmp, tmp, tmp2, ALU.add))
                    dve_link(V.copy_predicated(v, nonf, tmp))

            def expand_keys(dve):
                dve.wait_ge(k_sb, 2)
                for k in range(2):
                    src = over(k_fm[:, 512 * k:512 * k + 512].rearrange("p (b k) -> p b k", b=8), 2, 4)
                    hm = over(over(const[:, C_HM:C_HM + 4], 2, S), 1, 8)
                    ins = V.tensor_tensor(kx[:, 8 * k:8 * k + 8], src, hm, ALU.mult)
                ins.then_inc(kx_ready, 1)

            def evacuate(dve, g):
                dve.wait_ge(rows_in, 16)
                dve.wait_ge(v_ps, g + 1)
                V.tensor_tensor(vdup[:, g], ps[:, banks[g % nb], :].rearrange("p (b e) -> p b e", b=4),
                                over(row(bv), 1, 4), ALU.add).then_inc(v_sb, 1)

            def guard_values(dve, half):
                dve.wait_ge(v_sb, 4)
                guard(vdup[:, 2 * half:2 * half + 2].rearrange("p i b e -> p (i b e)"), 1024, work[:, 2048:5120])
                if half == 1:
                    V.sem_inc(v_sb, 1)

            def guard_keys(dve):
                dve.wait_ge(k_sb, 2)
                guard(k_fm[:], T, work[:, 2048:5120])

            def spread_values(act):
                act.wait_ge(v_sb, 5 if masked else 4)
                act.wait_ge(cleared, V4_CLEAR_AGAIN if masked else V4_CLEAR)
                for h2 in range(2):
                    for par in range(2):
                        r = slice(64 * h2, 64 * h2 + 64)
                        c0 = (par * 2 + h2) * HD
                        for g in range(4):
                            src = vdup[r, g].rearrange("p b (c h d) -> p b c h d", c=4, h=4)[:, :, :, par * 2 + h2, :]
                            dst = vx[r, 4 * g:4 * g + 4].rearrange("p b (c t) m -> p b c t m", t=2)[:, :, :, par, c0:c0 + HD]
                            ins = AC.activation(dst, src, ACT.Copy)
                ins.then_inc(vx_ready, 1)

            @block.tensor
            def _(pe):
                ready(pe)
                if layer == "L0":
                    pe.wait_ge(ctxf_in, 16)
                    pe.wait_ge(mats0_in, 16)
                else:
                    pe.wait_ge(mats_in, 32)
                for k in range(2):
                    PE.matmul(ps[:, 6 + k, :], mat(wk), ctx_fm[:, 512 * k:512 * k + 512],
                              start=True, stop=True).then_inc(k_ps, 1)
                pe.wait_ge(k_sb, 2)
                for g in range(4):
                    if g >= nb:
                        pe.wait_ge(v_sb, g - nb + 1)
                    for b in range(4):
                        for h2 in range(2):
                            ins = PE.matmul(ps[64 * h2:64 * h2 + 64, banks[g % nb], 128 * b:128 * b + 128],
                                            ctx_fm[:, (4 * g + b) * S:(4 * g + b + 1) * S], mat(wv),
                                            start=True, stop=True)
                    ins.then_inc(v_ps, 1)

            @block.scalar
            def _(act):
                ready(act)
                act.wait_ge(cols_in, 16)
                for k in range(2):
                    act.wait_ge(k_ps, k + 1)
                    AC.activation(k_fm[:, 512 * k:512 * k + 512], ps[:, 6 + k, :], ACT.Identity,
                                  bias=col(bk)).then_inc(k_sb, 1)
            if before_dve is not None:
                before_dve()
            if not masked:
                block.scalar(spread_values)

            @block.vector
            def _(dve):
                ready(dve)
                dve.wait_ge(const_in, 16)
                dve.wait_ge(cols_in, 16)
                V.tensor_scalar(bqs[:, int(masked):int(masked) + 1], col(bq), 1.0 if masked else SCALE, None,
                                ALU.mult).then_inc(bq_ok, 1)
                if not masked:
                    expand_keys(dve)
                    for g in range(4):
                        evacuate(dve, g)

            if masked:
                return (kx_ready, vx_ready, bq_ok, guard), (evacuate, guard_keys, expand_keys, guard_values, spread_values, v_sb)
            return kx_ready, vx_ready, bq_ok, guard

        def attention(n, layer, wq, wo, bo, prepared, masked, bm_ready=None):
            kx_ready, vx_ready, bq_ok, guard = prepared
            s = lambda name: sem(f"{layer}_{name}")
            prob = [arena[:, 1024 * i:1024 * i + 1024] for i in range(3)]
            pT = [arena[:, 3072 + 1024 * i:4096 + 1024 * i] for i in range(2)]
            mx = arena[:, 6144:6144 + 32].rearrange("p (i h) -> p i h", i=2)
            rb = arena[:, 6208:6208 + 128]
            ones = const[:, C_ONES:C_ONES + 64].rearrange("p (t m) -> p t m", t=2)
            q_ps, q_sb = s("q_ps"), s("q_sb")
            q_ok, mx_ready, clean = (s("q_ok"), s("max"), s("clean")) if masked else (None, None, None)
            sc_ready, sc_read, sub_ready, exp_ready = s("scores"), s("scores_read"), s("less_max"), s("exp")
            ptT_ready, pt_ready = s("probsT"), s("probsT_sb")
            o_ready, rb_ready = s("o_ps"), s("sums")
            of_ready, y_ready, y_added = s("o_fm"), s("y"), s("y_added")

            @block.tensor
            def _(pe):
                wait_h_fm(pe)
                if layer == "L3":
                    pe.wait_ge(x_done, n)
                for k in range(2):
                    PE.matmul(ps[:, 6 + k, :], mat(wq), h_fm[:, 512 * k:512 * k + 512],
                              start=True, stop=True).then_inc(q_ps, 1)

            @block.scalar
            def _(act):
                act.wait_ge(bq_ok, 1)
                for k in range(2):
                    act.wait_ge(q_ps, k + 1)
                    AC.activation(q_fm[:, 512 * k:512 * k + 512], ps[:, 6 + k, :], ACT.Identity,
                                  bias=bqs[:, int(masked):int(masked) + 1], scale=1.0 if masked else SCALE)\
                        .then_inc(q_sb, 1)

            @block.vector
            def _(dve):
                if masked:
                    dve.wait_ge(q_sb, 2)
                    guard(q_fm[:], T, arena[:, 0:3072])
                    V.tensor_scalar(q_fm[:], q_fm[:], SCALE, None, ALU.mult).then_inc(q_ok, 1)
                wait_h_tm(dve)
                dve.wait_ge(rows_in, 16)
                dve_link(V.tensor_tensor(x_tm[:], x_tm[:], over(row(bo), 1, NT), ALU.add))

            @block.tensor
            def _(pe):
                pe.wait_ge(q_ok if masked else q_sb, 1 if masked else 2)
                pe.wait_ge(kx_ready, 1)

                def scores(t):
                    for g in range(4):
                        if t >= 1 and g % 2 == 0:
                            pe.wait_ge(sc_read, 2 * (t - 1) + g // 2 + 1)
                        for b in range(2):
                            ins = PE.matmul(ps[64 * b:64 * b + 64, g, 0:256],
                                            q_fm[32 * g:32 * g + 32, t * P + 64 * b:t * P + 64 * b + 64],
                                            kx[32 * g:32 * g + 32, 2 * t + b].rearrange("p h k -> p (h k)"),
                                            start=True, stop=True)
                        if g % 2 == 1:
                            ins.then_inc(sc_ready, 1)

                scores(0)
                for t in range(NT + 3):
                    if t + 1 < NT:
                        scores(t + 1)
                    if 0 <= t - 1 < NT:
                        j = t - 1
                        pe.wait_ge(clean if masked else exp_ready, j + 1)
                        for k in range(2):
                            if j >= 1:
                                pe.wait_ge(pt_ready, 2 * (j - 1) + k + 1)
                            for c in range(4):
                                ins = PE.transpose(ps[:, 4 + k, 128 * c:128 * c + 128],
                                                   prob[j % 3][:, (4 * k + c) * 128:(4 * k + c + 1) * 128], ident)
                            ins.then_inc(ptT_ready, 1)
                    if 0 <= t - 2 < NT:
                        j = t - 2
                        pe.wait_ge(pt_ready, 2 * j + 2)
                        if j == 0:
                            pe.wait_ge(vx_ready, 1)
                        else:
                            pe.wait_ge(of_ready, j)
                        for b in range(2):
                            for c in range(8):
                                g = c // 2
                                PE.matmul(ps[32 * g:32 * g + 32, 6, 64 * b:64 * b + 64], vx[:, 2 * j + b, c, :],
                                          pT[j % 2][:, 128 * c + 64 * b:128 * c + 64 * b + 64],
                                          start=(c % 2 == 0), stop=(c % 2 == 1))
                        for c in range(8):
                            ins = PE.matmul(ps[32 * (c // 2):32 * (c // 2) + 32, 6, 128:256], ones[:, c % 2, :],
                                            pT[j % 2][:, 128 * c:128 * c + 128], start=(c % 2 == 0), stop=(c % 2 == 1))
                        ins.then_inc(o_ready, 1)
                    if 0 <= t - 3 < NT:
                        j = t - 3
                        pe.wait_ge(of_ready, j + 1)
                        if j >= 1:
                            pe.wait_ge(y_added, j)
                        PE.matmul(ps[:, 7, 0:128], o_fm[:, j * P:j * P + P], mat(wo), start=True, stop=True)\
                            .then_inc(y_ready, 1)

            @block.scalar
            def _(act):
                for t in range(NT + 2):
                    if t < NT:
                        act.wait_ge(sub_ready, t + 1)
                        AC.activation(prob[t % 3], prob[t % 3], ACT.Exp).then_inc(exp_ready, 1)
                    if 0 <= t - 1 < NT:
                        j = t - 1
                        if j >= 2:
                            act.wait_ge(o_ready, j - 1)
                        for k in range(2):
                            act.wait_ge(ptT_ready, 2 * j + k + 1)
                            AC.activation(pT[j % 2][:, 512 * k:512 * k + 512], ps[:, 4 + k, :], ACT.Copy)\
                                .then_inc(pt_ready, 1)

            if masked:
                @block.gpsimd
                def _(pool):
                    for j in range(NT):
                        pool.wait_ge(mx_ready, j + 1)
                        pr3 = prob[j % 3].rearrange("p (h k) -> p h k", h=H)
                        G.tensor_tensor(pr3, pr3, over(mx[:, j % 2], 2, S), ALU.subtract).then_inc(sub_ready, 1)

            @block.vector
            def _(dve):
                if masked:
                    dve.wait_ge(bm_ready, NT)
                for t in range(NT + 5):
                    if t < NT:
                        pr = prob[t % 3].rearrange("p (g h k) -> p g h k", g=4, h=4)
                        pr3 = prob[t % 3].rearrange("p (h k) -> p h k", h=H)
                        if t >= 3:
                            dve.wait_ge(ptT_ready, 2 * (t - 2))
                        sc = [ps[:, 2 * g:2 * g + 2, 0:256].rearrange("p g (h k) -> p g h k", h=4) for g in range(2)]
                        mx4 = mx[:, 0].rearrange("p (g h) -> p g h", g=4)
                        if masked:
                            for g in range(2):
                                dve.wait_ge(sc_ready, 2 * t + g + 1)
                                V.tensor_tensor(pr[:, 2 * g:2 * g + 2], sc[g], over(over(seen[:, t], 1, 4), 1, 2), ALU.mult)\
                                    .then_inc(sc_read, 1)
                            dve.wait_ge(sc_read, 2 * t + 2)
                            dve_link(V.tensor_tensor(pr3, pr3, seen_bias[:, t], ALU.add))
                            if t >= 2:
                                dve.wait_ge(sub_ready, t - 1)
                            V.tensor_reduce(mx[:, t % 2], pr3, AX.X, ALU.max).then_inc(mx_ready, 1)
                        else:
                            marks = []
                            for g in range(2):
                                dve.wait_ge(sc_ready, 2 * t + g + 1)
                                if g == 0 and t >= 1:
                                    dve.wait_ge(sc_read, 2 * t)
                                marks.append(dve_mark(V.tensor_reduce(mx4[:, 2 * g:2 * g + 2], sc[g], AX.X, ALU.max)))
                            for g in range(2):
                                dve.wait_ge(dve_chain, marks[g])
                                V.tensor_tensor(pr[:, 2 * g:2 * g + 2], sc[g], over(mx4[:, 2 * g:2 * g + 2], 3, S), ALU.subtract)\
                                    .then_inc(sc_read, 1)
                            dve.wait_ge(sc_read, 2 * t + 2)
                            V.sem_inc(sub_ready, 1)
                    if 0 <= t - 1 < NT and masked:
                        j = t - 1
                        dve.wait_ge(exp_ready, j + 1)
                        V.tensor_scalar(prob[j % 3], prob[j % 3], 0.0, None, ALU.max).then_inc(clean, 1)
                    if 0 <= t - 3 < NT:
                        j = t - 3
                        dve.wait_ge(o_ready, j + 1)
                        if masked:
                            dve_link(V.tensor_scalar(rb, ps[:, 6, 128:256], 1.0, None, ALU.max))
                            V.reciprocal(rb, rb).then_inc(rb_ready, 1)
                        else:
                            V.reciprocal(rb, ps[:, 6, 128:256]).then_inc(rb_ready, 1)
                        dve.wait_ge(rb_ready, j + 1)
                        V.tensor_tensor(o_fm[:, j * P:j * P + P], ps[:, 6, 0:128], rb, ALU.mult).then_inc(of_ready, 1)
                    if 0 <= t - 4 < NT:
                        j = t - 4
                        dve.wait_ge(y_ready, j + 1)
                        V.tensor_tensor(x_tm[:, j], x_tm[:, j], ps[:, 7, 0:128], ALU.add).then_inc(y_added, 1)
                    if 0 <= t - 5 < NT:
                        dve.wait_ge(y_added, t - 4)
                        ins = tile_stats(t - 5)
                dve_link(ins)
                V.sem_inc(x_done, 1)

        l0 = keys_values(0, "L0", "L0_xattn_Wk", "L0_xattn_Wv", "L0_xattn_bq", "L0_xattn_bk", "L0_xattn_bv",
                         False, arena[:, 0:5120], (0, 1, 2, 3), lambda eng: None, layernorm)
        attention(0, "L0", "L0_xattn_Wq", "L0_xattn_Wo", "L0_xattn_bo", l0, False)
        def moe0(n):
            s = lambda name: sem(f"moe0_{name}")
            lg_ps, lg_read, gates_ok, gT_ps, gT_ok = s("logits"), s("logits_read"), s("gates"), s("gatesT"), s("gatesT_sb")
            shifted, powered = s("less_max"), s("exp")
            by_ps, by_read = s("bias_ps"), s("bias_added")
            up_ps, silu_ok, glu_ok, y_ps, y_added = s("up_ps"), s("silu"), s("glu"), s("y_ps"), s("y_added")
            lin_ps = s("lin_ps")
            lg = arena[:, 0:64].rearrange("p (j e) -> p j e", j=NT)
            pr = arena[:, 64:128].rearrange("p (j e) -> p j e", j=NT)
            t1 = arena[:, 128:192].rearrange("p (j e) -> p j e", j=NT)
            t2 = arena[:, 192:256].rearrange("p (j e) -> p j e", j=NT)
            first = arena[:, 256:320].rearrange("p (j e) -> p j e", j=NT)
            m8 = arena[:, 320:328]
            back = arena[:, 328:336]
            gates = arena[:, 336:336 + NT * NQ].rearrange("p (j e) -> p j e", j=NT)
            gT = arena[0:NQ, 512:512 + T]
            silu = arena[:, 2048:2048 + 1024].rearrange("p (k t) -> p k t", k=2)
            glu = arena[:, 4096:4096 + 2048].rearrange("p (i k t) -> p i k t", i=2, k=2)
            units = [(e, half) for e in range(NQ) for half in range(2)]

            def bias_col(which, e, k):
                i = NC_EXP + which * 2 * NQ + 2 * e + k
                return cols[:, i:i + 1]

            @block.tensor
            def _(pe):
                pe.wait_ge(moe0_in, 96)
                wait_h_fm(pe)
                for j in range(NT):
                    ins = PE.matmul(ps[:, 6, NE * j:NE * j + NE], h_fm[:, j * P:j * P + P], gate_w[:],
                                    start=True, stop=True)
                ins.then_inc(lg_ps, 1)

            @block.scalar
            def _(act):
                act.wait_ge(shifted, 1)
                AC.activation(pr, t1, ACT.Exp).then_inc(powered, 1)

            def pick_first(src, dst):
                dve_link(V.tensor_reduce(m8, src, AX.X, ALU.max))
                dve_link(V.tensor_tensor(t2, src, over(m8, 2, NE), ALU.is_equal))
                dve_link(V.tensor_tensor(t2, t2, over(back, 1, NT), ALU.mult))
                dve_link(V.tensor_reduce(m8, t2, AX.X, ALU.max))
                dve_link(V.tensor_tensor(dst, t2, over(m8, 2, NE), ALU.is_equal))

            @block.vector
            def _(dve):
                V.tensor_scalar(back, const[:, C_IOTA:C_IOTA + NE], -1.0, float(NE), ALU.mult, ALU.add)
                V.memset(gates, 1.0 / NSH)
                dve.wait_ge(moe0_in, 96)
                dve.wait_ge(lg_ps, 1)
                dve_link(V.tensor_tensor(lg, ps[:, 6, 0:64].rearrange("p (j e) -> p j e", j=NT),
                                         over(gate_b[:], 1, NT), ALU.add))
                dve_link(V.tensor_reduce(m8, lg, AX.X, ALU.max))
                V.tensor_tensor(t1, lg, over(m8, 2, NE), ALU.subtract).then_inc(shifted, 1)
                dve.wait_ge(powered, 1)
                dve_link(V.tensor_reduce(m8, pr, AX.X, ALU.add))
                dve_link(V.reciprocal(m8, m8))
                dve_link(V.tensor_tensor(pr, pr, over(m8, 2, NE), ALU.mult))
                pick_first(pr, first)
                dve_link(V.scalar_tensor_tensor(out=t1, in0=first, scalar=-2.0, in1=pr, op0=ALU.mult, op1=ALU.add))
                dve_link(V.tensor_tensor(lg, first, pr, ALU.mult))
                pick_first(t1, first)
                dve_link(V.tensor_tensor(first, first, pr, ALU.mult))
                V.tensor_tensor(gates[:, :, 0:NE], lg, first, ALU.add).then_inc(gates_ok, 1)

            @block.tensor
            def _(pe):
                def up(u):
                    e, half = units[u]
                    t = slice(512 * half, 512 * half + 512)
                    for k in range(2):
                        if u >= 1:
                            pe.wait_ge(silu_ok, 2 * (u - 1) + k + 1)
                        PE.matmul(ps[:, k, :], w1[:, e, P * k:P * k + P], h_fm[:, t], start=True, stop=True)\
                            .then_inc(up_ps, 1)
                    for k in range(2):
                        if u >= 1:
                            pe.wait_ge(glu_ok, 2 * (u - 1) + k + 1)
                        PE.matmul(ps[:, 2 + k, :], w2[:, e, P * k:P * k + P], h_fm[:, t], start=True, stop=True)\
                            .then_inc(lin_ps, 1)

                def down(u):
                    e, half = units[u]
                    pe.wait_ge(glu_ok, 2 * u + 2)
                    if u >= 2:
                        pe.wait_ge(y_added, u - 1)
                    for t in range(4):
                        for k in range(2):
                            ins = PE.matmul(ps[:, 4 + u % 2, P * t:P * t + P], glu[:, u % 2, k, P * t:P * t + P],
                                            w3[:, e, k, :], start=(k == 0), stop=(k == 1))
                    ins.then_inc(y_ps, 1)

                up(0)
                up(1)
                for u in range(len(units)):
                    if u >= 1 and u + 1 < len(units):
                        up(u + 1)
                    if u == 1:
                        pe.wait_ge(gates_ok, 1)
                        for k in range(2):
                            for j in range(4):
                                ins = PE.transpose(ps[0:NQ, 6 + k, P * j:P * j + P], gates[:, 4 * k + j, :], ident)
                            ins.then_inc(gT_ps, 1)
                        pe.wait_ge(gT_ok, 2)
                        for k in range(2):
                            for j in range(4):
                                ins = PE.matmul(ps[:, 6 + k, P * j:P * j + P],
                                                gT[:, (4 * k + j) * P:(4 * k + j + 1) * P], b3[:], start=True, stop=True)
                            ins.then_inc(by_ps, 1)
                    down(u)

            @block.scalar
            def _(act):
                for u, (e, half) in enumerate(units):
                    for k in range(2):
                        act.wait_ge(up_ps, 2 * u + k + 1)
                        if u >= 1:
                            act.wait_ge(glu_ok, 2 * (u - 1) + k + 1)
                        AC.activation(silu[:, k, :], ps[:, k, :], ACT.Silu, bias=bias_col(0, e, k)).then_inc(silu_ok, 1)
                    if u == 1:
                        for k in range(2):
                            act.wait_ge(gT_ps, k + 1)
                            AC.activation(gT[:, 512 * k:512 * k + 512], ps[0:NQ, 6 + k, :], ACT.Copy).then_inc(gT_ok, 1)

            @block.vector
            def _(dve):
                dve.wait_ge(gates_ok, 1)

                def accumulate(u):
                    e, half = units[u]
                    dve.wait_ge(y_ps, u + 1)
                    if u >= 2:
                        dve.wait_ge(y_added, u - 1)
                    for t in range(4):
                        j = 4 * half + t
                        ins = V.scalar_tensor_tensor(out=x_tm[:, j], in0=ps[:, 4 + u % 2, P * t:P * t + P],
                                                     scalar=gates[:, j, e:e + 1], in1=x_tm[:, j],
                                                     op0=ALU.mult, op1=ALU.add)
                    ins.then_inc(y_added, 1)

                for u, (e, half) in enumerate(units):
                    for k in range(2):
                        dve.wait_ge(lin_ps, 2 * u + k + 1)
                        dve.wait_ge(silu_ok, 2 * u + k + 1)
                        if u >= 2:
                            dve.wait_ge(y_ps, u - 1)
                        V.scalar_tensor_tensor(out=glu[:, u % 2, k, :], in0=ps[:, 2 + k, :], scalar=bias_col(1, e, k),
                                               in1=silu[:, k, :], op0=ALU.add, op1=ALU.mult).then_inc(glu_ok, 1)
                    if u == 2:
                        for k in range(2):
                            dve.wait_ge(by_ps, k + 1)
                            dve_link(V.tensor_tensor(x_tm[:, 4 * k:4 * k + 4], x_tm[:, 4 * k:4 * k + 4],
                                                     ps[:, 6 + k, :].rearrange("p (j d) -> p j d", j=4), ALU.add))
                    if u >= 2:
                        accumulate(u - 2)
                    if u == 4:
                        input_scales(dve)
                accumulate(len(units) - 2)
                dve.wait_ge(y_added, len(units) - 1)
                all_stats(range(4))
                accumulate(len(units) - 1)
                dve.wait_ge(y_added, len(units))
                all_stats(range(4, NT))
                V.sem_inc(x_done, 1)

        wn = sb("wn", [P, 9, P])
        wT = sb("wT", [P, 9, P])
        halves_done = sem("halves_done")
        ffn3_in, scales_ok, wq_ok, wT_ps, wT_ok = (sem("ffn3_in"), sem("scales"), sem("ffn3_w"), sem("ffn3_wT_ps"),
                                                    sem("ffn3_wT"))
        blocks = wn[:].rearrange("p c (g i) -> p (c g) i", i=32)
        wsc, winv = sb("wsc", [P, 36]), sb("winv", [P, 36])

        @block.sync
        def _(sp):
            for i, name in enumerate(("w_gate", "w_up")):
                sp.dma_start(wn[:, 3 * i:3 * i + 3, :], A[name].rearrange("(c p) i -> p c i", p=P)).then_inc(ffn3_in, 16)
            sp.dma_start(wn[:, 6:9, :], A["w_down"].rearrange("p (c i) -> p c i", c=3)).then_inc(ffn3_in, 16)

        def input_scales(dve):
            dve.wait_ge(ffn3_in, 48)
            dve_link(V.tensor_reduce(wsc[:], blocks, AX.X, ALU.max, apply_absolute_value=True))
            dve_link(V.tensor_scalar(wsc[:], wsc[:], 1.0 / 7.0, 1e-12, ALU.mult, ALU.max))
            V.reciprocal(winv[:], wsc[:]).then_inc(scales_ok, 1)
            dve.wait_ge(mask_in, 32)
            dve_link(V.tensor_reduce(sinv[:], mask_sb[:], AX.X, ALU.add))
            dve_link(V.tensor_scalar(sign[:], sinv[:], -1.0, float(S - 1), ALU.mult, ALU.add))
            V.reciprocal(sinv[:], sign[:]).then_inc(scales_ok, 1)

        @block.gpsimd
        def _(pool):
            pool.wait_ge(scales_ok, 1)
            pool_link(G.tensor_tensor(blocks, blocks, over(winv[:], 2, 32), ALU.mult))
            pool_link(G.tensor_scalar(blocks, blocks, MAGIC, -MAGIC, ALU.add, ALU.add))
            G.tensor_tensor(blocks, blocks, over(wsc[:], 2, 32), ALU.mult).then_inc(wq_ok, 1)

        mask_sb = sb("mask_sb", [P, NT, S], I32)
        picks_b = sb("picks_b", [P, 26, P], BF16)
        sign, sinv = sb("sign", [P, NT]), sb("sinv", [P, NT])
        mask_in, picks_in, picks_ok = sem("mask_in"), sem("picks_in"), sem("picks_ok")
        kv_ps, kv_ok = sem("def_kv_ps"), sem("def_kv")
        kv = kexp[:].rearrange("p (j h v b d) -> p j h v b d", j=NT, h=H, v=2, b=2)

        @block.sync
        def _(sp):
            sp.dma_start(l2buf[:, 0:26 * P], A["picks"]).then_inc(picks_in, 16)
            for b in range(2):
                sp.dma_start(mask_sb[S * b:S * b + S],
                             A["mask"].rearrange("(j b) s -> b j s", b=2)[b].partition_broadcast(S)).then_inc(mask_in, 16)

        ab = l2buf[:, 0:4096].rearrange("p (m c) -> p m c", c=P)
        ka = l2buf[:, 4096:6144].rearrange("p (s j c) -> p s j c", s=2, j=NT)
        va = l2buf[:, 6144:8192].rearrange("p (s t) -> p s t", s=2)
        kg_ok, vg_ok = sem("chan_k"), sem("chan_v")

        @block.gpsimd
        def _(pool):
            pool.wait_ge(picks_in, 16)
            G.tensor_copy(picks_b[:].rearrange("p a b -> p (a b)"), l2buf[:, 0:26 * P]).then_inc(picks_ok, 1)
            pool.wait_ge(x_done, 1)
            G.memset(kexp[:], 0.0).then_inc(cleared, 1)
            pool.wait_ge(picks_ok, 1)
            G.memset(l2buf[:, 0:4096], 0.0).then_inc(cleared, 1)
            pool.wait_ge(ctxt_in, 16)
            pool.wait_ge(rows_in, 16)
            for i, name in enumerate(("g", "l")):
                G.tensor_tensor(ka[:, i], ctx_tm[:], over(row(f"L1_xattn_wk{name}"), 1, NT), ALU.mult)\
                    .then_inc(kg_ok, 1)
                pool.wait_ge(kg_ok, 2 * i + 1)
                G.tensor_tensor(ka[:, i], ka[:, i], over(row(f"L1_xattn_bk{name}"), 1, NT), ALU.add)\
                    .then_inc(kg_ok, 1)

        @block.scalar
        def _(act):
            act.wait_ge(cols_in, 16)
            act.wait_ge(ctxf_in, 16)
            for i, name in enumerate(("g", "l")):
                AC.activation(va[:, i], ctx_fm[:], ACT.Identity, bias=col(f"L1_xattn_bv{name}"),
                              scale=col(f"L1_xattn_wv{name}")).then_inc(vg_ok, 1)

        if LAST >= 2:
            layernorm()
            moe0(1)

        def keys_values_l2(pe, banks):
            wkv = mats[:, MATS.index("L2_xattn_Wk"):MATS.index("L2_xattn_Wk") + 2, :].rearrange("p a b -> p (a b)")
            bkv = over(rows[0:1, ROWS.index("L2_xattn_bk"):ROWS.index("L2_xattn_bk") + 2, :]
                       .rearrange("p a b -> p (a b)"), 1, 2)
            one = const[0:1, C_IOTA + 1:C_IOTA + 2].broadcast_to([1, P])
            for bank in banks:
                if bank >= 2:
                    pe.wait_ge(kv_ok, 2 * (bank - 1))
                at_ps = ps[:, 6 + bank % 2, :]
                PE.matmul(at_ps.rearrange("p (j c) -> p j c", j=2), one, bkv, start=True, stop=False)
                for i in range(2):
                    j = 2 * bank + i
                    ins = PE.matmul(at_ps[:, 256 * i:256 * i + 256], ctx_fm[:, P * j:P * j + P], wkv,
                                    start=False, stop=(i == 1))
                ins.then_inc(kv_ps, 1)

        def keys_values_l2_blocks(act, banks):
            act.wait_ge(cleared, KV_CLEAR)
            for bank in banks:
                act.wait_ge(kv_ps, bank + 1)
                for b in range(2):
                    r = slice(S * b, S * b + S)
                    for v in range(2):
                        src = ps[r, 6 + bank % 2, :].rearrange("p (j v h d) -> p j v h d", j=2, v=2, h=H)[:, :, v]
                        ins = AC.activation(kv[r, 2 * bank:2 * bank + 2, :, v, b, :], src, ACT.Copy)
                    ins.then_inc(kv_ok, 1)

        def channel_attention(n):
            s = lambda name: sem(f"chan_{name}")
            q_ok, s_ps, sub_ok, e_ok, n_ok, ab_ok, y_ps = (
                s("q"), s("scores"), s("less_max"), s("exp"), s("attn"), s("attnT"), s("y"))
            sets = 2
            weight_banks = ((6, 0, 4), (7, 4, 8), (6, 8, 9))
            qa = arena[:, 0:2048].rearrange("p (s j c) -> p s j c", s=2, j=NT)
            at = arena[:, 6144:7168].rearrange("p (m e) -> p m e", e=32)
            m32 = arena[:, 7168:7200]
            att = arena[:, 7424:8448].rearrange("p (j c) -> p j c", j=NT)

            layernorm(feature_major=False)

            @block.vector
            def _(dve):
                wait_h_tm(dve)
                for i, name in enumerate(("g", "l")):
                    dve_link(V.tensor_tensor(qa[:, i], h_tm[:], over(row(f"L1_xattn_wq{name}"), 1, NT), ALU.mult))
                    V.tensor_tensor(qa[:, i], qa[:, i], over(row(f"L1_xattn_bq{name}"), 1, NT), ALU.add)\
                        .then_inc(q_ok, 1)
                dve_link(V.tensor_tensor(x_tm[:], x_tm[:], over(row("L1_xattn_bp"), 1, NT), ALU.add))

            @block.tensor
            def _(pe):
                pe.wait_ge(wq_ok, 1)
                pe.wait_ge(x_done, n)
                for k, (bank, c0, c1) in enumerate(weight_banks):
                    if k == 2:
                        pe.wait_ge(wT_ok, 1)
                    for c in range(c0, c1):
                        ins = PE.transpose(ps[:, bank, P * (c - c0):P * (c - c0) + P], wn[:, c, :], ident)
                    ins.then_inc(wT_ps, 1)
                for i in range(sets):
                    pe.wait_ge(kg_ok, 2 * i + 2)
                    pe.wait_ge(q_ok, i + 1)
                    for b in range(B):
                        r = slice(S * (b % 2), S * (b % 2) + S)
                        for h in range(4):
                            c = slice(32 * h, 32 * h + 32)
                            ins = PE.matmul(ps[c, 2 * i + b % 2, 32 * (b // 2):32 * (b // 2) + 32], qa[r, i, b // 2, c], ka[r, i, b // 2, c],
                                            start=True, stop=True)
                    ins.then_inc(s_ps, 1)
                pe.wait_ge(wT_ok, 3)
                keys_values_l2(pe, (0, 1))
                pe.wait_ge(vg_ok, 2)
                pe.wait_ge(ab_ok, 1)
                for j in range(NT):
                    for half in range(2):
                        b = 2 * j + half
                        for i in range(sets):
                            ins = PE.matmul(ps[S * half:S * half + S, 4 + j // 4, P * (j % 4):P * (j % 4) + P],
                                            va[:, i, S * b:S * b + S], ab[:, B * i + NT * half + j, :],
                                            start=(i == 0), stop=(i == 1))
                    if j % 4 == 3:
                        ins.then_inc(y_ps, 1)

            @block.vector
            def _(dve):
                for i in range(sets):
                    mi = slice(B * i, B * i + B)
                    dve.wait_ge(s_ps, i + 1)
                    sc = ps[:, 2 * i:2 * i + 2, 0:256].rearrange("p b (m e) -> p b m e", e=32)
                    pair = lambda v: v.rearrange("p (b m) -> p b m", b=2)
                    dve_link(V.tensor_reduce(pair(m32[:, mi]), sc, AX.X, ALU.max))
                    V.tensor_tensor(at[:, mi].rearrange("p (b m) e -> p b m e", b=2), sc,
                                    over(pair(m32[:, mi]), 3, 32), ALU.subtract).then_inc(sub_ok, 1)
                    dve.wait_ge(e_ok, i + 1)
                    dve_link(V.tensor_reduce(m32[:, mi], at[:, mi], AX.X, ALU.add))
                    dve_link(V.reciprocal(m32[:, mi], m32[:, mi]))
                    dve_link(V.tensor_tensor(at[:, mi], at[:, mi], over(m32[:, mi], 2, 32), ALU.mult))
                    dve.wait_ge(cleared, AB_CLEAR)
                    for h in range(4):
                        c = slice(32 * h, 32 * h + 32)
                        ins = V.transpose(ab[c, mi, c], at[c, mi])
                ins.then_inc(ab_ok, 1)
                for k in range(2):
                    dve.wait_ge(y_ps, k + 1)
                    dve_link(V.scalar_tensor_tensor(out=att[:, 4 * k:4 * k + 4],
                                                    in0=ps[:, 4 + k, :].rearrange("p (j c) -> p j c", j=4), scalar=2.0,
                                                    in1=over(row("L1_xattn_wp"), 1, 4), op0=ALU.mult, op1=ALU.mult))
                    ins = V.tensor_tensor(x_tm[:, 4 * k:4 * k + 4], x_tm[:, 4 * k:4 * k + 4], att[:, 4 * k:4 * k + 4],
                                          ALU.add)
                    dve_link(ins)
                    all_stats(range(4 * k, 4 * k + 4))
                V.sem_inc(x_done, 1)

            @block.scalar
            def _(act):
                for k, (bank, c0, c1) in enumerate(weight_banks):
                    act.wait_ge(wT_ps, k + 1)
                    AC.activation(wT[:, c0:c1, :].rearrange("p c k -> p (c k)"), ps[:, bank, 0:P * (c1 - c0)], ACT.Copy)\
                        .then_inc(wT_ok, 1)
                for i in range(sets):
                    act.wait_ge(sub_ok, i + 1)
                    AC.activation(at[:, B * i:B * i + B], at[:, B * i:B * i + B], ACT.Exp,
                                  scale=float(D) ** -0.5).then_inc(e_ok, 1)
                keys_values_l2_blocks(act, (0, 1))

        if LAST >= 3:
            channel_attention(2)

        wq8_in = sem("wq8_in")
        wq8 = sb("wq8", [P, P], I32)
        wq8b = sb("wq8b", [P, P], BF16)
        ident_b = sb("ident_b", [P, P], BF16)

        def int8_linear(n):
            s = lambda name: sem(f"int8_{name}")
            xq_ok, xT_ps, xT_ok, y_ps = s("x"), s("xT_ps"), s("xT"), s("y")
            am = arena[:, 0:8]
            xs = arena[:, 8:16]
            inv = arena[:, 16:24]
            t = arena[:, 1024:2048].rearrange("p (j c) -> p j c", j=NT)
            y = arena[:, 2048:3072].rearrange("p (j c) -> p j c", j=NT)
            xq = arena[:, 3072:3584].bitcast(BF16).rearrange("p (j c) -> p j c", j=NT)
            xT = arena[:, 3584:4096].bitcast(BF16)

            @block.sync
            def _(sp):
                sp.dma_start(wq8[:], A["wq8"]).then_inc(wq8_in, 16)

            layernorm(feature_major=False)

            @block.vector
            def _(dve):
                dve.wait_ge(wq8_in, 16)
                V.tensor_copy(wq8b[:], wq8[:])
                V.tensor_copy(ident_b[:], ident)
                wait_h_tm(dve)
                dve_link(V.tensor_reduce(am, h_tm[:], AX.X, ALU.max, apply_absolute_value=True))
                dve_link(V.tensor_scalar(xs, am, 1e-6, 1.0 / 127.0, ALU.max, ALU.mult))
                dve_link(V.reciprocal(inv, xs))
                dve_link(V.tensor_tensor(t, h_tm[:], over(inv, 2, D), ALU.mult))
                dve_link(V.tensor_scalar(t, t, MAGIC, -MAGIC, ALU.add, ALU.add))
                V.tensor_scalar(xq, t, -128.0, 127.0, ALU.max, ALU.min).then_inc(xq_ok, 1)
                dve_link(V.tensor_tensor(x_tm[:], x_tm[:], over(row("L1_ffn_bias"), 1, NT), ALU.add))
                for k in range(2):
                    r = slice(4 * k, 4 * k + 4)
                    dve.wait_ge(y_ps, k + 1)
                    dve_link(V.tensor_tensor(y[:, r], ps[:, 2 + k, :].rearrange("p (j c) -> p j c", j=4),
                                             over(xs[:, r], 2, D), ALU.mult))
                    dve_link(V.tensor_tensor(y[:, r], y[:, r], over(row("L1_ffn_weight_scale"), 1, 4), ALU.mult))
                    dve_link(V.tensor_tensor(x_tm[:, r], x_tm[:, r], y[:, r], ALU.add))
                    all_stats(range(4 * k, 4 * k + 4))
                V.sem_inc(x_done, 1)

            @block.tensor
            def _(pe):
                tp = ps[:, 0, :].bitcast(BF16)

                keys_values_l2(pe, (2, 3))
                pe.wait_ge(xq_ok, 1)
                for j in range(NT):
                    ins = PE.transpose(tp[:, P * j:P * j + P], xq[:, j], ident_b[:])
                ins.then_inc(xT_ps, 1)
                pe.wait_ge(xT_ok, 1)
                for k in range(2):
                    for j in range(4):
                        i = 4 * k + j
                        ins = PE.matmul(ps[:, 2 + k, P * j:P * j + P], xT[:, P * i:P * i + P], wq8b[:],
                                        start=True, stop=True)
                    ins.then_inc(y_ps, 1)

            @block.scalar
            def _(act):
                keys_values_l2_blocks(act, (2, 3))
                act.wait_ge(xT_ps, 1)
                AC.activation(xT, ps[:, 0, :].bitcast(BF16), ACT.Copy).then_inc(xT_ok, 1)

        if LAST >= 4:
            int8_linear(3)

        def deformable(n):
            s = lambda name: sem(f"def_{name}")
            q_ps, q_sb, qt_ps, qt_ok, qx_ok = s("q_ps"), s("q_sb"), s("qt_ps"), s("qt"), s("qx")
            off_ps, parts_ok, parts1_ok, mv_ps, ix_ok = s("off_ps"), s("parts0"), s("parts1"), s("moved_ps"), s("ix")
            bc_ps, abs_ok, hat_ok = s("bc_ps"), s("abs"), s("hat")
            smp_ps, smp_sb0, smp_sb, turned = s("sampled_ps"), s("sampled_even"), s("sampled_odd"), s("turned")
            cx_ok = s("ctx_sb")
            v_ok, prod_ok, sc_ok, e_ok, c_ok, cT_ps, cT_ok, y_ps = (
                s("sv"), s("prod"), s("scores"), s("exp"), s("ctx"), s("ctxT_ps"), s("ctxT"), s("y"))
            off_sb = s("off_sb")
            kvc = kexp[:].rearrange("p (j h m) -> p j h m", j=NT, h=H)
            hats = arena[:].rearrange("p (i r c) -> p i r c", i=2, r=20)
            qt = v4[:, 64:1088].rearrange("p (i h b d) -> p i h b d", i=4, h=H, b=2)
            cxn = v4[:, 1088:2112].rearrange("p (i g c) -> p i g c", i=4, g=4)
            cx = l2buf[:, 2560:3584].rearrange("p (i b c) -> p i b c", i=4, b=2)
            smp = l2buf[:, 2560:3840].rearrange("p (i k c) -> p i k c", i=2, k=NK)
            prod = v4[:, 2112:2752].rearrange("p (i r c) -> p i r c", i=2, c=16)
            sc = v4[:, 2752:2752 + 320].rearrange("p (i r b) -> p i r b", i=2, b=2)
            mx = v4[:, 3072:3104]
            rs = v4[:, 3104:3136]
            spare = ctx_tm[:].rearrange("p j d -> p (j d)")
            off = [l2buf[:, 0:512], spare[:, 0:512]]
            t1 = [l2buf[:, 512:1024], spare[:, 512:1024]]
            parts = [v.bitcast(BF16).rearrange("p (i c) -> p i c", i=3) for v in (l2buf[:, 3840:4608], v4[:, 3136:3904])]
            ixm = l2buf[:, 4608:5632].bitcast(BF16).rearrange("p (g c) -> p g c", g=4)
            qx = l2buf[:, 0:2560].rearrange("p (i r c) -> p i r c", i=2, c=16)
            sv = l2buf[:, 5632:8192].rearrange("p (i r c) -> p i r c", i=2, c=16)
            units = [(hg, half) for hg in range(4) for half in range(2)]
            qscale = -0.5 / float(np.sqrt(HD))

            layernorm()

            @block.tensor
            def _(pe):
                wait_h_fm(pe)
                for k in range(2):
                    PE.matmul(ps[:, 6 + k, :], mat("L2_xattn_Wq"), h_fm[:, 512 * k:512 * k + 512],
                              start=True, stop=True).then_inc(q_ps, 1)
                pe.wait_ge(q_sb, 2)
                qv = q_fm[:].rearrange("p (j b q) -> p j b q", j=NT, b=2)
                for g in range(2):
                    for b in range(2):
                        ins = PE.matmul(ps[S * b:S * b + S, 2 + g, :], woff[:, g, :], qv[:, :, b, :], start=True, stop=True)
                    ins.then_inc(off_ps, 1)
                for j in range(NT):
                    for b in range(2):
                        c = (j // 2) * 256 + P * b
                        ins = PE.matmul(ps[S * (j % 2):S * (j % 2) + S, c // 512, c % 512:c % 512 + P],
                                        h_fm[:, P * j + S * b:P * j + S * b + S], mat("L2_xattn_Wq"), start=True, stop=True)
                ins.then_inc(qt_ps, 1)

            def move(pe, hg):
                if hg >= 1:
                    pe.wait_ge(ix_ok, hg)
                for i in range(3):
                    ins = PE.matmul(ps[:, 3, :], picks_b[:, 20 + 3 * (hg % 2) + i, :], parts[hg // 2][:, i],
                                    start=(i == 0), stop=(i == 2))
                ins.then_inc(mv_ps, 1)

            def keep_positions(act, hg):
                act.wait_ge(mv_ps, hg + 1)
                AC.activation(ixm[:, hg, :], ps[:, 3, :], ACT.Copy).then_inc(ix_ok, 1)

            @block.scalar
            def _(act):
                for k in range(2):
                    act.wait_ge(q_ps, k + 1)
                    AC.activation(q_fm[:, 512 * k:512 * k + 512], ps[:, 6 + k, :], ACT.Identity,
                                  bias=col("L2_xattn_bq")).then_inc(q_sb, 1)
                for g in range(2):
                    act.wait_ge(off_ps, g + 1)
                    AC.activation(off[g], ps[:, 2 + g, :], ACT.Identity,
                                  bias=cols[:, NC_EXP + 4 * NQ + g:NC_EXP + 4 * NQ + g + 1]).then_inc(off_sb, 1)

            def positions(eng, E, link, g, done):
                def jq(v):
                    return v[g].rearrange("p (j q) -> p j q", j=NT)

                eng.wait_ge(off_sb, g + 1)
                eng.wait_ge(scales_ok, 2)
                ref = over(const[:, C_REF:C_REF + S], 1, NT)
                sg, iv = over(sign[:], 2, S), over(sinv[:], 2, S)
                link(E.tensor_tensor(jq(off), jq(off), ref, ALU.add))
                link(E.tensor_tensor(jq(t1), jq(off), iv, ALU.mult))
                link(E.tensor_scalar(t1[g], t1[g], MAGIC, -MAGIC, ALU.add, ALU.add))
                link(E.tensor_tensor(jq(t1), jq(t1), sg, ALU.mult))
                link(E.tensor_tensor(off[g], off[g], t1[g], ALU.subtract))
                link(E.tensor_tensor(jq(t1), jq(off), iv, ALU.mult))
                link(E.tensor_scalar(t1[g], t1[g], 0.0, None, ALU.is_lt))
                link(E.tensor_tensor(jq(t1), jq(t1), sg, ALU.mult))
                link(E.tensor_tensor(off[g], off[g], t1[g], ALU.add))
                link(E.tensor_scalar(off[g], off[g], float(S) / (S - 1), -0.5, ALU.mult, ALU.add))
                link(E.tensor_copy(parts[g][:, 0], off[g]))
                link(E.tensor_tensor(t1[g], off[g], parts[g][:, 0], ALU.subtract))
                link(E.tensor_copy(parts[g][:, 1], t1[g]))
                E.tensor_tensor(parts[g][:, 2], t1[g], parts[g][:, 1], ALU.subtract).then_inc(done, 1)

            @block.gpsimd
            def _(pool):
                positions(pool, G, pool_link, 1, parts1_ok)

            @block.vector
            def _(dve):
                positions(dve, V, dve_link, 0, parts_ok)
                dve.wait_ge(qt_ps, 1)
                for c in range(4):
                    src = ps[:, c // 2, 256 * (c % 2):256 * (c % 2) + 256].rearrange("p (b h d) -> p h b d", b=2, h=H)
                    bias = over(row("L2_xattn_bq").rearrange("p (h d) -> p h d", h=H), 2, 2)
                    ins = V.tensor_tensor(qt[:, c], src, bias, ALU.add)
                ins.then_inc(qt_ok, 1)
                wait_h_tm(dve)
                dve_link(V.tensor_tensor(x_tm[:], x_tm[:], over(row("L2_xattn_bo"), 1, NT), ALU.add))

            NW = 2 * len(units)

            def chunks(w):
                return list(range(5 * (w % 2), 5 * (w % 2) + 5)) if w // 2 + 1 < len(units) else []

            @block.tensor
            def _(pe):
                def broadcast(u, c):
                    hg, half = units[u]
                    m = 10 * u + c
                    if m >= 3:
                        pe.wait_ge(abs_ok, m - 2)
                    for i in range(2):
                        ins = PE.matmul(ps[:, m % 3, 256 * i:256 * i + 256], picks_b[:, 2 * c + i, :],
                                        ixm[:, hg, 256 * half:256 * half + 256], start=True, stop=True)
                    ins.then_inc(bc_ps, 1)

                def sample(w):
                    u, i = w // 2, w % 2
                    hg, half = units[u]
                    pe.wait_ge(hat_ok, 10 * (u + 1))
                    if w >= 1:
                        pe.wait_ge(smp_sb0, w)
                        pe.wait_ge(smp_sb, w)
                    for par in range(2):
                        j = 4 * half + 2 * i + par
                        for hl in range(4):
                            ins = PE.matmul(ps[32 * hl:32 * hl + 32, 4 + par, 0:NK * S], kvc[:, j, 4 * hg + hl, :],
                                            hats[:, u % 2, NK * hl:NK * hl + NK, S * (2 * i + par):S * (2 * i + par) + S],
                                            start=True, stop=True)
                    ins.then_inc(smp_ps, 1)

                def turn(w):
                    pe.wait_ge(smp_sb0, w + 1)
                    pe.wait_ge(smp_sb, w + 1)
                    if w >= 1:
                        pe.wait_ge(prod_ok, w)
                        pe.wait_ge(v_ok, w)
                    for k in range(NK):
                        for h0, h1 in (((0, 2), (2, 4)) if k == 2 else ((0, 4),)):
                            at = 4 * k + h0
                            ins = PE.matmul(ps[:, 6 + at // 10, 32 * (at % 10):32 * (at % 10 + h1 - h0)], smp[:, w % 2, k, :],
                                            ident[:, 32 * h0:32 * h1], start=True, stop=True)
                    ins.then_inc(turned, 1)

                pe.wait_ge(off_sb, 2)
                pe.wait_ge(parts_ok, 1)
                move(pe, 0)
                pe.wait_ge(qt_ok, 1)
                pe.wait_ge(ix_ok, 1)
                for c in range(10):
                    broadcast(0, c)
                pe.wait_ge(kv_ok, 8)
                for w in range(NW + 1):
                    if w == 1:
                        move(pe, 1)
                    if w in (5, 7):
                        pe.wait_ge(parts1_ok, 1)
                        move(pe, 2 + w // 6)
                    if w in (2, 6, 10):
                        pe.wait_ge(ix_ok, w // 4 + 2)
                    for c in chunks(w)[:3]:
                        broadcast(w // 2 + 1, c)
                    if w >= 1:
                        turn(w - 1)
                    for c in chunks(w)[3:]:
                        broadcast(w // 2 + 1, c)
                    if w < NW:
                        sample(w)
                pe.wait_ge(cx_ok, 1)
                for jp in range(4):
                    for b in range(2):
                        ins = PE.transpose(ps[:, jp // 2, 256 * (jp % 2) + P * b:256 * (jp % 2) + P * b + P],
                                           cx[:, jp, b, :], ident)
                    if jp % 2 == 1:
                        ins.then_inc(cT_ps, 1)
                for k in range(2):
                    pe.wait_ge(cT_ok, k + 1)
                    for i in range(4):
                        j = 4 * k + i
                        ins = PE.matmul(ps[:, 2 + k, P * i:P * i + P], o_fm[:, P * j:P * j + P], mat("L2_xattn_Wo"),
                                        start=True, stop=True)
                    ins.then_inc(y_ps, 1)

            @block.scalar
            def _(act):
                def spread_q(hg):
                    act.wait_ge(qt_ok, 1)
                    if hg >= 2:
                        act.wait_ge(prod_ok, 4 * (hg - 1))
                    src = over(qt[:, :, 4 * hg:4 * hg + 4].rearrange("p i h b d -> p i (h b d)"), 2, NK)
                    dst = qx[:, hg % 2].rearrange("p (i k h) c -> p i k (h c)", i=4, k=NK)
                    AC.activation(dst, src, ACT.Copy, scale=qscale).then_inc(qx_ok, 1)

                def absolute(u, c):
                    m = 10 * u + c
                    act.wait_ge(bc_ps, m + 1)
                    if u >= 2 and c == 0:
                        act.wait_ge(smp_ps, 2 * (u - 1))
                    AC.activation(hats[:, u % 2, 2 * c:2 * c + 2, :].rearrange("p r c -> p (r c)"), ps[:, m % 3, :],
                                  ACT.Abs, bias=const[:, C_NEGM:C_NEGM + 1]).then_inc(abs_ok, 1)

                def exponentials(hg):
                    act.wait_ge(sc_ok, hg + 1)
                    AC.activation(sc[:, hg % 2], sc[:, hg % 2], ACT.Exp).then_inc(e_ok, 1)

                def to_sbuf(w):
                    act.wait_ge(smp_ps, w + 1)
                    if w >= 2:
                        act.wait_ge(turned, w - 1)
                    AC.activation(smp[:, w % 2, :, 0:S], ps[:, 4, 0:NK * S].rearrange("p (k q) -> p k q", k=NK), ACT.Copy)\
                        .then_inc(smp_sb0, 1)

                def keep_values(w):
                    hg, jp = w // 4, w % 4
                    act.wait_ge(prod_ok, w + 1)
                    if jp == 0 and hg >= 2:
                        act.wait_ge(c_ok, hg - 1)
                    src = ps[:, 6:8, 0:320].rearrange("p k (r c) -> p k r c", c=32)[:, :, :, 16:32]
                    dst = sv[:, hg % 2, 20 * jp:20 * jp + 20].rearrange("p (k r) c -> p k r c", k=2)
                    AC.activation(dst, src, ACT.Copy).then_inc(v_ok, 1)

                keep_positions(act, 0)
                for c in range(10):
                    absolute(0, c)
                spread_q(0)
                for w in range(NW + 1):
                    if w in (1, 5, 7):
                        keep_positions(act, {1: 1, 5: 2, 7: 3}[w])
                    if w >= 1:
                        to_sbuf(w - 1)
                    for c in chunks(w):
                        absolute(w // 2 + 1, c)
                    if w >= 1:
                        keep_values(w - 1)
                    if w % 4 == 2 and w // 4 + 1 < 4:
                        spread_q(w // 4 + 1)
                    if w % 4 == 1 and w >= 5:
                        exponentials(w // 4 - 1)
                exponentials(3)
                act.wait_ge(c_ok, 4)
                for b in range(2):
                    src = cxn[:].rearrange("p i g (h b d) -> p i (g h) b d", h=4, b=2)[:, :, :, b, :]
                    ins = AC.activation(cx[:, :, b, :].rearrange("p i (h d) -> p i h d", h=H), src, ACT.Copy)
                ins.then_inc(cx_ok, 1)
                for k in range(2):
                    act.wait_ge(cT_ps, k + 1)
                    dst = o_fm[:, 512 * k:512 * k + 512].rearrange("p (i t b q) -> p i t b q", i=2, t=2, b=2)
                    src = ps[:, k, :].rearrange("p (i b t q) -> p i t b q", i=2, b=2, t=2)
                    for i in range(2):
                        ins = AC.activation(dst[:, i], src[:, i], ACT.Copy)
                    ins.then_inc(cT_ok, 1)

            @block.vector
            def _(dve):
                def hat(u, c):
                    dve.wait_ge(abs_ok, 10 * u + c + 1)
                    v = hats[:, u % 2, 2 * c:2 * c + 2, :].rearrange("p r c -> p (r c)")
                    V.tensor_scalar(v, v, 1.0, -1.0, ALU.min, ALU.add).then_inc(hat_ok, 1)

                def to_sbuf(w):
                    dve.wait_ge(smp_ps, w + 1)
                    if w >= 2:
                        dve.wait_ge(turned, w - 1)
                    V.tensor_copy(smp[:, w % 2, :, S:P], ps[:, 5, 0:NK * S].rearrange("p (k q) -> p k q", k=NK))\
                        .then_inc(smp_sb, 1)

                def multiply(w):
                    hg, jp = w // 4, w % 4
                    dve.wait_ge(turned, w + 1)
                    if jp == 0:
                        dve.wait_ge(qx_ok, hg + 1)
                    src = ps[:, 6:8, 0:320].rearrange("p k (r c) -> p k r c", c=32)[:, :, :, 0:16]
                    pr = prod[:, w % 2]
                    V.tensor_tensor(pr.rearrange("p (k r) c -> p k r c", k=2), src,
                                    qx[:, hg % 2, 20 * jp:20 * jp + 20].rearrange("p (k r) c -> p k r c", k=2),
                                    ALU.mult).then_inc(prod_ok, 1)

                def add_up(w):
                    hg, jp, pr = w // 4, w % 4, prod[:, w % 2]
                    dve.wait_ge(prod_ok, w + 1)
                    dve_link(V.tensor_reduce(sc[:, hg % 2, 20 * jp:20 * jp + 20, :],
                                             pr.rearrange("p r (b d) -> p r b d", b=2), AX.X, ALU.add))

                def by_point(hg):
                    v = sc[:, hg % 2].rearrange("p (i k h) b -> p i (h b) k", i=4, k=NK)
                    return v, lambda t: t.rearrange("p (i c) -> p i c", i=4)

                def softmax(hg):
                    v, ic = by_point(hg)
                    dve_link(V.tensor_reduce(ic(mx), v, AX.X, ALU.max))
                    V.tensor_tensor(v, v, over(ic(mx), 3, NK), ALU.subtract).then_inc(sc_ok, 1)

                def context(hg):
                    v, ic = by_point(hg)
                    dve.wait_ge(e_ok, hg + 1)
                    dve_link(V.tensor_reduce(ic(rs), v, AX.X, ALU.add))
                    dve_link(V.reciprocal(rs, rs))
                    dve_link(V.tensor_scalar(rs, rs, -0.5, None, ALU.mult))
                    dve_link(V.tensor_tensor(v, v, over(ic(rs), 3, NK), ALU.mult))
                    dve.wait_ge(v_ok, 4 * hg + 4)
                    values = sv[:, hg % 2].rearrange("p r (b d) -> p (r b) d", b=2)
                    dve_link(V.tensor_tensor(values, values, over(sc[:, hg % 2].rearrange("p r b -> p (r b)"), 2, HD), ALU.mult))
                    V.tensor_reduce(cxn[:, :, hg], sv[:, hg % 2].rearrange("p (i k h) c -> p i (h c) k", i=4, k=NK),
                                    AX.X, ALU.add).then_inc(c_ok, 1)

                for c in range(10):
                    hat(0, c)
                for w in range(NW + 1):
                    if w >= 1:
                        to_sbuf(w - 1)
                    for c in chunks(w)[:3]:
                        hat(w // 2 + 1, c)
                    if w >= 1:
                        multiply(w - 1)
                    for c in chunks(w)[3:4]:
                        hat(w // 2 + 1, c)
                    if w >= 1:
                        add_up(w - 1)
                    for c in chunks(w)[4:]:
                        hat(w // 2 + 1, c)
                    if w % 4 == 0 and w >= 4:
                        softmax(w // 4 - 1)
                    if w % 4 == 2 and w >= 6:
                        context(w // 4 - 1)
                context(3)
                for k in range(2):
                    dve.wait_ge(y_ps, k + 1)
                    dve_link(V.tensor_tensor(x_tm[:, 4 * k:4 * k + 4], x_tm[:, 4 * k:4 * k + 4],
                                             ps[:, 2 + k, :].rearrange("p (j d) -> p j d", j=4), ALU.add))
                    all_stats(range(4 * k, 4 * k + 4))
                V.sem_inc(x_done, 1)

        if LAST >= 5:
            @block.tensor
            def _(pe):
                pe.wait_ge(picks_ok, 1)

            deformable(4)

        moe2_in = sem("moe2_in")
        bias_in, bm_ready, bm_done = sem("bias_in"), sem("bias_seen"), sem("bias_ready")
        m2w1 = weights[:, 0:4096].rearrange("p (e f) -> p e f", e=NE)
        m2w2 = weights[:, 4096:8192].rearrange("p (e k d) -> p e k d", e=NE, k=4)
        idx = sb("idx", [P, 4, TOPK], I32)
        gw = sb("gw", [P, 4, TOPK])

        def moe2(n, beside_experts, beside_gelu):
            s = lambda name: sem(f"moe2_{name}")
            up_ps, g_ok, y_ps, y_added, gates_ok = s("up_ps"), s("gelu"), s("y"), s("y_added"), s("gates")
            hid = arena[:, 0:4096].rearrange("p (i k t) -> p i k t", i=2, k=4)
            idf = arena[:, 4096:4104].rearrange("p (j k) -> p j k", j=4)
            g2 = arena[:, 4128:4192].rearrange("p (j k e) -> p j k e", j=4, k=2)
            gates = arena[:, 4192:4224].rearrange("p (j e) -> p j e", j=4)

            layernorm()

            @block.vector
            def _(dve):
                dve.wait_ge(moe2_in, 64)
                dve_link(V.tensor_copy(idf, idx[:]))
                for k in range(TOPK):
                    eq = over(idf[:, :, k], 2, NE)
                    ins = V.tensor_tensor(g2[:, :, k, :], eq, over(const[:, C_IOTA:C_IOTA + NE], 1, 4), ALU.is_equal)
                dve_link(ins)
                for k in range(TOPK):
                    ins = V.tensor_tensor(g2[:, :, k, :], g2[:, :, k, :], over(gw[:, :, k], 2, NE), ALU.mult)
                dve_link(ins)
                dve_link(V.tensor_tensor(gates, g2[:, :, 0, :], g2[:, :, 1, :], ALU.add))
                wait_h_tm(dve)
                dve_link(V.tensor_tensor(x_tm[:], x_tm[:], over(row("L2_ffn_bias"), 1, NT), ALU.add))
                for j in range(4, NT):
                    tile_stats(j)
                beside_experts(dve, -1)
                for e in range(NE):
                    dve.wait_ge(y_ps, e + 1)
                    if e >= 1:
                        dve.wait_ge(y_added, e)
                    for j in range(4):
                        ins = V.scalar_tensor_tensor(out=x_tm[:, j], in0=ps[:, 4 + e % 2, P * j:P * j + P],
                                                     scalar=gates[:, j, e:e + 1], in1=x_tm[:, j],
                                                     op0=ALU.mult, op1=ALU.add)
                    ins.then_inc(y_added, 1)
                    beside_experts(dve, e)
                dve.wait_ge(y_added, NE)
                for j in range(4):
                    ins = tile_stats(j)
                dve_link(ins)
                V.sem_inc(x_done, 1)

            @block.tensor
            def _(pe):
                wait_h_fm(pe)
                pe.wait_ge(moe2_in, 64)

                def up(e):
                    for k in range(4):
                        if e >= 1:
                            pe.wait_ge(g_ok, 4 * (e - 1) + k + 1)
                        elif k >= 2:
                            pe.wait_ge(l3_v_sb, 4 if k == 2 else 3)
                        PE.matmul(ps[:, k, :], m2w1[:, e, P * k:P * k + P], h_fm[:, 0:T2], start=True, stop=True)\
                            .then_inc(up_ps, 1)

                def down(e):
                    pe.wait_ge(g_ok, 4 * e + 4)
                    if e >= 2:
                        pe.wait_ge(y_added, e - 1)
                    for j in range(4):
                        for k in range(4):
                            ins = PE.matmul(ps[:, 4 + e % 2, P * j:P * j + P], hid[:, e % 2, k, P * j:P * j + P],
                                            m2w2[:, e, k, :], start=(k == 0), stop=(k == 3))
                    ins.then_inc(y_ps, 1)

                up(0)
                for e in range(NE):
                    if e + 1 < NE:
                        up(e + 1)
                    down(e)

            @block.scalar
            def _(act):
                for e in range(NE):
                    if e >= 2:
                        act.wait_ge(y_ps, e - 1)
                    for k in range(4):
                        act.wait_ge(up_ps, 4 * e + k + 1)
                        AC.activation(hid[:, e % 2, k, :], ps[:, k, :], ACT.Gelu).then_inc(g_ok, 1)
                    beside_gelu(act, e)

        if LAST >= 6:
            @block.sync
            def _(sp):
                sp.wait_ge(x_done, 2)
                sp.dma_start(m2w1, A["moe2_w1"]).then_inc(moe2_in, 16)
                sp.dma_start(m2w2, A["moe2_w2"]).then_inc(moe2_in, 16)
                sp.dma_start(idx[:], A["moe2_idx"]).then_inc(moe2_in, 16)
                sp.dma_start(gw[:], A["moe2_gw"]).then_inc(moe2_in, 16)

            @block.gpsimd
            def _(pool):
                pool.wait_ge(x_done, 5)
                G.memset(v4[:], 0.0).then_inc(cleared, 1)

            @block.sync
            def _(sp):
                sp.wait_ge(x_done, 5)
                sp.dma_start(masks, A["attn_mask"].rearrange("(j p) k -> p j k", p=P)).then_inc(bias_in, 16)
                for b in range(2):
                    sp.dma_start(bias[S * b:S * b + S].rearrange("p (h k) -> p h k", h=H),
                                 A["attn_bias"].rearrange("h q k -> q h k")).then_inc(bias_in, 16)

            def free_after_5(eng):
                eng.wait_ge(x_done, 5)

            l3, (evacuate, guard_keys, expand_keys, guard_values, spread_values, l3_v_sb) = keys_values(
                6, "L3", "L3_xattn_W_k", "L3_xattn_W_v", "L3_xattn_b_q", "L3_xattn_b_k", "L3_xattn_b_v",
                True, l2buf[:, 0:5120], (6, 7, 3, 2), free_after_5)

            def beside_experts(dve, e):
                if e < 0:
                    for g in range(4):
                        evacuate(dve, g)
                elif e == 0:
                    guard_keys(dve)
                elif e == 1:
                    expand_keys(dve)
                elif e in (2, 3):
                    guard_values(dve, e - 2)
                elif e == 4:
                    pen = arena[:, 7680:8192].rearrange("p (j k) -> p j k", j=NT)
                    tmp = arena[:, 6144:7168]
                    dve.wait_ge(bias_in, 48)
                    V.tensor_scalar(tmp, bias, 0.0, 1e4, ALU.max, ALU.min)
                    V.tensor_scalar(seen, masks, 0, None, ALU.not_equal)
                    dve_link(V.tensor_scalar(bias, bias, 0.0, -1e4, ALU.min, ALU.max))
                    V.tensor_scalar(pen, seen, 1e4, -1e4, ALU.mult, ALU.add)
                    dve_link(V.tensor_tensor(bias, bias, tmp, ALU.add))
                    dve.wait_ge(l3[1], 1)
                if e in (5, 6, 7):
                    for j in range(3 * (e - 5), min(3 * (e - 4), NT)):
                        V.tensor_tensor(seen_bias[:, j], bias.rearrange("p (h k) -> p h k", h=H),
                                        over(seen[:, j], 1, H), ALU.mult).then_inc(bm_ready, 1)

            @block.gpsimd
            def _(pool):
                pen = arena[:, 7680:8192].rearrange("p (j k) -> p j k", j=NT)
                for j in range(NT):
                    pool.wait_ge(bm_ready, j + 1)
                    G.tensor_tensor(seen_bias[:, j], seen_bias[:, j], over(pen[:, j], 1, H), ALU.add)\
                        .then_inc(bm_done, 1)

            def beside_gelu(act, e):
                if e == 4:
                    spread_values(act)

            moe2(5, beside_experts, beside_gelu)

        if LAST >= 7:
            layernorm()
            attention(6, "L3", "L3_xattn_W_q", "L3_xattn_W_o", "L3_xattn_b_o", l3, True, bm_done)

        def ffn3(n):
            s = lambda name: sem(f"ffn3_{name}")
            col_ok, all_ps, scale_ok = s("max_cols"), s("max_all"), s("scale")
            x_ok, mm_ps, mm_sb, g_ok, u_ok, sig_ok, st_ok, p_ok, gt_ok, o_ok, y_ps = (
                s("x"), s("up_ps"), s("up_sb"), s("gate"), s("up"), s("sigmoid"), s("sigmoid_t"), s("product"),
                s("rounded"), s("out"), s("y"))
            NCH = I3 // P
            chunk = lambda v, c: v[:, 1024 * c:1024 * c + 1024]
            up = arena[:, 0:3072]
            gate = arena[:, 3072:6144]
            sig = arena[:, 6144:9216]
            cm = arena[:, 9324:9340]
            top = arena[:, 9342:9343]
            amax = arena[:, 9343:9344]
            scl = arena[:, 9344:9350]
            inv = arena[:, 9350:9356]
            real = arena[:, 9356:9362]
            magic = arena[:, 9364:9365]
            X, GT, UP, GS, OUT = range(5)
            n_max = [0]

            def half(v, k):
                return v.rearrange("p (c t) -> p c t", c=NCH)[:, :, 512 * k:512 * k + 512]

            layernorm()

            def all_max(dve, maxes, i, width=1):
                m = n_max[0]
                n_max[0] += 1
                if width > 1:
                    dve_link(V.tensor_reduce(top, maxes, AX.X, ALU.max))
                    maxes = top
                V.tensor_copy(amax, maxes).then_inc(col_ok, 1)
                dve.wait_ge(all_ps, m + 1)
                dve_link(V.tensor_reduce(top, ps[:, 7, 0:P], AX.X, ALU.max))
                if i == X:
                    dve_link(V.tensor_scalar(scl[:, i:i + 1], top, 1.0 / 32767.0, 1e-12, ALU.mult, ALU.max))
                    dve_link(V.reciprocal(inv[:, i:i + 1], scl[:, i:i + 1]))
                    return
                dve_link(V.tensor_scalar(scl[:, i:i + 1], top, real[:, i:i + 1], 1.0 / 32767.0, ALU.mult, ALU.mult))
                dve_link(V.tensor_scalar(scl[:, i:i + 1], scl[:, i:i + 1], 1e-12, None, ALU.max))
                dve_link(V.reciprocal(inv[:, i:i + 1], scl[:, i:i + 1]))
                V.tensor_tensor(inv[:, i:i + 1], inv[:, i:i + 1], real[:, i:i + 1], ALU.mult).then_inc(scale_ok, 1)
                dve.wait_ge(scale_ok, m)

            @block.tensor
            def _(pe):
                def maximum(m):
                    pe.wait_ge(col_ok, m + 1)
                    PE.matmul(ps[:, 7, 0:P], amax.broadcast_to([P, P]), ident, start=True, stop=True).then_inc(all_ps, 1)

                maximum(X)
                pe.wait_ge(x_ok, 1)
                pe.wait_ge(wT_ok, 3)
                for i, c0 in ((0, 0), (1, 3)):
                    for c in range(NCH):
                        for k in range(2):
                            m = 6 * i + 2 * c + k
                            if m >= 4:
                                pe.wait_ge(mm_sb, m - 3)
                            PE.matmul(ps[:, m % 4, :], wT[:, c0 + c, :], h_fm[:, 512 * k:512 * k + 512],
                                      start=True, stop=True).then_inc(mm_ps, 1)
                    maximum(GT + i)
                maximum(GS)
                maximum(OUT)
                for k in range(2):
                    pe.wait_ge(o_ok, k + 1)
                    for j in range(4 * k, 4 * k + 4):
                        for c in range(NCH):
                            ins = PE.matmul(ps[:, k, P * (j % 4):P * (j % 4) + P],
                                            up[:, 1024 * c + P * j:1024 * c + P * j + P], wT[:, 6 + c, :],
                                            start=(c == 0), stop=(c == NCH - 1))
                    ins.then_inc(y_ps, 1)

            @block.scalar
            def _(act):
                def evacuate(i):
                    for m in range(6 * i, 6 * i + 6):
                        act.wait_ge(mm_ps, m + 1)
                        AC.activation((gate, up)[i][:, 512 * (m % 6):512 * (m % 6) + 512], ps[:, m % 4, :], ACT.Copy)\
                            .then_inc(mm_sb, 1)

                evacuate(0)
                evacuate(1)
                for c in range(NCH):
                    act.wait_ge(g_ok, c + 1)
                    AC.activation(chunk(sig, c), chunk(gate, c), ACT.Sigmoid, scale=scl[:, GT:GT + 1]).then_inc(sig_ok, 1)
                    act.wait_ge(sig_ok, c + 1)
                    AC.activation(chunk(sig, c), chunk(sig, c), ACT.Identity, bias=magic, scale=65536.0).then_inc(st_ok, 1)
                act.wait_ge(scale_ok, GS)
                for c in range(NCH):
                    AC.activation(chunk(gate, c), chunk(gate, c), ACT.Identity, bias=magic, scale=inv[:, GS:GS + 1])\
                        .then_inc(gt_ok, 1)
                act.wait_ge(scale_ok, OUT)
                AC.activation(half(up, 1), half(up, 1), ACT.Identity, bias=magic, scale=inv[:, OUT:OUT + 1]).then_inc(gt_ok, 1)

            @block.vector
            def _(dve):
                V.memset(magic, MAGIC)
                wait_h_tm(dve)
                dve_link(V.tensor_reduce(cm[:, 0:1], h_tm[:].rearrange("p j d -> p (j d)"), AX.X, ALU.max,
                                         apply_absolute_value=True))
                all_max(dve, cm[:, 0:1], X)
                wait_h_fm(dve)
                for k in range(2):
                    v = h_fm[:, 512 * k:512 * k + 512]
                    dve_link(V.tensor_scalar(v, v, inv[:, X:X + 1], MAGIC, ALU.mult, ALU.add))
                    ins = V.tensor_scalar(v, v, -MAGIC, None, ALU.add)
                ins.then_inc(x_ok, 1)
                for i in (GT, UP):
                    ins = V.tensor_copy(real[:, i:i + 1], scl[:, X:X + 1])
                dve_link(ins)

                def maxima(i):
                    for c in range(6):
                        dve.wait_ge(mm_sb, 6 * i + c + 1)
                        ins = V.tensor_reduce(cm[:, c:c + 1], (gate, up)[i][:, 512 * c:512 * c + 512], AX.X, ALU.max,
                                              apply_absolute_value=True)
                    dve_link(ins)
                    all_max(dve, cm[:, 0:6], GT + i, 6)

                def to_integers(v, i, done):
                    for c in range(NCH):
                        dve_link(V.tensor_scalar(chunk(v, c), chunk(v, c), inv[:, i:i + 1], MAGIC, ALU.mult, ALU.add))
                        V.tensor_scalar(chunk(v, c), chunk(v, c), -MAGIC, None, ALU.add).then_inc(done, 1)

                maxima(0)
                to_integers(gate, GT, g_ok)
                V.tensor_scalar(real[:, GS:GS + 1], scl[:, GT:GT + 1], 1.0 / 65536.0, None, ALU.mult)
                maxima(1)
                to_integers(up, UP, u_ok)
                for c in range(NCH):
                    dve.wait_ge(st_ok, c + 1)
                    dve_link(V.tensor_scalar(chunk(sig, c), chunk(sig, c), -MAGIC, 65535.0, ALU.add, ALU.min))
                    dve_link(V.tensor_tensor(chunk(gate, c), chunk(gate, c), chunk(sig, c), ALU.mult))
                    ins = V.tensor_reduce(cm[:, c:c + 1], chunk(gate, c), AX.X, ALU.max, apply_absolute_value=True)
                dve_link(ins)
                all_max(dve, cm[:, 0:NCH], GS, NCH)
                V.tensor_tensor(real[:, OUT:OUT + 1], scl[:, GS:GS + 1], scl[:, UP:UP + 1], ALU.mult)
                dve.wait_ge(u_ok, NCH)
                for c in range(NCH):
                    dve.wait_ge(gt_ok, c + 1)
                    dve_link(V.scalar_tensor_tensor(out=chunk(up, c), in0=chunk(gate, c), scalar=-MAGIC, in1=chunk(up, c),
                                                    op0=ALU.add, op1=ALU.mult))
                    ins = V.tensor_reduce(cm[:, c:c + 1], chunk(up, c), AX.X, ALU.max, apply_absolute_value=True)
                dve_link(ins)
                all_max(dve, cm[:, 0:NCH], OUT, NCH)
                dve_link(V.tensor_scalar(half(up, 0), half(up, 0), inv[:, OUT:OUT + 1], MAGIC, ALU.mult, ALU.add))
                V.tensor_scalar(half(up, 0), half(up, 0), -MAGIC, None, ALU.add).then_inc(o_ok, 1)
                dve.wait_ge(gt_ok, NCH + 1)
                V.tensor_scalar(half(up, 1), half(up, 1), -MAGIC, None, ALU.add).then_inc(o_ok, 1)
                for k in range(2):
                    dve.wait_ge(y_ps, k + 1)
                    V.scalar_tensor_tensor(out=x_tm[:, 4 * k:4 * k + 4], in0=ps[:, k, :].rearrange("p (j d) -> p j d", j=4),
                                           scalar=scl[:, OUT:OUT + 1], in1=x_tm[:, 4 * k:4 * k + 4],
                                           op0=ALU.mult, op1=ALU.add).then_inc(halves_done, 1)
                dve.wait_ge(halves_done, 2)
                V.sem_inc(x_done, 1)

        if LAST >= 8:
            ffn3(7)

        out_done = sem("out_done")

        @block.sync
        def _(sp):
            if LAST < 8:
                sp.wait_ge(x_done, LAST)
                sp.sem_inc(halves_done, 2)
                for sm_, n_ in ((ctxt_in, 16), (moe0_in, 96), (mats_in, 32)):
                    sp.wait_ge(sm_, n_)
            for k in range(2):
                sp.wait_ge(halves_done, k + 1)
                sp.dma_start(out.rearrange("(j p) d -> p j d", p=P)[:, 4 * k:4 * k + 4], x_tm[:, 4 * k:4 * k + 4])\
                    .then_inc(out_done, 16)
            sp.wait_ge(out_done, 32)


def kernel(**inputs):
    import concourse.bacc as _bacc
    from concourse.bass_utils import run_bass_kernel_spmd as _run

    a = {k: np.asarray(v) for k, v in inputs.items()}

    def T_(m):
        return np.ascontiguousarray(m.T)

    def split(w, k):
        e, f, n = w.shape
        w = w.reshape(e, k, f // k, n).transpose(2, 0, 1, 3)
        return np.ascontiguousarray(w.reshape(f // k, e, n) if k == 1 else w)

    experts = {i: np.concatenate([a[f"L0_ffn_rw{i}"], a[f"L0_ffn_sw{i}"]]) for i in (1, 2, 3)}
    biases = {i: np.concatenate([a[f"L0_ffn_rb{i}"], a[f"L0_ffn_sb{i}"]]) for i in (1, 2, 3)}
    woff = np.zeros((P, 2, S), np.float32)
    boff = np.zeros((2, S, 2), np.float32)
    for g in range(2):
        woff[:, g, :40] = a["L2_xattn_Woff"][40 * g:40 * g + 40].T
        boff[:, :40, g] = a["L2_xattn_boff"][40 * g:40 * g + 40]
    cols = np.concatenate(
        [np.stack([a[n] for n in COLS], 1)]
        + [biases[i].reshape(NQ, 2, P).transpose(2, 0, 1).reshape(P, 2 * NQ) for i in (1, 2)]
        + [boff.reshape(P, 2)], 1)
    send = {
        "x": a["x"].reshape(T, D),
        "ctx": a["ctx_1024"].reshape(T, D),
        "ctx_fm": T_(a["ctx_1024"].reshape(T, D)),
        "const": shape_constants(), "picks": row_picks(),
        "rows": np.stack([a[n] for n in ROWS]),
        "cols": cols,
        "mats": np.ascontiguousarray(np.stack([a[n].T for n in MATS], 1)),
        "woff": woff,
        "moe0_w1": split(experts[1], 1), "moe0_w2": split(experts[2], 1), "moe0_w3": split(experts[3], 2),
        "moe0_b3": biases[3],
        "gate_w": a["L0_ffn_gate_w"], "gate_b": a["L0_ffn_gate_b"],
        "mask": a["mask_BxS2_if0"],
        "attn_bias": a["fside_1x16xSxS2_0"][0],
        "attn_mask": a["mask_Bx1xSxS2_ik1"].reshape(T, S),
        "wq8": T_(a["L1_ffn_weight_q"]).astype(np.int32),
        "moe2_w1": split(a["L2_ffn_w1"], 1), "moe2_w2": split(a["L2_ffn_w2"], 4),
        "moe2_idx": np.ascontiguousarray(a["L2_ffn_expert_indices"].reshape(4, P, 2).transpose(1, 0, 2)),
        "moe2_gw": np.ascontiguousarray(a["L2_ffn_expert_weights"].reshape(4, P, 2).transpose(1, 0, 2)),
        "w_gate": a["L3_ffn_w_gate"], "w_up": a["L3_ffn_w_up"], "w_down": a["L3_ffn_w_down"],
    }
    nc = _bacc.Bacc("TRN2", target_bir_lowering=False, num_devices=1)
    arrays, A = {}, {}
    for name, v in send.items():
        v = np.ascontiguousarray(v)
        arrays[f"in_{name}"] = v
        A[name] = nc.dram_tensor(f"in_{name}", v.shape, mybir.dt.from_np(v.dtype), kind="ExternalInput").ap()
    out = nc.dram_tensor("out_x", (T, D), F32, kind="ExternalOutput").ap()
    build(nc, A, out)
    r = _run(nc, [arrays], core_ids=[0])
    return r.results[0]["out_x"].reshape(B, S, D)
```

```python
from contextlib import ExitStack

import numpy as np

import concourse.bass as bass
from concourse import mybir

P = 128
B, S, D = 16, 64, 128
T = B * S
NT = T // P
H, HD = 16, 8
NK = 5
NE, NSH, TOPK, FH = 8, 2, 2, 256
T2 = 512
I3 = 384
EPS = 1e-5
MAGIC = 12582912.0
F32 = mybir.dt.float32
BF16 = mybir.dt.bfloat16
I32 = mybir.dt.int32
ALU = mybir.AluOpType
ACT = mybir.ActivationFunctionType
AX = mybir.AxisListType

ROWS = ["L0_xattn_bv", "L0_xattn_bo", "L1_xattn_wqg", "L1_xattn_wql", "L1_xattn_bqg", "L1_xattn_bql",
        "L1_xattn_wkg", "L1_xattn_wkl", "L1_xattn_bkg", "L1_xattn_bkl", "L1_xattn_wp", "L1_xattn_bp",
        "L1_ffn_weight_scale", "L1_ffn_bias", "L2_xattn_bk", "L2_xattn_bv", "L2_xattn_bo",
        "L2_xattn_bq", "L2_ffn_bias", "L3_xattn_b_v", "L3_xattn_b_o"]
COLS = ["L0_xattn_bq", "L0_xattn_bk", "L1_xattn_wvg", "L1_xattn_bvg", "L1_xattn_wvl", "L1_xattn_bvl",
        "L2_xattn_bq", "L3_xattn_b_q", "L3_xattn_b_k"]
NC_EXP = len(COLS)
MATS = ["L0_xattn_Wq", "L0_xattn_Wk", "L0_xattn_Wv", "L0_xattn_Wo",
        "L2_xattn_Wk", "L2_xattn_Wv", "L2_xattn_Wq", "L2_xattn_Wo",
        "L3_xattn_W_q", "L3_xattn_W_k", "L3_xattn_W_v", "L3_xattn_W_o"]
NQ = NE + NSH

C_ID = 0
C_HM = C_ID + P
C_NEGM = C_HM + 4
C_REF = C_NEGM + 1
C_IOTA = C_REF + S
C_ONES = C_IOTA + NE
C_END = C_ONES + 64


def shape_constants():
    c = np.zeros((P, C_END), np.float32)
    p = np.arange(P)
    c[p, C_ID + p] = 1.0
    for h in range(4):
        c[:, C_HM + h] = (p // HD) % 4 == h
    c[:, C_NEGM] = -(p % S)
    c[:, C_REF:C_REF + S] = ((p % S) % NK - 3)[:, None] + np.arange(S)[None, :]
    c[:, C_IOTA:C_IOTA + NE] = np.arange(NE)
    ones = c[:, C_ONES:C_ONES + 64].reshape(P, 2, 4, HD)
    for par in range(2):
        for h2 in range(2):
            ones[S * h2:S * h2 + S, par, 2 * par + h2] = 1.0
    c[:, C_ONES:C_ONES + 64] = ones.reshape(P, 64)
    return c


def row_picks():
    c = np.zeros((P, 26, P), np.float32)
    for b in range(2):
        for r in range(20):
            for part in range(3):
                c[S * b + 20 * part + r, r, S * b:S * b + S] = 1.0
                for g in range(2):
                    c[S * b + 20 * g + r, 20 + 3 * g + part, S * b + 20 * part + r] = 1.0
    return c.reshape(P, 26 * P)


def over(ap, axis, n):
    wide = ap.unsqueeze(axis)
    shape = list(wide.shape)
    shape[axis] = n
    return wide.broadcast_to(shape)


def build(nc, A, out):
    ctx = ExitStack()
    with ctx:
        def sb(name, shape, dt=F32):
            return ctx.enter_context(nc.sbuf_tensor(name, shape, dt))

        def sem(name):
            return ctx.enter_context(nc.semaphore(name))

        V, G, PE, AC = nc.vector, nc.gpsimd, nc.tensor, nc.scalar

        const = sb("const", [P, C_END])
        rows = sb("rows", [P, len(ROWS), D])
        cols = sb("cols", [P, NC_EXP + 4 * NQ + 2])
        mats = sb("mats", [P, len(MATS), D])
        woff = sb("woff", [P, 2, S])
        x_tm = sb("x_tm", [P, NT, D])
        h_tm = sb("h_tm", [P, NT, D])
        h_fm = sb("h_fm", [P, T])
        ctx_fm = sb("ctx_fm", [P, T])
        ctx_tm = sb("ctx_tm", [P, NT, D])
        stats = sb("stats", [P, NT, 6])
        mv = sb("mv", [P, NT, 2])
        rstd = sb("rstd", [P, NT])
        kexp = sb("kexp", [P, B * 4 * S])
        v4 = sb("v4", [P, B * 8 * 32])
        arena = sb("arena", [P, 10240])
        weights = sb("weights", [P, 8192])

        ps = ctx.enter_context(nc.psum_tensor("ps", [P, 8, 512], F32))

        def row(name):
            return rows[:, ROWS.index(name), :]

        def col(name):
            i = COLS.index(name)
            return cols[:, i:i + 1]

        def mat(name):
            return mats[:, MATS.index(name), :]

        ident = const[:, C_ID:C_ID + P]

        dve_chain, pool_chain = sem("dve_chain"), sem("pool_chain")
        chained = {"dve": 0, "pool": 0}

        def dve_link(ins):
            chained["dve"] += 1
            ins.then_inc(dve_chain, 1)
            V.wait_ge(dve_chain, chained["dve"])

        def dve_mark(ins):
            chained["dve"] += 1
            ins.then_inc(dve_chain, 1)
            return chained["dve"]

        def pool_link(ins):
            chained["pool"] += 1
            ins.then_inc(pool_chain, 1)
            G.wait_ge(pool_chain, chained["pool"])

        x_in, const_in, ctxf_in, ctxt_in = sem("x_in"), sem("const_in"), sem("ctxf_in"), sem("ctxt_in")
        rows_in, cols_in, mats_in = sem("rows_in"), sem("cols_in"), sem("mats_in")
        moe0_in = sem("moe0_in")
        x_done = sem("x_done")
        hf_ready = sem("hf_ready")
        b3 = sb("b3", [NQ, D])
        gate_w = sb("gate_w", [P, NE])
        gate_b = sb("gate_b", [P, NE])
        w1 = weights[:, 0:NQ * FH].rearrange("p (e h) -> p e h", e=NQ)
        w2 = weights[:, NQ * FH:2 * NQ * FH].rearrange("p (e h) -> p e h", e=NQ)
        w3 = weights[:, 2 * NQ * FH:3 * NQ * FH].rearrange("p (e k d) -> p e k d", e=NQ, k=2)

        block = ctx.enter_context(nc.Block())

        first_mats = 4
        mats0_in = sem("mats0_in")

        @block.sync
        def _(sp):
            sp.dma_start(mats[:, 0:first_mats], A["mats"][:, 0:first_mats]).then_inc(mats0_in, 16)
            sp.dma_start(x_tm[:], A["x"].rearrange("(j p) d -> p j d", p=P)).then_inc(x_in, 16)
            sp.dma_start(const[:], A["const"]).then_inc(const_in, 16)
            sp.dma_start(w1, A["moe0_w1"]).then_inc(moe0_in, 16)
            sp.dma_start(w2, A["moe0_w2"]).then_inc(moe0_in, 16)
            sp.dma_start(w3, A["moe0_w3"]).then_inc(moe0_in, 16)
            sp.dma_start(b3[:], A["moe0_b3"]).then_inc(moe0_in, 16)
            sp.dma_start(gate_w[:], A["gate_w"]).then_inc(moe0_in, 16)
            sp.dma_start(gate_b[:], A["gate_b"].partition_broadcast(P)).then_inc(moe0_in, 16)
            sp.dma_start(mats[:, first_mats:], A["mats"][:, first_mats:]).then_inc(mats_in, 16)
            sp.dma_start(woff[:], A["woff"]).then_inc(mats_in, 16)

        @block.scalar
        def _(act):
            act.dma_start(ctx_fm[:], A["ctx_fm"]).then_inc(ctxf_in, 16)
            act.dma_start(cols[:], A["cols"]).then_inc(cols_in, 16)
            act.dma_start(rows[:], A["rows"].partition_broadcast(P)).then_inc(rows_in, 16)
            act.dma_start(ctx_tm[:], A["ctx"].rearrange("(j p) d -> p j d", p=P)).then_inc(ctxt_in, 16)

        cleared = sem("cleared")
        V4_CLEAR, KV_CLEAR, AB_CLEAR, V4_CLEAR_AGAIN = 1, 2, 3, 4

        @block.gpsimd
        def _(pool):
            G.memset(v4[:], 0.0).then_inc(cleared, 1)

        n_sub, n_fm = [0], [0]
        stat_ready, std_ready, tr_ready = sem("var"), sem("std"), sem("hT")
        shift_ready, h_first, h_rest = sem("shift"), sem("h_first"), sem("h_rest")
        shift = sb("shift", [P, NT])
        ON_DVE = 5

        def tile_stats(j):
            return V.bn_stats(stats[:, j, :], x_tm[:, j, :])

        def layernorm(feature_major=True):
            n = n_sub[0]
            n_sub[0] += 1
            nf = n_fm[0]

            @block.vector
            def _(dve):
                if n == 0:
                    dve.wait_ge(x_in, 16)
                    for j in range(NT):
                        ins = tile_stats(j)
                    dve_link(ins)
                for j in range(NT):
                    ins = V.bn_aggr(mv[:, j, :], stats[:, j, :])
                dve_link(ins)
                V.tensor_scalar(rstd[:], mv[:, :, 1], EPS, None, ALU.add).then_inc(stat_ready, 1)
                dve.wait_ge(std_ready, n + 1)
                dve_link(V.reciprocal(rstd[:], rstd[:]))
                V.scalar_tensor_tensor(out=shift[:], in0=mv[:, :, 0], scalar=-1.0, in1=rstd[:],
                                       op0=ALU.mult, op1=ALU.mult).then_inc(shift_ready, 1)
                for j in range(ON_DVE):
                    ins = V.tensor_scalar(h_tm[:, j, :], x_tm[:, j, :], mv[:, j, 0:1], rstd[:, j:j + 1],
                                          ALU.subtract, ALU.mult)
                    if j == 3:
                        ins.then_inc(h_first, 1)
                ins.then_inc(h_rest, 1)

            @block.scalar
            def _(act):
                act.wait_ge(stat_ready, n + 1)
                AC.activation(rstd[:], rstd[:], ACT.Sqrt).then_inc(std_ready, 1)
                act.wait_ge(shift_ready, n + 1)
                for j in range(ON_DVE, NT):
                    ins = AC.activation(h_tm[:, j, :], x_tm[:, j, :], ACT.Identity, bias=shift[:, j:j + 1],
                                        scale=rstd[:, j:j + 1])
                ins.then_inc(h_rest, 1)
                if feature_major:
                    for k in range(2):
                        act.wait_ge(tr_ready, 2 * nf + k + 1)
                        AC.activation(h_fm[:, 512 * k:512 * k + 512], ps[:, 4 + k, :], ACT.Copy)\
                            .then_inc(hf_ready, 1)

            if feature_major:
                @block.tensor
                def _(pe):
                    if n == 0:
                        pe.wait_ge(const_in, 16)
                    for k in range(2):
                        if k == 0:
                            pe.wait_ge(h_first, n + 1)
                        else:
                            pe.wait_ge(h_rest, 2 * n + 2)
                        for j in range(4):
                            ins = PE.transpose(ps[:, 4 + k, 128 * j:128 * j + 128], h_tm[:, 4 * k + j, :], ident)
                        ins.then_inc(tr_ready, 1)
                n_fm[0] += 1

        def all_stats(tiles=range(NT)):
            for j in tiles:
                ins = tile_stats(j)
            dve_link(ins)

        def wait_h_tm(eng):
            eng.wait_ge(h_first, n_sub[0])
            eng.wait_ge(h_rest, 2 * n_sub[0])

        def wait_h_fm(eng, half=1):
            eng.wait_ge(hf_ready, 2 * n_fm[0] - 1 + half)

        k_fm = sb("k_fm", [P, T])
        q_fm = sb("q_fm", [P, T])
        o_fm = sb("o_fm", [P, T])

        SCALE = 1.0 / float(np.sqrt(np.float32(HD)))
        kx = kexp[:].rearrange("p (b h k) -> p b h k", b=B, h=4)
        vx = v4[:].rearrange("p (b c m) -> p b c m", b=B, c=8)
        l2buf = sb("l2buf", [P, 8192])
        bqs = sb("bqs", [P, 2])
        bias = arena[:, 8192:9216]
        masks = arena[:, 9216:9728].bitcast(I32).rearrange("p (j k) -> p j k", j=NT)
        seen = arena[:, 9728:10240].rearrange("p (j k) -> p j k", j=NT)
        seen_scale = arena[:, 7168:7680].rearrange("p (j k) -> p j k", j=NT)
        seen_bias = l2buf[:].rearrange("p (j h k) -> p j h k", j=NT, h=H)

        def keys_values(n, layer, wk, wv, bq, bk, bv, masked, work, banks, ready, before_dve=None, keys=None):
            s = lambda name: sem(f"{layer}_{name}")
            k_ps, k_sb = keys or (s("k_ps"), s("k_sb"))
            kx_ready = s("kx")
            v_ps, v_sb, vx_ready, bq_ok = s("v_ps"), s("v_sb"), s("vx"), s("bq")
            vdup = work[:, 0:2048].rearrange("p (i b e) -> p i b e", i=4, b=4)
            nb = len(banks)

            def guard(t, width, scratch):
                tmp, tmp2, nonf = scratch[:, 0:1024], scratch[:, 1024:2048], scratch[:, 2048:3072].bitcast(I32)
                step = min(width, 1024)
                tmp, tmp2, nonf = tmp[:, 0:step], tmp2[:, 0:step], nonf[:, 0:step]
                for at in range(0, width, step):
                    v = t[:, at:at + step]
                    V.tensor_scalar(nonf, v, 0.0, 0.0, ALU.mult, ALU.not_equal)
                    V.tensor_scalar(tmp, v, 0.0, 1e4, ALU.max, ALU.min)
                    dve_link(V.tensor_scalar(tmp2, v, 0.0, -1e4, ALU.min, ALU.max))
                    dve_link(V.tensor_tensor(tmp, tmp, tmp2, ALU.add))
                    dve_link(V.copy_predicated(v, nonf, tmp))

            def expand_keys(dve):
                dve.wait_ge(k_sb, 2)
                for k in range(2):
                    src = over(k_fm[:, 512 * k:512 * k + 512].rearrange("p (b k) -> p b k", b=8), 2, 4)
                    hm = over(over(const[:, C_HM:C_HM + 4], 2, S), 1, 8)
                    ins = V.tensor_tensor(kx[:, 8 * k:8 * k + 8], src, hm, ALU.mult)
                ins.then_inc(kx_ready, 1)

            def evacuate(dve, g):
                dve.wait_ge(rows_in, 16)
                dve.wait_ge(v_ps, g + 1)
                V.tensor_tensor(vdup[:, g], ps[:, banks[g % nb], :].rearrange("p (b e) -> p b e", b=4),
                                over(row(bv), 1, 4), ALU.add).then_inc(v_sb, 1)

            def guard_values(dve, half):
                dve.wait_ge(v_sb, 4)
                guard(vdup[:, 2 * half:2 * half + 2].rearrange("p i b e -> p (i b e)"), 1024, work[:, 2048:5120])
                if half == 1:
                    V.sem_inc(v_sb, 1)

            def guard_keys(dve):
                dve.wait_ge(k_sb, 2)
                guard(k_fm[:], T, work[:, 2048:5120])

            def spread_values(act, parts=range(4)):
                act.wait_ge(v_sb, 5 if masked else 4)
                act.wait_ge(cleared, V4_CLEAR_AGAIN if masked else V4_CLEAR)
                for part in parts:
                    h2, par = part // 2, part % 2
                    r = slice(64 * h2, 64 * h2 + 64)
                    c0 = (par * 2 + h2) * HD
                    for g in range(4):
                        src = vdup[r, g].rearrange("p b (c h d) -> p b c h d", c=4, h=4)[:, :, :, par * 2 + h2, :]
                        dst = vx[r, 4 * g:4 * g + 4].rearrange("p b (c t) m -> p b c t m", t=2)[:, :, :, par, c0:c0 + HD]
                        ins = AC.activation(dst, src, ACT.Copy)
                    ins.then_inc(vx_ready, 1)

            @block.tensor
            def _(pe):
                ready(pe)
                if layer == "L0":
                    pe.wait_ge(ctxf_in, 16)
                    pe.wait_ge(mats0_in, 16)
                else:
                    pe.wait_ge(mats_in, 32)
                for k in range(0 if keys else 2):
                    PE.matmul(ps[:, 6 + k, :], mat(wk), ctx_fm[:, 512 * k:512 * k + 512],
                              start=True, stop=True).then_inc(k_ps, 1)
                if not keys:
                    pe.wait_ge(k_sb, 2)
                for g in range(4):
                    if g >= nb:
                        pe.wait_ge(v_sb, g - nb + 1)
                    for b in range(4):
                        for h2 in range(2):
                            ins = PE.matmul(ps[64 * h2:64 * h2 + 64, banks[g % nb], 128 * b:128 * b + 128],
                                            ctx_fm[:, (4 * g + b) * S:(4 * g + b + 1) * S], mat(wv),
                                            start=True, stop=True)
                    ins.then_inc(v_ps, 1)

            @block.scalar
            def _(act):
                ready(act)
                act.wait_ge(cols_in, 16)
                for k in range(0 if keys else 2):
                    act.wait_ge(k_ps, k + 1)
                    AC.activation(k_fm[:, 512 * k:512 * k + 512], ps[:, 6 + k, :], ACT.Identity,
                                  bias=col(bk)).then_inc(k_sb, 1)
            if before_dve is not None:
                before_dve()
            if not masked:
                block.scalar(spread_values)

            @block.vector
            def _(dve):
                ready(dve)
                dve.wait_ge(const_in, 16)
                dve.wait_ge(cols_in, 16)
                V.tensor_scalar(bqs[:, int(masked):int(masked) + 1], col(bq), 1.0 if masked else SCALE, None,
                                ALU.mult).then_inc(bq_ok, 1)
                if not masked:
                    expand_keys(dve)
                    for g in range(4):
                        evacuate(dve, g)

            if masked:
                return (kx_ready, vx_ready, bq_ok, guard), (evacuate, guard_keys, expand_keys, guard_values, spread_values, v_sb)
            return kx_ready, vx_ready, bq_ok, guard

        def attention(n, layer, wq, wo, bo, prepared, masked, bm_ready=None):
            kx_ready, vx_ready, bq_ok, guard = prepared
            s = lambda name: sem(f"{layer}_{name}")
            prob = [arena[:, 1024 * i:1024 * i + 1024] for i in range(3)]
            pT = [arena[:, 3072 + 1024 * i:4096 + 1024 * i] for i in range(2)]
            mx = arena[:, 6144:6144 + 32].rearrange("p (i h) -> p i h", i=2)
            rb = arena[:, 6208:6208 + 128]
            ones = const[:, C_ONES:C_ONES + 64].rearrange("p (t m) -> p t m", t=2)
            q_ps, q_sb = s("q_ps"), s("q_sb")
            q_ok, mx_ready, clean = (s("q_ok"), s("max"), s("clean")) if masked else (None, None, None)
            sc_ready, sc_read, sub_ready, exp_ready = s("scores"), s("scores_read"), s("less_max"), s("exp")
            ptT_ready, pt_ready = s("probsT"), s("probsT_sb")
            o_ready, rb_ready = s("o_ps"), s("sums")
            of_ready, y_ready, y_added = s("o_fm"), s("y"), s("y_added")

            @block.tensor
            def _(pe):
                if layer == "L3":
                    pe.wait_ge(x_done, n)
                for k in range(2):
                    wait_h_fm(pe, k if masked else 1)
                    PE.matmul(ps[:, 6 + k, :], mat(wq), h_fm[:, 512 * k:512 * k + 512],
                              start=True, stop=True).then_inc(q_ps, 1)

            @block.scalar
            def _(act):
                act.wait_ge(bq_ok, 1)
                for k in range(2):
                    act.wait_ge(q_ps, k + 1)
                    AC.activation(q_fm[:, 512 * k:512 * k + 512], ps[:, 6 + k, :], ACT.Identity,
                                  bias=bqs[:, int(masked):int(masked) + 1], scale=1.0 if masked else SCALE)\
                        .then_inc(q_sb, 1)

            @block.vector
            def _(dve):
                if masked:
                    for k in range(2):
                        dve.wait_ge(q_sb, k + 1)
                        guard(q_fm[:, 512 * k:512 * k + 512], 512, arena[:, 0:3072])
                        V.sem_inc(q_ok, 1)
                else:
                    wait_h_tm(dve)
                    dve.wait_ge(rows_in, 16)
                    dve_link(V.tensor_tensor(x_tm[:], x_tm[:], over(row(bo), 1, NT), ALU.add))

            @block.tensor
            def _(pe):
                pe.wait_ge(q_ok if masked else q_sb, 1 if masked else 2)
                pe.wait_ge(kx_ready, 1)

                def scores(t):
                    if masked and t == NT // 2:
                        pe.wait_ge(q_ok, 2)
                    for g in range(4):
                        if t >= 2 and g < 2:
                            pe.wait_ge(sc_read, 2 * (t - 2) + g + 1)
                        if g >= 2:
                            pe.wait_ge(sc_ready, 4 * t + g - 1)
                        for b in range(2):
                            ins = PE.matmul(ps[64 * b:64 * b + 64, 2 * (t % 2) + g % 2, 256 * (g // 2):256 * (g // 2) + 256],
                                            q_fm[32 * g:32 * g + 32, t * P + 64 * b:t * P + 64 * b + 64],
                                            kx[32 * g:32 * g + 32, 2 * t + b].rearrange("p h k -> p (h k)"),
                                            start=True, stop=True)
                        ins.then_inc(sc_ready, 1)

                def transposes(j):
                    pe.wait_ge(clean if masked else exp_ready, j + 1)
                    for k in range(2):
                        if j >= 1:
                            pe.wait_ge(pt_ready, 2 * (j - 1) + k + 1)
                        for c in range(4):
                            ins = PE.transpose(ps[:, 4 + k, 128 * c:128 * c + 128],
                                               prob[j % 3][:, (4 * k + c) * 128:(4 * k + c + 1) * 128], ident)
                        ins.then_inc(ptT_ready, 1)

                def weigh_values(j):
                    pe.wait_ge(pt_ready, 2 * j + 2)
                    if j == 0:
                        pe.wait_ge(vx_ready, 4)
                    else:
                        pe.wait_ge(of_ready, j)
                    for b in range(2):
                        for c in range(8):
                            g = c // 2
                            PE.matmul(ps[32 * g:32 * g + 32, 6, 64 * b:64 * b + 64], vx[:, 2 * j + b, c, :],
                                      pT[j % 2][:, 128 * c + 64 * b:128 * c + 64 * b + 64],
                                      start=(c % 2 == 0), stop=(c % 2 == 1))
                    for c in range(8):
                        ins = PE.matmul(ps[32 * (c // 2):32 * (c // 2) + 32, 6, 128:256], ones[:, c % 2, :],
                                        pT[j % 2][:, 128 * c:128 * c + 128], start=(c % 2 == 0), stop=(c % 2 == 1))
                    ins.then_inc(o_ready, 1)

                scores(0)
                for t in range(NT + 3):
                    if t + 1 < NT:
                        scores(t + 1)
                    if 0 <= t - 1 < NT and not masked:
                        transposes(t - 1)
                    if 0 <= t - 2 < NT:
                        weigh_values(t - 2)
                    if 0 <= t - 1 < NT and masked:
                        transposes(t - 1)
                    if 0 <= t - 3 < NT:
                        j = t - 3
                        pe.wait_ge(of_ready, j + 1)
                        if j >= 1:
                            pe.wait_ge(y_added, j)
                        PE.matmul(ps[:, 7, 0:128], o_fm[:, j * P:j * P + P], mat(wo), start=True, stop=True)\
                            .then_inc(y_ready, 1)

            @block.scalar
            def _(act):
                for t in range(NT + 2):
                    if t < NT:
                        act.wait_ge(sub_ready, t + 1)
                        AC.activation(prob[t % 3], prob[t % 3], ACT.Exp).then_inc(exp_ready, 1)
                    if 0 <= t - 1 < NT:
                        j = t - 1
                        if j >= 2:
                            act.wait_ge(o_ready, j - 1)
                        for k in range(2):
                            act.wait_ge(ptT_ready, 2 * j + k + 1)
                            AC.activation(pT[j % 2][:, 512 * k:512 * k + 512], ps[:, 4 + k, :], ACT.Copy)\
                                .then_inc(pt_ready, 1)

            if masked:
                @block.gpsimd
                def _(pool):
                    wait_h_tm(pool)
                    pool.wait_ge(rows_in, 16)
                    pool_link(G.tensor_tensor(x_tm[:], x_tm[:], over(row(bo), 1, NT), ALU.add))
                    for j in range(NT):
                        pool.wait_ge(mx_ready, j + 1)
                        pr3 = prob[j % 3].rearrange("p (h k) -> p h k", h=H)
                        G.tensor_tensor(pr3, pr3, over(mx[:, j % 2], 2, S), ALU.subtract).then_inc(sub_ready, 1)

            @block.vector
            def _(dve):
                if masked:
                    dve.wait_ge(bm_ready, NT)
                for t in range(NT + 5):
                    if t < NT:
                        pr = prob[t % 3].rearrange("p (g h k) -> p g h k", g=4, h=4)
                        pr3 = prob[t % 3].rearrange("p (h k) -> p h k", h=H)
                        if t >= 3:
                            dve.wait_ge(ptT_ready, 2 * (t - 2))
                        sc = [ps[:, 2 * (t % 2) + g].rearrange("p (g h k) -> p g h k", g=2, h=4) for g in range(2)]
                        mx4 = mx[:, 0].rearrange("p (g h) -> p g h", g=4)
                        if masked:
                            for g in range(2):
                                dve.wait_ge(sc_ready, 4 * t + g + 3)
                                V.tensor_tensor(pr[:, g::2], sc[g], over(over(seen_scale[:, t], 1, 4), 1, 2), ALU.mult)\
                                    .then_inc(sc_read, 1)
                            dve.wait_ge(sc_read, 2 * t + 2)
                            dve_link(V.tensor_tensor(pr3, pr3, seen_bias[:, t], ALU.add))
                            if t >= 2:
                                dve.wait_ge(sub_ready, t - 1)
                            V.tensor_reduce(mx[:, t % 2], pr3, AX.X, ALU.max).then_inc(mx_ready, 1)
                        else:
                            marks = []
                            for g in range(2):
                                dve.wait_ge(sc_ready, 4 * t + g + 3)
                                if g == 0 and t >= 1:
                                    dve.wait_ge(sc_read, 2 * t)
                                marks.append(dve_mark(V.tensor_reduce(mx4[:, g::2], sc[g], AX.X, ALU.max)))
                            for g in range(2):
                                dve.wait_ge(dve_chain, marks[g])
                                V.tensor_tensor(pr[:, g::2], sc[g], over(mx4[:, g::2], 3, S), ALU.subtract)\
                                    .then_inc(sc_read, 1)
                            dve.wait_ge(sc_read, 2 * t + 2)
                            V.sem_inc(sub_ready, 1)
                    if 0 <= t - 1 < NT and masked:
                        j = t - 1
                        dve.wait_ge(exp_ready, j + 1)
                        V.tensor_scalar(prob[j % 3], prob[j % 3], 0.0, None, ALU.max).then_inc(clean, 1)
                    if 0 <= t - 3 < NT:
                        j = t - 3
                        dve.wait_ge(o_ready, j + 1)
                        if masked:
                            dve_link(V.tensor_scalar(rb, ps[:, 6, 128:256], 1.0, None, ALU.max))
                            V.reciprocal(rb, rb).then_inc(rb_ready, 1)
                        else:
                            V.reciprocal(rb, ps[:, 6, 128:256]).then_inc(rb_ready, 1)
                        dve.wait_ge(rb_ready, j + 1)
                        V.tensor_tensor(o_fm[:, j * P:j * P + P], ps[:, 6, 0:128], rb, ALU.mult).then_inc(of_ready, 1)
                    if 0 <= t - 4 < NT:
                        j = t - 4
                        dve.wait_ge(y_ready, j + 1)
                        V.tensor_tensor(x_tm[:, j], x_tm[:, j], ps[:, 7, 0:128], ALU.add).then_inc(y_added, 1)
                    if 0 <= t - 5 < NT:
                        dve.wait_ge(y_added, t - 4)
                        ins = tile_stats(t - 5)
                dve_link(ins)
                V.sem_inc(x_done, 1)

        l0 = keys_values(0, "L0", "L0_xattn_Wk", "L0_xattn_Wv", "L0_xattn_bq", "L0_xattn_bk", "L0_xattn_bv",
                         False, arena[:, 0:5120], (0, 1, 2, 3), lambda eng: None, layernorm)
        attention(0, "L0", "L0_xattn_Wq", "L0_xattn_Wo", "L0_xattn_bo", l0, False)
        def moe0(n):
            s = lambda name: sem(f"moe0_{name}")
            lg_ps, gates_ok, gT_ps, gT_ok = s("logits"), s("gates"), s("gatesT"), s("gatesT_sb")
            shifted, powered = s("less_max"), s("exp")
            by_ps = s("bias_ps")
            up_ps, silu_ok, glu_ok, y_ps, y_added = s("up_ps"), s("silu"), s("glu"), s("y_ps"), s("y_added")
            lin_ps = s("lin_ps")
            lg = arena[:, 0:64].rearrange("p (j e) -> p j e", j=NT)
            pr = arena[:, 64:128].rearrange("p (j e) -> p j e", j=NT)
            t1 = arena[:, 128:192].rearrange("p (j e) -> p j e", j=NT)
            t2 = arena[:, 192:256].rearrange("p (j e) -> p j e", j=NT)
            first = arena[:, 256:320].rearrange("p (j e) -> p j e", j=NT)
            m8 = arena[:, 320:328]
            back = arena[:, 328:336]
            gates = arena[:, 336:336 + NT * NQ].rearrange("p (j e) -> p j e", j=NT)
            gT = arena[0:NQ, 512:512 + T]
            silu = arena[:, 2048:2048 + 1024].rearrange("p (k t) -> p k t", k=2)
            glu = arena[:, 4096:4096 + 2048].rearrange("p (i k t) -> p i k t", i=2, k=2)
            units = [(e, half) for e in range(NQ) for half in range(2)]

            def bias_col(which, e, k):
                i = NC_EXP + which * 2 * NQ + 2 * e + k
                return cols[:, i:i + 1]

            @block.tensor
            def _(pe):
                pe.wait_ge(moe0_in, 96)
                wait_h_fm(pe)
                for j in range(NT):
                    ins = PE.matmul(ps[:, 6, NE * j:NE * j + NE], h_fm[:, j * P:j * P + P], gate_w[:],
                                    start=True, stop=True)
                ins.then_inc(lg_ps, 1)

            @block.scalar
            def _(act):
                act.wait_ge(shifted, 1)
                AC.activation(pr, t1, ACT.Exp).then_inc(powered, 1)

            def pick_first(src, dst):
                dve_link(V.tensor_reduce(m8, src, AX.X, ALU.max))
                dve_link(V.tensor_tensor(t2, src, over(m8, 2, NE), ALU.is_equal))
                dve_link(V.tensor_tensor(t2, t2, over(back, 1, NT), ALU.mult))
                dve_link(V.tensor_reduce(m8, t2, AX.X, ALU.max))
                dve_link(V.tensor_tensor(dst, t2, over(m8, 2, NE), ALU.is_equal))

            @block.vector
            def _(dve):
                V.tensor_scalar(back, const[:, C_IOTA:C_IOTA + NE], -1.0, float(NE), ALU.mult, ALU.add)
                V.memset(gates, 1.0 / NSH)
                dve.wait_ge(moe0_in, 96)
                dve.wait_ge(lg_ps, 1)
                dve_link(V.tensor_tensor(lg, ps[:, 6, 0:64].rearrange("p (j e) -> p j e", j=NT),
                                         over(gate_b[:], 1, NT), ALU.add))
                dve_link(V.tensor_reduce(m8, lg, AX.X, ALU.max))
                V.tensor_tensor(t1, lg, over(m8, 2, NE), ALU.subtract).then_inc(shifted, 1)
                dve.wait_ge(powered, 1)
                dve_link(V.tensor_reduce(m8, pr, AX.X, ALU.add))
                dve_link(V.reciprocal(m8, m8))
                dve_link(V.tensor_tensor(pr, pr, over(m8, 2, NE), ALU.mult))
                pick_first(pr, first)
                dve_link(V.scalar_tensor_tensor(out=t1, in0=first, scalar=-2.0, in1=pr, op0=ALU.mult, op1=ALU.add))
                dve_link(V.tensor_tensor(lg, first, pr, ALU.mult))
                pick_first(t1, first)
                dve_link(V.tensor_tensor(first, first, pr, ALU.mult))
                V.tensor_tensor(gates[:, :, 0:NE], lg, first, ALU.add).then_inc(gates_ok, 1)

            @block.tensor
            def _(pe):
                def up(u):
                    e, half = units[u]
                    t = slice(512 * half, 512 * half + 512)
                    for k in range(2):
                        if u >= 1:
                            pe.wait_ge(silu_ok, 2 * (u - 1) + k + 1)
                        PE.matmul(ps[:, k, :], w1[:, e, P * k:P * k + P], h_fm[:, t], start=True, stop=True)\
                            .then_inc(up_ps, 1)
                    for k in range(2):
                        if u >= 1:
                            pe.wait_ge(glu_ok, 2 * (u - 1) + k + 1)
                        PE.matmul(ps[:, 2 + k, :], w2[:, e, P * k:P * k + P], h_fm[:, t], start=True, stop=True)\
                            .then_inc(lin_ps, 1)

                def down(u):
                    e, half = units[u]
                    pe.wait_ge(glu_ok, 2 * u + 2)
                    if u >= 2:
                        pe.wait_ge(y_added, u - 1)
                    for t in range(4):
                        for k in range(2):
                            ins = PE.matmul(ps[:, 4 + u % 2, P * t:P * t + P], glu[:, u % 2, k, P * t:P * t + P],
                                            w3[:, e, k, :], start=(k == 0), stop=(k == 1))
                    ins.then_inc(y_ps, 1)

                up(0)
                up(1)
                for u in range(len(units)):
                    if u >= 1 and u + 1 < len(units):
                        up(u + 1)
                    if u == 1:
                        pe.wait_ge(gates_ok, 1)
                        for k in range(2):
                            for j in range(4):
                                ins = PE.transpose(ps[0:NQ, 6 + k, P * j:P * j + P], gates[:, 4 * k + j, :], ident)
                            ins.then_inc(gT_ps, 1)
                        pe.wait_ge(gT_ok, 2)
                        for k in range(2):
                            for j in range(4):
                                ins = PE.matmul(ps[:, 6 + k, P * j:P * j + P],
                                                gT[:, (4 * k + j) * P:(4 * k + j + 1) * P], b3[:], start=True, stop=True)
                            ins.then_inc(by_ps, 1)
                    down(u)

            @block.scalar
            def _(act):
                for u, (e, half) in enumerate(units):
                    for k in range(2):
                        act.wait_ge(up_ps, 2 * u + k + 1)
                        if u >= 1:
                            act.wait_ge(glu_ok, 2 * (u - 1) + k + 1)
                        AC.activation(silu[:, k, :], ps[:, k, :], ACT.Silu, bias=bias_col(0, e, k)).then_inc(silu_ok, 1)
                    if u == 1:
                        for k in range(2):
                            act.wait_ge(gT_ps, k + 1)
                            AC.activation(gT[:, 512 * k:512 * k + 512], ps[0:NQ, 6 + k, :], ACT.Copy).then_inc(gT_ok, 1)

            @block.vector
            def _(dve):
                dve.wait_ge(gates_ok, 1)

                def accumulate(u):
                    e, half = units[u]
                    dve.wait_ge(y_ps, u + 1)
                    if u >= 2:
                        dve.wait_ge(y_added, u - 1)
                    for t in range(4):
                        j = 4 * half + t
                        ins = V.scalar_tensor_tensor(out=x_tm[:, j], in0=ps[:, 4 + u % 2, P * t:P * t + P],
                                                     scalar=gates[:, j, e:e + 1], in1=x_tm[:, j],
                                                     op0=ALU.mult, op1=ALU.add)
                    ins.then_inc(y_added, 1)

                for u, (e, half) in enumerate(units):
                    for k in range(2):
                        dve.wait_ge(lin_ps, 2 * u + k + 1)
                        dve.wait_ge(silu_ok, 2 * u + k + 1)
                        if u >= 2:
                            dve.wait_ge(y_ps, u - 1)
                        V.scalar_tensor_tensor(out=glu[:, u % 2, k, :], in0=ps[:, 2 + k, :], scalar=bias_col(1, e, k),
                                               in1=silu[:, k, :], op0=ALU.add, op1=ALU.mult).then_inc(glu_ok, 1)
                    if u == 2:
                        for k in range(2):
                            dve.wait_ge(by_ps, k + 1)
                            dve_link(V.tensor_tensor(x_tm[:, 4 * k:4 * k + 4], x_tm[:, 4 * k:4 * k + 4],
                                                     ps[:, 6 + k, :].rearrange("p (j d) -> p j d", j=4), ALU.add))
                    if u >= 2:
                        accumulate(u - 2)
                    if u == 4:
                        input_scales(dve)
                accumulate(len(units) - 2)
                dve.wait_ge(y_added, len(units) - 1)
                all_stats(range(4))
                accumulate(len(units) - 1)
                dve.wait_ge(y_added, len(units))
                all_stats(range(4, NT))
                V.sem_inc(x_done, 1)

        wn = sb("wn", [P, 9, P])
        wT = sb("wT", [P, 9, P])
        halves_done = sem("halves_done")
        ffn3_in, scales_ok, wq_ok, wT_ps, wT_ok = (sem("ffn3_in"), sem("scales"), sem("ffn3_w"), sem("ffn3_wT_ps"),
                                                    sem("ffn3_wT"))
        blocks = wn[:].rearrange("p c (g i) -> p (c g) i", i=32)
        wsc, winv = sb("wsc", [P, 36]), sb("winv", [P, 36])

        @block.sync
        def _(sp):
            for i, name in enumerate(("w_gate", "w_up")):
                sp.dma_start(wn[:, 3 * i:3 * i + 3, :], A[name].rearrange("(c p) i -> p c i", p=P)).then_inc(ffn3_in, 16)
            sp.dma_start(wn[:, 6:9, :], A["w_down"].rearrange("p (c i) -> p c i", c=3)).then_inc(ffn3_in, 16)

        def input_scales(dve):
            dve.wait_ge(ffn3_in, 48)
            dve_link(V.tensor_reduce(wsc[:], blocks, AX.X, ALU.max, apply_absolute_value=True))
            dve_link(V.tensor_scalar(wsc[:], wsc[:], 1.0 / 7.0, 1e-12, ALU.mult, ALU.max))
            V.reciprocal(winv[:], wsc[:]).then_inc(scales_ok, 1)
            dve.wait_ge(mask_in, 32)
            dve_link(V.tensor_reduce(sinv[:], mask_sb[:], AX.X, ALU.add))
            dve_link(V.tensor_scalar(sign[:], sinv[:], -1.0, float(S - 1), ALU.mult, ALU.add))
            V.reciprocal(sinv[:], sign[:]).then_inc(scales_ok, 1)

        @block.gpsimd
        def _(pool):
            pool.wait_ge(scales_ok, 1)
            pool_link(G.tensor_tensor(blocks, blocks, over(winv[:], 2, 32), ALU.mult))
            pool_link(G.tensor_scalar(blocks, blocks, MAGIC, -MAGIC, ALU.add, ALU.add))
            G.tensor_tensor(blocks, blocks, over(wsc[:], 2, 32), ALU.mult).then_inc(wq_ok, 1)

        mask_sb = sb("mask_sb", [P, NT, S], I32)
        picks_b = sb("picks_b", [P, 26, P], BF16)
        sign, sinv = sb("sign", [P, NT]), sb("sinv", [P, NT])
        mask_in, picks_in, picks_ok = sem("mask_in"), sem("picks_in"), sem("picks_ok")
        kv_ps, kv_ok = sem("def_kv_ps"), sem("def_kv")
        kv = kexp[:].rearrange("p (j h v b d) -> p j h v b d", j=NT, h=H, v=2, b=2)

        @block.sync
        def _(sp):
            sp.dma_start(l2buf[:, 0:26 * P], A["picks"]).then_inc(picks_in, 16)
            for b in range(2):
                sp.dma_start(mask_sb[S * b:S * b + S],
                             A["mask"].rearrange("(j b) s -> b j s", b=2)[b].partition_broadcast(S)).then_inc(mask_in, 16)

        ab = l2buf[:, 0:4096].rearrange("p (m c) -> p m c", c=P)
        ka = l2buf[:, 4096:6144].rearrange("p (s j c) -> p s j c", s=2, j=NT)
        va = l2buf[:, 6144:8192].rearrange("p (s t) -> p s t", s=2)
        kg_ok, vg_ok = sem("chan_k"), sem("chan_v")

        @block.gpsimd
        def _(pool):
            pool.wait_ge(picks_in, 16)
            G.tensor_copy(picks_b[:].rearrange("p a b -> p (a b)"), l2buf[:, 0:26 * P]).then_inc(picks_ok, 1)
            pool.wait_ge(x_done, 1)
            G.memset(kexp[:], 0.0).then_inc(cleared, 1)
            pool.wait_ge(picks_ok, 1)
            G.memset(l2buf[:, 0:4096], 0.0).then_inc(cleared, 1)
            pool.wait_ge(ctxt_in, 16)
            pool.wait_ge(rows_in, 16)
            for i, name in enumerate(("g", "l")):
                G.tensor_tensor(ka[:, i], ctx_tm[:], over(row(f"L1_xattn_wk{name}"), 1, NT), ALU.mult)\
                    .then_inc(kg_ok, 1)
                pool.wait_ge(kg_ok, 2 * i + 1)
                G.tensor_tensor(ka[:, i], ka[:, i], over(row(f"L1_xattn_bk{name}"), 1, NT), ALU.add)\
                    .then_inc(kg_ok, 1)

        @block.scalar
        def _(act):
            act.wait_ge(cols_in, 16)
            act.wait_ge(ctxf_in, 16)
            for i, name in enumerate(("g", "l")):
                AC.activation(va[:, i], ctx_fm[:], ACT.Identity, bias=col(f"L1_xattn_bv{name}"),
                              scale=col(f"L1_xattn_wv{name}")).then_inc(vg_ok, 1)

        layernorm()
        moe0(1)

        def keys_values_l2(pe, banks):
            wkv = mats[:, MATS.index("L2_xattn_Wk"):MATS.index("L2_xattn_Wk") + 2, :].rearrange("p a b -> p (a b)")
            bkv = over(rows[0:1, ROWS.index("L2_xattn_bk"):ROWS.index("L2_xattn_bk") + 2, :]
                       .rearrange("p a b -> p (a b)"), 1, 2)
            one = const[0:1, C_IOTA + 1:C_IOTA + 2].broadcast_to([1, P])
            for bank in banks:
                if bank >= 2:
                    pe.wait_ge(kv_ok, 2 * (bank - 1))
                at_ps = ps[:, 6 + bank % 2, :]
                PE.matmul(at_ps.rearrange("p (j c) -> p j c", j=2), one, bkv, start=True, stop=False)
                for i in range(2):
                    j = 2 * bank + i
                    ins = PE.matmul(at_ps[:, 256 * i:256 * i + 256], ctx_fm[:, P * j:P * j + P], wkv,
                                    start=False, stop=(i == 1))
                ins.then_inc(kv_ps, 1)

        def keys_values_l2_blocks(act, banks):
            act.wait_ge(cleared, KV_CLEAR)
            for bank in banks:
                act.wait_ge(kv_ps, bank + 1)
                for b in range(2):
                    r = slice(S * b, S * b + S)
                    for v in range(2):
                        src = ps[r, 6 + bank % 2, :].rearrange("p (j v h d) -> p j v h d", j=2, v=2, h=H)[:, :, v]
                        ins = AC.activation(kv[r, 2 * bank:2 * bank + 2, :, v, b, :], src, ACT.Copy)
                    ins.then_inc(kv_ok, 1)

        def channel_attention(n):
            s = lambda name: sem(f"chan_{name}")
            q_ok, s_ps, sub_ok, e_ok, ab_ok, y_ps = (
                s("q"), s("scores"), s("less_max"), s("exp"), s("attnT"), s("y"))
            sets = 2
            weight_banks = ((6, 0, 4), (7, 4, 8), (6, 8, 9))
            qa = arena[:, 0:2048].rearrange("p (s j c) -> p s j c", s=2, j=NT)
            at = arena[:, 6144:7168].rearrange("p (m e) -> p m e", e=32)
            m32 = arena[:, 7168:7200]
            att = arena[:, 7424:8448].rearrange("p (j c) -> p j c", j=NT)

            layernorm(feature_major=False)

            @block.vector
            def _(dve):
                wait_h_tm(dve)
                for i, name in enumerate(("g", "l")):
                    dve_link(V.tensor_tensor(qa[:, i], h_tm[:], over(row(f"L1_xattn_wq{name}"), 1, NT), ALU.mult))
                    V.tensor_tensor(qa[:, i], qa[:, i], over(row(f"L1_xattn_bq{name}"), 1, NT), ALU.add)\
                        .then_inc(q_ok, 1)
                dve_link(V.tensor_tensor(x_tm[:], x_tm[:], over(row("L1_xattn_bp"), 1, NT), ALU.add))

            @block.tensor
            def _(pe):
                pe.wait_ge(wq_ok, 1)
                pe.wait_ge(x_done, n)
                for k, (bank, c0, c1) in enumerate(weight_banks):
                    if k == 2:
                        pe.wait_ge(wT_ok, 1)
                    for c in range(c0, c1):
                        ins = PE.transpose(ps[:, bank, P * (c - c0):P * (c - c0) + P], wn[:, c, :], ident)
                    ins.then_inc(wT_ps, 1)
                for i in range(sets):
                    pe.wait_ge(kg_ok, 2 * i + 2)
                    pe.wait_ge(q_ok, i + 1)
                    for b in range(B):
                        r = slice(S * (b % 2), S * (b % 2) + S)
                        for h in range(4):
                            c = slice(32 * h, 32 * h + 32)
                            ins = PE.matmul(ps[c, 2 * i + b % 2, 32 * (b // 2):32 * (b // 2) + 32], qa[r, i, b // 2, c], ka[r, i, b // 2, c],
                                            start=True, stop=True)
                    ins.then_inc(s_ps, 1)
                pe.wait_ge(wT_ok, 3)
                keys_values_l2(pe, (0, 1))
                pe.wait_ge(vg_ok, 2)
                pe.wait_ge(ab_ok, 1)
                for j in range(NT):
                    for half in range(2):
                        b = 2 * j + half
                        for i in range(sets):
                            ins = PE.matmul(ps[S * half:S * half + S, 4 + j // 4, P * (j % 4):P * (j % 4) + P],
                                            va[:, i, S * b:S * b + S], ab[:, B * i + NT * half + j, :],
                                            start=(i == 0), stop=(i == 1))
                    if j % 4 == 3:
                        ins.then_inc(y_ps, 1)

            @block.vector
            def _(dve):
                for i in range(sets):
                    mi = slice(B * i, B * i + B)
                    dve.wait_ge(s_ps, i + 1)
                    sc = ps[:, 2 * i:2 * i + 2, 0:256].rearrange("p b (m e) -> p b m e", e=32)
                    pair = lambda v: v.rearrange("p (b m) -> p b m", b=2)
                    dve_link(V.tensor_reduce(pair(m32[:, mi]), sc, AX.X, ALU.max))
                    V.tensor_tensor(at[:, mi].rearrange("p (b m) e -> p b m e", b=2), sc,
                                    over(pair(m32[:, mi]), 3, 32), ALU.subtract).then_inc(sub_ok, 1)
                    dve.wait_ge(e_ok, i + 1)
                    dve_link(V.tensor_reduce(m32[:, mi], at[:, mi], AX.X, ALU.add))
                    dve_link(V.reciprocal(m32[:, mi], m32[:, mi]))
                    dve_link(V.tensor_tensor(at[:, mi], at[:, mi], over(m32[:, mi], 2, 32), ALU.mult))
                    dve.wait_ge(cleared, AB_CLEAR)
                    for h in range(4):
                        c = slice(32 * h, 32 * h + 32)
                        ins = V.transpose(ab[c, mi, c], at[c, mi])
                ins.then_inc(ab_ok, 1)
                for k in range(2):
                    dve.wait_ge(y_ps, k + 1)
                    dve_link(V.scalar_tensor_tensor(out=att[:, 4 * k:4 * k + 4],
                                                    in0=ps[:, 4 + k, :].rearrange("p (j c) -> p j c", j=4), scalar=2.0,
                                                    in1=over(row("L1_xattn_wp"), 1, 4), op0=ALU.mult, op1=ALU.mult))
                    ins = V.tensor_tensor(x_tm[:, 4 * k:4 * k + 4], x_tm[:, 4 * k:4 * k + 4], att[:, 4 * k:4 * k + 4],
                                          ALU.add)
                    dve_link(ins)
                    all_stats(range(4 * k, 4 * k + 4))
                V.sem_inc(x_done, 1)

            @block.scalar
            def _(act):
                for k, (bank, c0, c1) in enumerate(weight_banks):
                    act.wait_ge(wT_ps, k + 1)
                    AC.activation(wT[:, c0:c1, :].rearrange("p c k -> p (c k)"), ps[:, bank, 0:P * (c1 - c0)], ACT.Copy)\
                        .then_inc(wT_ok, 1)
                for i in range(sets):
                    act.wait_ge(sub_ok, i + 1)
                    AC.activation(at[:, B * i:B * i + B], at[:, B * i:B * i + B], ACT.Exp,
                                  scale=float(D) ** -0.5).then_inc(e_ok, 1)
                keys_values_l2_blocks(act, (0, 1))

        channel_attention(2)

        wq8_in = sem("wq8_in")
        wq8 = sb("wq8", [P, P], I32)
        wq8b = sb("wq8b", [P, P], BF16)
        ident_b = sb("ident_b", [P, P], BF16)

        l3_keys = (sem("L3_k_ps"), sem("L3_k_sb"))

        def int8_linear(n):
            s = lambda name: sem(f"int8_{name}")
            xq_ok, xT_ps, xT_ok, y_ps = s("x"), s("xT_ps"), s("xT"), s("y")
            am = arena[:, 0:8]
            xs = arena[:, 8:16]
            inv = arena[:, 16:24]
            t = arena[:, 1024:2048].rearrange("p (j c) -> p j c", j=NT)
            y = arena[:, 2048:3072].rearrange("p (j c) -> p j c", j=NT)
            xq = arena[:, 3072:3584].bitcast(BF16).rearrange("p (j c) -> p j c", j=NT)
            xT = arena[:, 3584:4096].bitcast(BF16)

            @block.sync
            def _(sp):
                sp.dma_start(wq8[:], A["wq8"]).then_inc(wq8_in, 16)

            layernorm(feature_major=False)

            @block.vector
            def _(dve):
                dve.wait_ge(wq8_in, 16)
                V.tensor_copy(wq8b[:], wq8[:])
                V.tensor_copy(ident_b[:], ident)
                wait_h_tm(dve)
                dve_link(V.tensor_reduce(am, h_tm[:], AX.X, ALU.max, apply_absolute_value=True))
                dve_link(V.tensor_scalar(xs, am, 1e-6, 1.0 / 127.0, ALU.max, ALU.mult))
                dve_link(V.reciprocal(inv, xs))
                dve_link(V.tensor_tensor(t, h_tm[:], over(inv, 2, D), ALU.mult))
                dve_link(V.tensor_scalar(t, t, MAGIC, -MAGIC, ALU.add, ALU.add))
                V.tensor_scalar(xq, t, -128.0, 127.0, ALU.max, ALU.min).then_inc(xq_ok, 1)
                dve_link(V.tensor_tensor(x_tm[:], x_tm[:], over(row("L1_ffn_bias"), 1, NT), ALU.add))
                for k in range(2):
                    r = slice(4 * k, 4 * k + 4)
                    dve.wait_ge(y_ps, k + 1)
                    dve_link(V.tensor_tensor(y[:, r], ps[:, 2 + k, :].rearrange("p (j c) -> p j c", j=4),
                                             over(xs[:, r], 2, D), ALU.mult))
                    dve_link(V.tensor_tensor(y[:, r], y[:, r], over(row("L1_ffn_weight_scale"), 1, 4), ALU.mult))
                    dve_link(V.tensor_tensor(x_tm[:, r], x_tm[:, r], y[:, r], ALU.add))
                    all_stats(range(4 * k, 4 * k + 4))
                V.sem_inc(x_done, 1)

            @block.tensor
            def _(pe):
                tp = ps[:, 0, :].bitcast(BF16)

                keys_values_l2(pe, (2, 3))
                pe.wait_ge(xq_ok, 1)
                for j in range(NT):
                    ins = PE.transpose(tp[:, P * j:P * j + P], xq[:, j], ident_b[:])
                ins.then_inc(xT_ps, 1)
                pe.wait_ge(xT_ok, 1)
                for k in range(2):
                    for j in range(4):
                        i = 4 * k + j
                        ins = PE.matmul(ps[:, 2 + k, P * j:P * j + P], xT[:, P * i:P * i + P], wq8b[:],
                                        start=True, stop=True)
                    ins.then_inc(y_ps, 1)
                for k in range(2):
                    PE.matmul(ps[:, k, :], mat("L3_xattn_W_k"), ctx_fm[:, 512 * k:512 * k + 512],
                              start=True, stop=True).then_inc(l3_keys[0], 1)

            @block.scalar
            def _(act):
                keys_values_l2_blocks(act, (2, 3))
                act.wait_ge(xT_ps, 1)
                AC.activation(xT, ps[:, 0, :].bitcast(BF16), ACT.Copy).then_inc(xT_ok, 1)

        int8_linear(3)

        def deformable(n):
            s = lambda name: sem(f"def_{name}")
            q_ps, q_sb, qt_ps, qt_ok, qx_ok = s("q_ps"), s("q_sb"), s("qt_ps"), s("qt"), s("qx")
            off_ps, parts_ok, parts1_ok, mv_ps, ix_ok = s("off_ps"), s("parts0"), s("parts1"), s("moved_ps"), s("ix")
            bc_ps, abs_ok, hat_ok = s("bc_ps"), s("abs"), s("hat")
            smp_ps, smp_sb0, smp_sb, turned = s("sampled_ps"), s("sampled_even"), s("sampled_odd"), s("turned")
            cx_ok = s("ctx_sb")
            v_ok, prod_ok, sc_ok, e_ok, c_ok, cT_ps, cT_ok, y_ps = (
                s("sv"), s("prod"), s("scores"), s("exp"), s("ctx"), s("ctxT_ps"), s("ctxT"), s("y"))
            off_sb = s("off_sb")
            kvc = kexp[:].rearrange("p (j h m) -> p j h m", j=NT, h=H)
            hats = arena[:].rearrange("p (i r c) -> p i r c", i=2, r=20)
            qt = v4[:, 64:1088].rearrange("p (i h b d) -> p i h b d", i=4, h=H, b=2)
            cxn = v4[:, 1088:2112].rearrange("p (i g c) -> p i g c", i=4, g=4)
            cx = l2buf[:, 2560:3584].rearrange("p (i b c) -> p i b c", i=4, b=2)
            smp = l2buf[:, 2560:3840].rearrange("p (i k c) -> p i k c", i=2, k=NK)
            prod = v4[:, 2112:2752].rearrange("p (i r c) -> p i r c", i=2, c=16)
            sc = v4[:, 2752:2752 + 320].rearrange("p (i r b) -> p i r b", i=2, b=2)
            mx = v4[:, 3072:3104]
            rs = v4[:, 3104:3136]
            spare = ctx_tm[:].rearrange("p j d -> p (j d)")
            off = [l2buf[:, 5632:6144], spare[:, 0:512]]
            t1 = [l2buf[:, 6144:6656], spare[:, 512:1024]]
            parts = [v.bitcast(BF16).rearrange("p (i c) -> p i c", i=3) for v in (l2buf[:, 3840:4608], v4[:, 3136:3904])]
            ixm = l2buf[:, 4608:5632].bitcast(BF16).rearrange("p (g c) -> p g c", g=4)
            qx = l2buf[:, 0:2560].rearrange("p (i r c) -> p i r c", i=2, c=16)
            sv = l2buf[:, 5632:8192].rearrange("p (i r c) -> p i r c", i=2, c=16)
            units = [(hg, half) for hg in range(4) for half in range(2)]
            qscale = -0.5 / float(np.sqrt(HD))

            layernorm()

            @block.tensor
            def _(pe):
                for k in range(2):
                    wait_h_fm(pe, k)
                    PE.matmul(ps[:, 6 + k, :], mat("L2_xattn_Wq"), h_fm[:, 512 * k:512 * k + 512],
                              start=True, stop=True).then_inc(q_ps, 1)
                pe.wait_ge(q_sb, 2)
                qv = q_fm[:].rearrange("p (j b q) -> p j b q", j=NT, b=2)
                for g in range(2):
                    for b in range(2):
                        ins = PE.matmul(ps[S * b:S * b + S, 2 + g, :], woff[:, g, :], qv[:, :, b, :], start=True, stop=True)
                    ins.then_inc(off_ps, 1)
                pe.wait_ge(l3_keys[1], 2)
                for j in range(NT):
                    for b in range(2):
                        c = (j // 2) * 256 + P * b
                        ins = PE.matmul(ps[S * (j % 2):S * (j % 2) + S, c // 512, c % 512:c % 512 + P],
                                        h_fm[:, P * j + S * b:P * j + S * b + S], mat("L2_xattn_Wq"), start=True, stop=True)
                ins.then_inc(qt_ps, 1)

            MOVES = ((0, slice(0, 256)), (0, slice(256, 512)), (1, slice(0, 512)), (2, slice(0, 512)), (3, slice(0, 512)))
            MOVE_STEPS = (None, 0, 1, 5, 7)

            def move(pe, k):
                hg, c = MOVES[k]
                if k >= 1:
                    pe.wait_ge(ix_ok, k)
                    pe.wait_ge(parts1_ok, 1 if hg < 2 else 2)
                for i in range(3):
                    ins = PE.matmul(ps[:, 3, c], picks_b[:, 20 + 3 * (hg % 2) + i, :], parts[hg // 2][:, i, c],
                                    start=(i == 0), stop=(i == 2))
                ins.then_inc(mv_ps, 1)

            def keep_positions(act, k):
                hg, c = MOVES[k]
                act.wait_ge(mv_ps, k + 1)
                AC.activation(ixm[:, hg, c], ps[:, 3, c], ACT.Copy).then_inc(ix_ok, 1)

            @block.scalar
            def _(act):
                for k in range(2):
                    act.wait_ge(q_ps, k + 1)
                    AC.activation(q_fm[:, 512 * k:512 * k + 512], ps[:, 6 + k, :], ACT.Identity,
                                  bias=col("L2_xattn_bq")).then_inc(q_sb, 1)
                for g in range(2):
                    act.wait_ge(off_ps, g + 1)
                    AC.activation(off[g], ps[:, 2 + g, :], ACT.Identity,
                                  bias=cols[:, NC_EXP + 4 * NQ + g:NC_EXP + 4 * NQ + g + 1]).then_inc(off_sb, 1)
                    if g == 0:
                        for k in range(2):
                            act.wait_ge(l3_keys[0], k + 1)
                            AC.activation(k_fm[:, 512 * k:512 * k + 512], ps[:, k, :], ACT.Identity,
                                          bias=col("L3_xattn_b_k")).then_inc(l3_keys[1], 1)

            def positions(eng, E, link, g, pairs, done):
                c = slice(S * pairs.start, S * pairs.stop)
                o, t = off[g][:, c], t1[g][:, c]

                def jq(v):
                    return v.rearrange("p (j q) -> p j q", q=S)

                eng.wait_ge(off_sb, g + 1)
                eng.wait_ge(scales_ok, 2)
                ref = over(const[:, C_REF:C_REF + S], 1, pairs.stop - pairs.start)
                sg, iv = over(sign[:, pairs], 2, S), over(sinv[:, pairs], 2, S)
                link(E.tensor_tensor(jq(o), jq(o), ref, ALU.add))
                link(E.tensor_tensor(jq(t), jq(o), iv, ALU.mult))
                link(E.tensor_scalar(t, t, MAGIC, -MAGIC, ALU.add, ALU.add))
                link(E.tensor_tensor(jq(t), jq(t), sg, ALU.mult))
                link(E.tensor_tensor(o, o, t, ALU.subtract))
                link(E.tensor_tensor(jq(t), jq(o), iv, ALU.mult))
                link(E.tensor_scalar(t, t, 0.0, None, ALU.is_lt))
                link(E.tensor_tensor(jq(t), jq(t), sg, ALU.mult))
                link(E.tensor_tensor(o, o, t, ALU.add))
                link(E.tensor_scalar(o, o, float(S) / (S - 1), -0.5, ALU.mult, ALU.add))
                link(E.tensor_copy(parts[g][:, 0, c], o))
                link(E.tensor_tensor(t, o, parts[g][:, 0, c], ALU.subtract))
                link(E.tensor_copy(parts[g][:, 1, c], t))
                E.tensor_tensor(parts[g][:, 2, c], t, parts[g][:, 1, c], ALU.subtract).then_inc(done, 1)

            @block.gpsimd
            def _(pool):
                positions(pool, G, pool_link, 0, slice(4, 8), parts1_ok)
                positions(pool, G, pool_link, 1, slice(0, 8), parts1_ok)

            @block.vector
            def _(dve):
                positions(dve, V, dve_link, 0, slice(0, 4), parts_ok)
                dve.wait_ge(qt_ps, 1)
                for c in range(4):
                    src = ps[:, c // 2, 256 * (c % 2):256 * (c % 2) + 256].rearrange("p (b h d) -> p h b d", b=2, h=H)
                    bias = over(row("L2_xattn_bq").rearrange("p (h d) -> p h d", h=H), 2, 2)
                    ins = V.tensor_tensor(qt[:, c], src, bias, ALU.add)
                ins.then_inc(qt_ok, 1)
                wait_h_tm(dve)
                dve_link(V.tensor_tensor(x_tm[:], x_tm[:], over(row("L2_xattn_bo"), 1, NT), ALU.add))

            NW = 2 * len(units)

            def chunks(w):
                return list(range(5 * (w % 2), 5 * (w % 2) + 5)) if w // 2 + 1 < len(units) else []

            @block.tensor
            def _(pe):
                def broadcast(u, c):
                    hg, half = units[u]
                    m = 10 * u + c
                    if m >= 3:
                        pe.wait_ge(abs_ok, m - 2)
                    for i in range(2):
                        ins = PE.matmul(ps[:, m % 3, 256 * i:256 * i + 256], picks_b[:, 2 * c + i, :],
                                        ixm[:, hg, 256 * half:256 * half + 256], start=True, stop=True)
                    ins.then_inc(bc_ps, 1)

                def sample(w):
                    u, i = w // 2, w % 2
                    hg, half = units[u]
                    pe.wait_ge(hat_ok, 10 * (u + 1))
                    if w >= 1:
                        pe.wait_ge(smp_sb0, w)
                        pe.wait_ge(smp_sb, w)
                    for par in range(2):
                        j = 4 * half + 2 * i + par
                        for hl in range(4):
                            ins = PE.matmul(ps[32 * hl:32 * hl + 32, 4 + par, 0:NK * S], kvc[:, j, 4 * hg + hl, :],
                                            hats[:, u % 2, NK * hl:NK * hl + NK, S * (2 * i + par):S * (2 * i + par) + S],
                                            start=True, stop=True)
                    ins.then_inc(smp_ps, 1)

                def turn(w):
                    pe.wait_ge(smp_sb0, w + 1)
                    pe.wait_ge(smp_sb, w + 1)
                    if w >= 1:
                        pe.wait_ge(prod_ok, w)
                        pe.wait_ge(v_ok, w)
                    for k in range(NK):
                        for h0, h1 in (((0, 2), (2, 4)) if k == 2 else ((0, 4),)):
                            at = 4 * k + h0
                            ins = PE.matmul(ps[:, 6 + at // 10, 32 * (at % 10):32 * (at % 10 + h1 - h0)], smp[:, w % 2, k, :],
                                            ident[:, 32 * h0:32 * h1], start=True, stop=True)
                    ins.then_inc(turned, 1)

                pe.wait_ge(off_sb, 2)
                pe.wait_ge(parts_ok, 1)
                move(pe, 0)
                pe.wait_ge(qt_ok, 1)
                pe.wait_ge(ix_ok, 1)
                for c in range(10):
                    broadcast(0, c)
                pe.wait_ge(kv_ok, 8)
                for w in range(NW + 2):
                    if w in MOVE_STEPS[1:]:
                        move(pe, MOVE_STEPS.index(w))
                    if w in (0, 2, 6, 10):
                        pe.wait_ge(ix_ok, {0: 2, 2: 3, 6: 4, 10: 5}[w])
                    for c in chunks(w)[:3]:
                        broadcast(w // 2 + 1, c)
                    if w >= 2:
                        turn(w - 2)
                    for c in chunks(w)[3:]:
                        broadcast(w // 2 + 1, c)
                    if w < NW:
                        sample(w)
                pe.wait_ge(cx_ok, 1)
                for jp in range(4):
                    for b in range(2):
                        ins = PE.transpose(ps[:, jp // 2, 256 * (jp % 2) + P * b:256 * (jp % 2) + P * b + P],
                                           cx[:, jp, b, :], ident)
                    if jp % 2 == 1:
                        ins.then_inc(cT_ps, 1)
                for k in range(2):
                    pe.wait_ge(cT_ok, k + 1)
                    for i in range(4):
                        j = 4 * k + i
                        ins = PE.matmul(ps[:, 2 + k, P * i:P * i + P], o_fm[:, P * j:P * j + P], mat("L2_xattn_Wo"),
                                        start=True, stop=True)
                    ins.then_inc(y_ps, 1)

            @block.scalar
            def _(act):
                def spread_q(hg):
                    act.wait_ge(qt_ok, 1)
                    if hg >= 2:
                        act.wait_ge(prod_ok, 4 * (hg - 1))
                    src = over(qt[:, :, 4 * hg:4 * hg + 4].rearrange("p i h b d -> p i (h b d)"), 2, NK)
                    dst = qx[:, hg % 2].rearrange("p (i k h) c -> p i k (h c)", i=4, k=NK)
                    AC.activation(dst, src, ACT.Copy, scale=qscale).then_inc(qx_ok, 1)

                def absolute(u, c):
                    m = 10 * u + c
                    act.wait_ge(bc_ps, m + 1)
                    if u >= 2 and c == 0:
                        act.wait_ge(smp_ps, 2 * (u - 1))
                    AC.activation(hats[:, u % 2, 2 * c:2 * c + 2, :].rearrange("p r c -> p (r c)"), ps[:, m % 3, :],
                                  ACT.Abs, bias=const[:, C_NEGM:C_NEGM + 1]).then_inc(abs_ok, 1)

                def exponentials(hg):
                    act.wait_ge(sc_ok, hg + 1)
                    AC.activation(sc[:, hg % 2], sc[:, hg % 2], ACT.Exp).then_inc(e_ok, 1)

                def to_sbuf(w):
                    act.wait_ge(smp_ps, w + 1)
                    if w >= 2:
                        act.wait_ge(turned, w - 1)
                    AC.activation(smp[:, w % 2, :, 0:S], ps[:, 4, 0:NK * S].rearrange("p (k q) -> p k q", k=NK), ACT.Copy)\
                        .then_inc(smp_sb0, 1)

                def keep_values(w):
                    hg, jp = w // 4, w % 4
                    act.wait_ge(prod_ok, w + 1)
                    if jp == 0 and hg >= 2:
                        act.wait_ge(c_ok, hg - 1)
                    src = ps[:, 6:8, 0:320].rearrange("p k (r c) -> p k r c", c=32)[:, :, :, 16:32]
                    dst = sv[:, hg % 2, 20 * jp:20 * jp + 20].rearrange("p (k r) c -> p k r c", k=2)
                    AC.activation(dst, src, ACT.Copy).then_inc(v_ok, 1)

                keep_positions(act, 0)
                for c in range(10):
                    absolute(0, c)
                spread_q(0)
                for w in range(NW + 2):
                    if w in MOVE_STEPS[1:]:
                        keep_positions(act, MOVE_STEPS.index(w))
                    if 1 <= w <= NW:
                        to_sbuf(w - 1)
                    for c in chunks(w):
                        absolute(w // 2 + 1, c)
                    if w >= 2:
                        keep_values(w - 2)
                    if w % 4 == 2 and w // 4 + 1 < 4:
                        spread_q(w // 4 + 1)
                    if w % 4 == 2 and w >= 6:
                        exponentials(w // 4 - 1)
                exponentials(3)
                act.wait_ge(c_ok, 4)
                for b in range(2):
                    src = cxn[:].rearrange("p i g (h b d) -> p i (g h) b d", h=4, b=2)[:, :, :, b, :]
                    ins = AC.activation(cx[:, :, b, :].rearrange("p i (h d) -> p i h d", h=H), src, ACT.Copy)
                ins.then_inc(cx_ok, 1)
                for k in range(2):
                    act.wait_ge(cT_ps, k + 1)
                    dst = o_fm[:, 512 * k:512 * k + 512].rearrange("p (i t b q) -> p i t b q", i=2, t=2, b=2)
                    src = ps[:, k, :].rearrange("p (i b t q) -> p i t b q", i=2, b=2, t=2)
                    for i in range(2):
                        ins = AC.activation(dst[:, i], src[:, i], ACT.Copy)
                    ins.then_inc(cT_ok, 1)

            @block.vector
            def _(dve):
                def hat(u, c):
                    dve.wait_ge(abs_ok, 10 * u + c + 1)
                    v = hats[:, u % 2, 2 * c:2 * c + 2, :].rearrange("p r c -> p (r c)")
                    V.tensor_scalar(v, v, 1.0, -1.0, ALU.min, ALU.add).then_inc(hat_ok, 1)

                def to_sbuf(w):
                    dve.wait_ge(smp_ps, w + 1)
                    if w >= 2:
                        dve.wait_ge(turned, w - 1)
                    V.tensor_copy(smp[:, w % 2, :, S:P], ps[:, 5, 0:NK * S].rearrange("p (k q) -> p k q", k=NK))\
                        .then_inc(smp_sb, 1)

                def multiply(w):
                    hg, jp = w // 4, w % 4
                    dve.wait_ge(turned, w + 1)
                    if jp == 0:
                        dve.wait_ge(qx_ok, hg + 1)
                    src = ps[:, 6:8, 0:320].rearrange("p k (r c) -> p k r c", c=32)[:, :, :, 0:16]
                    pr = prod[:, w % 2]
                    V.tensor_tensor(pr.rearrange("p (k r) c -> p k r c", k=2), src,
                                    qx[:, hg % 2, 20 * jp:20 * jp + 20].rearrange("p (k r) c -> p k r c", k=2),
                                    ALU.mult).then_inc(prod_ok, 1)

                def add_up(w):
                    hg, jp, pr = w // 4, w % 4, prod[:, w % 2]
                    dve.wait_ge(prod_ok, w + 1)
                    dve_link(V.tensor_reduce(sc[:, hg % 2, 20 * jp:20 * jp + 20, :],
                                             pr.rearrange("p r (b d) -> p r b d", b=2), AX.X, ALU.add))

                def by_point(hg):
                    v = sc[:, hg % 2].rearrange("p (i k h) b -> p i (h b) k", i=4, k=NK)
                    return v, lambda t: t.rearrange("p (i c) -> p i c", i=4)

                def softmax(hg):
                    v, ic = by_point(hg)
                    dve_link(V.tensor_reduce(ic(mx), v, AX.X, ALU.max))
                    V.tensor_tensor(v, v, over(ic(mx), 3, NK), ALU.subtract).then_inc(sc_ok, 1)

                def context(hg):
                    v, ic = by_point(hg)
                    dve.wait_ge(e_ok, hg + 1)
                    dve_link(V.tensor_reduce(ic(rs), v, AX.X, ALU.add))
                    dve_link(V.reciprocal(rs, rs))
                    dve_link(V.tensor_scalar(rs, rs, -0.5, None, ALU.mult))
                    dve_link(V.tensor_tensor(v, v, over(ic(rs), 3, NK), ALU.mult))
                    dve.wait_ge(v_ok, 4 * hg + 4)
                    values = sv[:, hg % 2].rearrange("p r (b d) -> p (r b) d", b=2)
                    dve_link(V.tensor_tensor(values, values, over(sc[:, hg % 2].rearrange("p r b -> p (r b)"), 2, HD), ALU.mult))
                    V.tensor_reduce(cxn[:, :, hg], sv[:, hg % 2].rearrange("p (i k h) c -> p i (h c) k", i=4, k=NK),
                                    AX.X, ALU.add).then_inc(c_ok, 1)

                for c in range(10):
                    hat(0, c)
                for w in range(NW + 2):
                    if 1 <= w <= NW:
                        to_sbuf(w - 1)
                    for c in chunks(w)[:3]:
                        hat(w // 2 + 1, c)
                    if w >= 2:
                        multiply(w - 2)
                    for c in chunks(w)[3:4]:
                        hat(w // 2 + 1, c)
                    if w >= 2:
                        add_up(w - 2)
                    for c in chunks(w)[4:]:
                        hat(w // 2 + 1, c)
                    if w % 4 == 1 and w >= 5:
                        softmax(w // 4 - 1)
                    if w % 4 == 3 and w >= 7:
                        context(w // 4 - 1)
                context(3)
                for k in range(2):
                    dve.wait_ge(y_ps, k + 1)
                    dve_link(V.tensor_tensor(x_tm[:, 4 * k:4 * k + 4], x_tm[:, 4 * k:4 * k + 4],
                                             ps[:, 2 + k, :].rearrange("p (j d) -> p j d", j=4), ALU.add))
                    all_stats(range(4 * k, 4 * k + 4))
                V.sem_inc(x_done, 1)

        @block.tensor
        def _(pe):
            pe.wait_ge(picks_ok, 1)

        deformable(4)

        moe2_in = sem("moe2_in")
        bias_in, bm_ready, bm_done = sem("bias_in"), sem("bias_seen"), sem("bias_ready")
        m2w1 = weights[:, 0:4096].rearrange("p (e f) -> p e f", e=NE)
        m2w2 = weights[:, 4096:8192].rearrange("p (e k d) -> p e k d", e=NE, k=4)
        idx = sb("idx", [P, 4, TOPK], I32)
        gw = sb("gw", [P, 4, TOPK])

        def moe2(n, beside_experts, beside_gelu):
            s = lambda name: sem(f"moe2_{name}")
            up_ps, g_ok, y_ps, y_added, gates_ok = s("up_ps"), s("gelu"), s("y"), s("y_added"), s("gates")
            hid = arena[:, 0:4096].rearrange("p (i k t) -> p i k t", i=2, k=4)
            idf = arena[:, 4096:4104].rearrange("p (j k) -> p j k", j=4)
            g2 = arena[:, 4128:4192].rearrange("p (j k e) -> p j k e", j=4, k=2)
            gates = arena[:, 4192:4224].rearrange("p (j e) -> p j e", j=4)

            layernorm()

            @block.vector
            def _(dve):
                beside_experts(dve, -1)
                dve.wait_ge(moe2_in, 64)
                dve_link(V.tensor_copy(idf, idx[:]))
                for k in range(TOPK):
                    eq = over(idf[:, :, k], 2, NE)
                    ins = V.tensor_tensor(g2[:, :, k, :], eq, over(const[:, C_IOTA:C_IOTA + NE], 1, 4), ALU.is_equal)
                dve_link(ins)
                for k in range(TOPK):
                    ins = V.tensor_tensor(g2[:, :, k, :], g2[:, :, k, :], over(gw[:, :, k], 2, NE), ALU.mult)
                dve_link(ins)
                dve_link(V.tensor_tensor(gates, g2[:, :, 0, :], g2[:, :, 1, :], ALU.add))
                wait_h_tm(dve)
                dve_link(V.tensor_tensor(x_tm[:], x_tm[:], over(row("L2_ffn_bias"), 1, NT), ALU.add))
                for j in range(4, NT):
                    tile_stats(j)
                for e in range(NE):
                    dve.wait_ge(y_ps, e + 1)
                    if e >= 1:
                        dve.wait_ge(y_added, e)
                    for j in range(4):
                        ins = V.scalar_tensor_tensor(out=x_tm[:, j], in0=ps[:, 4 + e % 2, P * j:P * j + P],
                                                     scalar=gates[:, j, e:e + 1], in1=x_tm[:, j],
                                                     op0=ALU.mult, op1=ALU.add)
                    ins.then_inc(y_added, 1)
                    beside_experts(dve, e)
                dve.wait_ge(y_added, NE)
                for j in range(4):
                    ins = tile_stats(j)
                dve_link(ins)
                V.sem_inc(x_done, 1)

            @block.tensor
            def _(pe):
                wait_h_fm(pe)
                pe.wait_ge(moe2_in, 64)

                def up(e):
                    for k in range(4):
                        if e >= 1:
                            pe.wait_ge(g_ok, 4 * (e - 1) + k + 1)
                        elif k >= 2:
                            pe.wait_ge(l3_v_sb, 4 if k == 2 else 3)
                        PE.matmul(ps[:, k, :], m2w1[:, e, P * k:P * k + P], h_fm[:, 0:T2], start=True, stop=True)\
                            .then_inc(up_ps, 1)

                def down(e):
                    pe.wait_ge(g_ok, 4 * e + 4)
                    if e >= 2:
                        pe.wait_ge(y_added, e - 1)
                    for j in range(4):
                        for k in range(4):
                            ins = PE.matmul(ps[:, 4 + e % 2, P * j:P * j + P], hid[:, e % 2, k, P * j:P * j + P],
                                            m2w2[:, e, k, :], start=(k == 0), stop=(k == 3))
                    ins.then_inc(y_ps, 1)

                up(0)
                for e in range(NE):
                    if e + 1 < NE:
                        up(e + 1)
                    down(e)

            @block.scalar
            def _(act):
                for e in range(NE):
                    if e >= 2:
                        act.wait_ge(y_ps, e - 1)
                    for k in range(4):
                        act.wait_ge(up_ps, 4 * e + k + 1)
                        AC.activation(hid[:, e % 2, k, :], ps[:, k, :], ACT.Gelu).then_inc(g_ok, 1)
                    beside_gelu(act, e)

        @block.sync
        def _(sp):
            sp.wait_ge(x_done, 2)
            sp.dma_start(m2w1, A["moe2_w1"]).then_inc(moe2_in, 16)
            sp.dma_start(m2w2, A["moe2_w2"]).then_inc(moe2_in, 16)
            sp.dma_start(idx[:], A["moe2_idx"]).then_inc(moe2_in, 16)
            sp.dma_start(gw[:], A["moe2_gw"]).then_inc(moe2_in, 16)

        @block.gpsimd
        def _(pool):
            pool.wait_ge(x_done, 5)
            G.memset(v4[:], 0.0).then_inc(cleared, 1)

        @block.sync
        def _(sp):
            sp.wait_ge(x_done, 5)
            sp.dma_start(masks, A["attn_mask"].rearrange("(j p) k -> p j k", p=P)).then_inc(bias_in, 16)
            for b in range(2):
                sp.dma_start(bias[S * b:S * b + S].rearrange("p (h k) -> p h k", h=H),
                             A["attn_bias"].rearrange("h q k -> q h k")).then_inc(bias_in, 16)

        def free_after_5(eng):
            eng.wait_ge(x_done, 5)

        l3, (evacuate, guard_keys, expand_keys, guard_values, spread_values, l3_v_sb) = keys_values(
            6, "L3", "L3_xattn_W_k", "L3_xattn_W_v", "L3_xattn_b_q", "L3_xattn_b_k", "L3_xattn_b_v",
            True, l2buf[:, 0:5120], (6, 7, 3, 2), free_after_5, keys=l3_keys)

        seen_order = (7, 6, 5, 4, 3, 2, 1, 0)

        def beside_experts(dve, e):
            if e < 0:
                for g in range(4):
                    evacuate(dve, g)
            elif e == 0:
                guard_keys(dve)
            elif e == 1:
                expand_keys(dve)
            elif e in (2, 3):
                guard_values(dve, e - 2)
            if e == 3:
                pen = arena[:, 7680:8192].rearrange("p (j k) -> p j k", j=NT)
                tmp = arena[:, 6144:7168]
                dve.wait_ge(bias_in, 48)
                V.tensor_scalar(tmp, bias, 0.0, 1e4, ALU.max, ALU.min)
                V.tensor_scalar(seen, masks, 0, None, ALU.not_equal)
                dve_link(V.tensor_scalar(bias, bias, 0.0, -1e4, ALU.min, ALU.max))
                V.tensor_scalar(pen, seen, 1e4, -1e4, ALU.mult, ALU.add)
                V.tensor_scalar(seen_scale, seen, SCALE, None, ALU.mult)
                dve_link(V.tensor_tensor(bias, bias, tmp, ALU.add))
            if e in (4, 5, 6):
                if e == 6:
                    dve.wait_ge(l3[1], 4)
                for j in seen_order[3 * (e - 4):3 * (e - 3)]:
                    V.tensor_tensor(seen_bias[:, j], bias.rearrange("p (h k) -> p h k", h=H),
                                    over(seen[:, j], 1, H), ALU.mult).then_inc(bm_ready, 1)

        @block.gpsimd
        def _(pool):
            pen = arena[:, 7680:8192].rearrange("p (j k) -> p j k", j=NT)
            for i, j in enumerate(seen_order):
                pool.wait_ge(bm_ready, i + 1)
                G.tensor_tensor(seen_bias[:, j], seen_bias[:, j], over(pen[:, j], 1, H), ALU.add)\
                    .then_inc(bm_done, 1)

        def beside_gelu(act, e):
            if e >= 5:
                spread_values(act, {5: (0, 1), 6: (2,), 7: (3,)}[e])

        moe2(5, beside_experts, beside_gelu)

        layernorm()
        attention(6, "L3", "L3_xattn_W_q", "L3_xattn_W_o", "L3_xattn_b_o", l3, True, bm_done)

        def ffn3(n):
            s = lambda name: sem(f"ffn3_{name}")
            col_ok, all_ps, scale_ok = s("max_cols"), s("max_all"), s("scale")
            x_ok, mm_ps, mm_sb, g_ok, sig_ok, st_ok, up_ok, gt_ok, o_ok, y_ps = (
                s("x"), s("products"), s("products_sb"), s("gate"), s("sigmoid"), s("sigmoid_t"), s("up"),
                s("rounded"), s("out"), s("y"))
            NCH = I3 // P
            chunk = lambda v, c: v[:, 1024 * c:1024 * c + 1024]
            up = arena[:, 0:3072]
            gate = arena[:, 3072:6144]
            sig = arena[:, 6144:9216]
            cm = arena[:, 9324:9340]
            top = arena[:, 9342:9343]
            amax = arena[:, 9343:9344]
            scl = arena[:, 9344:9350]
            inv = arena[:, 9350:9356]
            real = arena[:, 9356:9362]
            magic, minus_magic = arena[:, 9364:9365], arena[:, 9365:9366]
            X, GT, UP, GS, OUT = range(5)

            def tokens(v, start, n):
                return v.rearrange("p (c t) -> p c t", c=NCH)[:, :, start:start + n]

            layernorm()

            def all_max(dve, i):
                dve.wait_ge(all_ps, i + 1)
                dve_link(V.tensor_reduce(top, ps[:, 7, 0:P], AX.X, ALU.max))
                dve_link(V.tensor_scalar(scl[:, i:i + 1], top, real[:, i:i + 1], 1e-12, ALU.mult, ALU.max))
                dve_link(V.reciprocal(inv[:, i:i + 1], scl[:, i:i + 1]))
                V.scalar_tensor_tensor(out=inv[:, i:i + 1], in0=inv[:, i:i + 1], scalar=32767.0, in1=real[:, i:i + 1],
                                       op0=ALU.mult, op1=ALU.mult).then_inc(scale_ok, 1)
                dve.wait_ge(scale_ok, i + 1)

            @block.tensor
            def _(pe):
                def maximum(m):
                    pe.wait_ge(col_ok, m + 1)
                    PE.matmul(ps[:, 7, 0:P], amax.broadcast_to([P, P]), ident, start=True, stop=True).then_inc(all_ps, 1)

                maximum(X)
                pe.wait_ge(wT_ok, 3)
                for i, c0 in ((0, 0), (1, 3)):
                    for c in range(NCH):
                        for k in range(2):
                            m = 6 * i + 2 * c + k
                            if m < 2:
                                pe.wait_ge(x_ok, k + 1)
                            if m >= 4:
                                pe.wait_ge(mm_sb, m - 3)
                            PE.matmul(ps[:, m % 4, :], wT[:, c0 + c, :], h_fm[:, 512 * k:512 * k + 512],
                                      start=True, stop=True).then_inc(mm_ps, 1)
                    maximum(GT + i)
                maximum(GS)
                maximum(OUT)
                for k in range(2):
                    for j in range(4 * k, 4 * k + 4):
                        if j % 2 == 0:
                            pe.wait_ge(o_ok, min(j // 2 + 1, 3))
                        for c in range(NCH):
                            ins = PE.matmul(ps[:, k, P * (j % 4):P * (j % 4) + P],
                                            up[:, 1024 * c + P * j:1024 * c + P * j + P], wT[:, 6 + c, :],
                                            start=(c == 0), stop=(c == NCH - 1))
                    ins.then_inc(y_ps, 1)

            @block.scalar
            def _(act):
                def evacuate(i):
                    for m in range(6 * i, 6 * i + 6):
                        act.wait_ge(mm_ps, m + 1)
                        AC.activation((gate, up)[i][:, 512 * (m % 6):512 * (m % 6) + 512], ps[:, m % 4, :], ACT.Copy)\
                            .then_inc(mm_sb, 1)

                evacuate(0)
                evacuate(1)
                for c in range(NCH):
                    act.wait_ge(g_ok, c + 1)
                    AC.activation(chunk(sig, c), chunk(gate, c), ACT.Sigmoid, scale=scl[:, GT:GT + 1]).then_inc(sig_ok, 1)
                    act.wait_ge(sig_ok, c + 1)
                    AC.activation(chunk(sig, c), chunk(sig, c), ACT.Identity, bias=magic, scale=65536.0).then_inc(st_ok, 1)
                act.wait_ge(scale_ok, UP + 1)
                for c in range(NCH):
                    AC.activation(chunk(up, c), chunk(up, c), ACT.Identity, bias=magic, scale=inv[:, UP:UP + 1])\
                        .then_inc(up_ok, 1)
                for c in range(NCH):
                    act.wait_ge(up_ok, c + 1)
                    AC.activation(chunk(up, c), chunk(up, c), ACT.Identity, bias=minus_magic).then_inc(gt_ok, 1)
                act.wait_ge(scale_ok, GS + 1)
                for c in range(NCH):
                    AC.activation(chunk(gate, c), chunk(gate, c), ACT.Identity, bias=magic, scale=inv[:, GS:GS + 1])\
                        .then_inc(gt_ok, 1)
                act.wait_ge(scale_ok, OUT + 1)
                AC.activation(tokens(up, 512, 512), tokens(up, 512, 512), ACT.Identity, bias=magic, scale=inv[:, OUT:OUT + 1]).then_inc(gt_ok, 1)

            @block.vector
            def _(dve):
                V.memset(magic, MAGIC)
                V.memset(minus_magic, -MAGIC)
                V.memset(real[:, X:X + 1], 1.0 / 32767.0)
                wait_h_tm(dve)
                V.tensor_reduce(amax, h_tm[:].rearrange("p j d -> p (j d)"), AX.X, ALU.max, apply_absolute_value=True)\
                    .then_inc(col_ok, 1)
                all_max(dve, X)
                wait_h_fm(dve)
                marks = []
                for k in range(2):
                    v = h_fm[:, 512 * k:512 * k + 512]
                    marks.append(dve_mark(V.tensor_scalar(v, v, inv[:, X:X + 1], MAGIC, ALU.mult, ALU.add)))
                for k in range(2):
                    v = h_fm[:, 512 * k:512 * k + 512]
                    dve.wait_ge(dve_chain, marks[k])
                    V.tensor_scalar(v, v, -MAGIC, None, ALU.add).then_inc(x_ok, 1)
                for i in (GT, UP):
                    ins = V.tensor_scalar(real[:, i:i + 1], scl[:, X:X + 1], 1.0 / 32767.0, None, ALU.mult)
                dve_link(ins)

                def maxima(i):
                    for c in range(6):
                        dve.wait_ge(mm_sb, 6 * i + c + 1)
                        ins = V.tensor_reduce(cm[:, c:c + 1], (gate, up)[i][:, 512 * c:512 * c + 512], AX.X, ALU.max,
                                              apply_absolute_value=True)
                    dve_link(ins)
                    V.tensor_reduce(amax, cm[:, 0:6], AX.X, ALU.max).then_inc(col_ok, 1)

                maxima(0)
                all_max(dve, GT)
                mark = dve_mark(V.tensor_scalar(chunk(gate, 0), chunk(gate, 0), inv[:, GT:GT + 1], MAGIC, ALU.mult, ALU.add))
                for c in range(NCH):
                    after = mark
                    if c + 1 < NCH:
                        mark = dve_mark(V.tensor_scalar(chunk(gate, c + 1), chunk(gate, c + 1), inv[:, GT:GT + 1], MAGIC,
                                                        ALU.mult, ALU.add))
                    dve.wait_ge(dve_chain, after)
                    V.tensor_scalar(chunk(gate, c), chunk(gate, c), -MAGIC, None, ALU.add).then_inc(g_ok, 1)
                V.tensor_scalar(real[:, GS:GS + 1], scl[:, GT:GT + 1], 1.0 / 65536.0 / 32767.0, None, ALU.mult)
                maxima(1)

                for c in range(NCH):
                    dve.wait_ge(st_ok, c + 1)
                    dve_link(V.tensor_scalar(chunk(sig, c), chunk(sig, c), -MAGIC, 65535.0, ALU.add, ALU.min))
                    dve_link(V.tensor_tensor(chunk(gate, c), chunk(gate, c), chunk(sig, c), ALU.mult))
                    ins = V.tensor_reduce(cm[:, c:c + 1], chunk(gate, c), AX.X, ALU.max, apply_absolute_value=True)
                    if c == 0:
                        all_max(dve, UP)
                dve_link(ins)
                V.tensor_reduce(amax, cm[:, 0:NCH], AX.X, ALU.max).then_inc(col_ok, 1)
                all_max(dve, GS)
                V.scalar_tensor_tensor(out=real[:, OUT:OUT + 1], in0=scl[:, GS:GS + 1], scalar=1.0 / 32767.0,
                                       in1=scl[:, UP:UP + 1], op0=ALU.mult, op1=ALU.mult)
                for c in range(NCH):
                    dve.wait_ge(gt_ok, NCH + c + 1)
                    dve_link(V.scalar_tensor_tensor(out=chunk(up, c), in0=chunk(gate, c), scalar=-MAGIC, in1=chunk(up, c),
                                                    op0=ALU.add, op1=ALU.mult))
                    ins = V.tensor_reduce(cm[:, c:c + 1], chunk(up, c), AX.X, ALU.max, apply_absolute_value=True)
                dve_link(ins)
                V.tensor_reduce(amax, cm[:, 0:NCH], AX.X, ALU.max).then_inc(col_ok, 1)
                all_max(dve, OUT)
                for q in range(2):
                    v = tokens(up, 256 * q, 256)
                    dve_link(V.tensor_scalar(v, v, inv[:, OUT:OUT + 1], MAGIC, ALU.mult, ALU.add))
                    V.tensor_scalar(v, v, -MAGIC, None, ALU.add).then_inc(o_ok, 1)
                dve.wait_ge(gt_ok, 2 * NCH + 1)
                v = tokens(up, 512, 512)
                V.tensor_scalar(v, v, -MAGIC, None, ALU.add).then_inc(o_ok, 1)
                for k in range(2):
                    dve.wait_ge(y_ps, k + 1)
                    V.scalar_tensor_tensor(out=x_tm[:, 4 * k:4 * k + 4], in0=ps[:, k, :].rearrange("p (j d) -> p j d", j=4),
                                           scalar=scl[:, OUT:OUT + 1], in1=x_tm[:, 4 * k:4 * k + 4],
                                           op0=ALU.mult, op1=ALU.add).then_inc(halves_done, 1)

        ffn3(7)

        out_done = sem("out_done")

        @block.sync
        def _(sp):
            for k in range(2):
                sp.wait_ge(halves_done, k + 1)
                sp.dma_start(out.rearrange("(j p) d -> p j d", p=P)[:, 4 * k:4 * k + 4], x_tm[:, 4 * k:4 * k + 4])\
                    .then_inc(out_done, 16)
            sp.wait_ge(out_done, 32)


def kernel(**inputs):
    import concourse.bacc as _bacc
    from concourse.bass_utils import run_bass_kernel_spmd as _run

    a = {k: np.asarray(v) for k, v in inputs.items()}

    def T_(m):
        return np.ascontiguousarray(m.T)

    def split(w, k):
        e, f, n = w.shape
        w = w.reshape(e, k, f // k, n).transpose(2, 0, 1, 3)
        return np.ascontiguousarray(w.reshape(f // k, e, n) if k == 1 else w)

    experts = {i: np.concatenate([a[f"L0_ffn_rw{i}"], a[f"L0_ffn_sw{i}"]]) for i in (1, 2, 3)}
    biases = {i: np.concatenate([a[f"L0_ffn_rb{i}"], a[f"L0_ffn_sb{i}"]]) for i in (1, 2, 3)}
    woff = np.zeros((P, 2, S), np.float32)
    boff = np.zeros((2, S, 2), np.float32)
    for g in range(2):
        woff[:, g, :40] = a["L2_xattn_Woff"][40 * g:40 * g + 40].T
        boff[:, :40, g] = a["L2_xattn_boff"][40 * g:40 * g + 40]
    cols = np.concatenate(
        [np.stack([a[n] for n in COLS], 1)]
        + [biases[i].reshape(NQ, 2, P).transpose(2, 0, 1).reshape(P, 2 * NQ) for i in (1, 2)]
        + [boff.reshape(P, 2)], 1)
    send = {
        "x": a["x"].reshape(T, D),
        "ctx": a["ctx_1024"].reshape(T, D),
        "ctx_fm": T_(a["ctx_1024"].reshape(T, D)),
        "const": shape_constants(), "picks": row_picks(),
        "rows": np.stack([a[n] for n in ROWS]),
        "cols": cols,
        "mats": np.ascontiguousarray(np.stack([a[n].T for n in MATS], 1)),
        "woff": woff,
        "moe0_w1": split(experts[1], 1), "moe0_w2": split(experts[2], 1), "moe0_w3": split(experts[3], 2),
        "moe0_b3": biases[3],
        "gate_w": a["L0_ffn_gate_w"], "gate_b": a["L0_ffn_gate_b"],
        "mask": a["mask_BxS2_if0"],
        "attn_bias": a["fside_1x16xSxS2_0"][0],
        "attn_mask": a["mask_Bx1xSxS2_ik1"].reshape(T, S),
        "wq8": T_(a["L1_ffn_weight_q"]).astype(np.int32),
        "moe2_w1": split(a["L2_ffn_w1"], 1), "moe2_w2": split(a["L2_ffn_w2"], 4),
        "moe2_idx": np.ascontiguousarray(a["L2_ffn_expert_indices"].reshape(4, P, 2).transpose(1, 0, 2)),
        "moe2_gw": np.ascontiguousarray(a["L2_ffn_expert_weights"].reshape(4, P, 2).transpose(1, 0, 2)),
        "w_gate": a["L3_ffn_w_gate"], "w_up": a["L3_ffn_w_up"], "w_down": a["L3_ffn_w_down"],
    }
    nc = _bacc.Bacc("TRN2", target_bir_lowering=False, num_devices=1)
    arrays, A = {}, {}
    for name, v in send.items():
        v = np.ascontiguousarray(v)
        arrays[f"in_{name}"] = v
        A[name] = nc.dram_tensor(f"in_{name}", v.shape, mybir.dt.from_np(v.dtype), kind="ExternalInput").ap()
    out = nc.dram_tensor("out_x", (T, D), F32, kind="ExternalOutput").ap()
    build(nc, A, out)
    r = _run(nc, [arrays], core_ids=[0])
    return r.results[0]["out_x"].reshape(B, S, D)
```
